# Optimizing a Trainium2 kernel written in Bass

```python
import numpy as np
import jax
import jax.numpy as jnp

def _softmax(x, axis=-1):
    return jax.nn.softmax(x, axis=axis)

def _gelu(x):
    return jax.nn.gelu(x, approximate=True)

def _silu(x):
    return jax.nn.silu(x)

def _sigmoid(x):
    return jax.nn.sigmoid(x)

def _layernorm(x, axis=-1, eps=1e-05):
    m = jnp.mean(x, axis=axis, keepdims=True)
    v = jnp.var(x, axis=axis, keepdims=True)
    return (x - m) / jnp.sqrt(v + eps)

def _scatter_add(tgt, idx, src, axis=0):
    return tgt.at[idx].add(src)

def _segment_sum(src, seg, n):
    return jax.ops.segment_sum(src, seg, n)
kernel_name = 'mk_pixart_seq_d4_seqx_r4_ae0cba'

def setup_inputs(seed: int=0):
    np.random.seed(seed)
    _w = jnp.asarray

    def _rec_inputs():
        import jax
        import jax.numpy as jnp
        _rk = jax.random.key(seed)
        x = -0.0002928 + 1 * jax.random.normal(jax.random.fold_in(_rk, 1), (1, 2048, 256), jnp.float32)
        _lenS = 2048 - jax.random.randint(jax.random.fold_in(_rk, 7), (1,), 0, max(1, 2048 // 4) + 1, jnp.int32)
        _lenS2 = 1601 - jax.random.randint(jax.random.fold_in(_rk, 8), (1,), 0, max(1, 1601 // 4) + 1, jnp.int32)
        cond_1024 = 0.000887014 + 1.03683 * jax.random.normal(jax.random.fold_in(_rk, 11), (1, 256), jnp.float32)
        _ctx_1024P = jax.random.normal(jax.random.fold_in(_rk, 12), (1, 16, 256), jnp.float32)
        _ctx_1024c = jax.random.dirichlet(jax.random.fold_in(_rk, 512), 0.3 * jnp.ones((16,), jnp.float32), (1, 1601))
        _ctx_1024t = jnp.einsum('bsk,bkd->bsd', _ctx_1024c, _ctx_1024P)
        _ctx_1024t = _ctx_1024t * jax.lax.rsqrt(jnp.mean(jnp.square(_ctx_1024t)) + 1e-12) * 0.953939
        ctx_1024 = 0.00086875 + 0.999764 * (_ctx_1024t + 0.3 * jax.random.normal(jax.random.fold_in(_rk, 612), (1, 1601, 256), jnp.float32))
        _validS = jnp.arange(2048)[None, :] < _lenS[:, None]
        _validS2 = jnp.arange(1601)[None, :] < _lenS2[:, None]
        _causal = jnp.tril(jnp.ones((2048, 2048), dtype=bool))
        mask_BxS2_bf0 = jnp.logical_not(jnp.ones((1, 1601), dtype=bool))
        return (x, cond_1024, ctx_1024, mask_BxS2_bf0)
    x, cond_1024, ctx_1024, mask_BxS2_bf0 = _rec_inputs()

    def _L0_xcond_setup():
        import jax, jax.numpy as jnp
        import numpy as np
        import math
        D_MODEL = 256
        N_HEADS = 16
        HEAD_DIM = D_MODEL // N_HEADS
        D_FF = 1024
        EPS = 1e-05
        ROPE_BASE = 10000.0

        def _rope(t):
            L, Dh = (t.shape[1], t.shape[-1])
            half = Dh // 2
            inv_freq = 1.0 / ROPE_BASE ** (jnp.arange(half, dtype=t.dtype) / half)
            ang = jnp.arange(L, dtype=t.dtype)[:, None] * inv_freq[None, :]
            cos = jnp.cos(ang)[None, :, None, :]
            sin = jnp.sin(ang)[None, :, None, :]
            t1, t2 = (t[..., :half], t[..., half:])
            return jnp.concatenate([t1 * cos - t2 * sin, t2 * cos + t1 * sin], axis=-1)

        def _adaln(x, emb, w, b):
            e = emb[:, 0, :]
            gb = e @ w.T + b
            gamma, beta = jnp.split(gb, 2, axis=-1)
            mu = x.mean(-1, keepdims=True)
            var = x.var(-1, keepdims=True)
            xn = (x - mu) * jax.lax.rsqrt(var + EPS)
            return xn * (1.0 + gamma[:, None, :]) + beta[:, None, :]

        def _attn(q, k, v):
            scale = 1.0 / math.sqrt(HEAD_DIM)
            scores = jnp.einsum('bqhd,bkhd->bhqk', q, k) * scale
            w = jax.nn.softmax(scores, axis=-1)
            out = jnp.einsum('bhqk,bkhd->bqhd', w, v)
            B, Lq = (out.shape[0], out.shape[1])
            return out.reshape(B, Lq, D_MODEL)
        key = jax.random.key(seed)
        ks = jax.random.split(key, 24)
        s = 0.02
        inp = {'x': jax.random.normal(ks[0], (2, 512, D_MODEL), jnp.float32), 'noise_emb': jax.random.normal(ks[1], (2, 1, D_MODEL), jnp.float32), 'context': jax.random.normal(ks[2], (2, 256, D_MODEL), jnp.float32), 'ln1_w': jax.random.normal(ks[3], (2 * D_MODEL, D_MODEL), jnp.float32) * s, 'ln1_b': jax.random.normal(ks[4], (2 * D_MODEL,), jnp.float32) * s, 'ln2_w': jax.random.normal(ks[5], (2 * D_MODEL, D_MODEL), jnp.float32) * s, 'ln2_b': jax.random.normal(ks[6], (2 * D_MODEL,), jnp.float32) * s, 'ln3_w': jax.random.normal(ks[7], (2 * D_MODEL, D_MODEL), jnp.float32) * s, 'ln3_b': jax.random.normal(ks[8], (2 * D_MODEL,), jnp.float32) * s, 'qkv_w': jax.random.normal(ks[9], (3 * D_MODEL, D_MODEL), jnp.float32) * s, 'sa_out_w': jax.random.normal(ks[10], (D_MODEL, D_MODEL), jnp.float32) * s, 'q_w': jax.random.normal(ks[11], (D_MODEL, D_MODEL), jnp.float32) * s, 'k_w': jax.random.normal(ks[12], (D_MODEL, D_MODEL), jnp.float32) * s, 'v_w': jax.random.normal(ks[13], (D_MODEL, D_MODEL), jnp.float32) * s, 'ca_out_w': jax.random.normal(ks[14], (D_MODEL, D_MODEL), jnp.float32) * s, 'ffn_w1': jax.random.normal(ks[15], (D_FF, D_MODEL), jnp.float32) * s, 'ffn_b1': jax.random.normal(ks[16], (D_FF,), jnp.float32) * s, 'ffn_w2': jax.random.normal(ks[17], (D_MODEL, D_FF), jnp.float32) * s, 'ffn_b2': jax.random.normal(ks[18], (D_MODEL,), jnp.float32) * s}
        return inp
    _L0_xcond_all = _L0_xcond_setup()
    _L0_xcond_in = {k: v for k, v in _L0_xcond_all.items() if k in ('ln1_w', 'ln1_b', 'ln2_w', 'ln2_b', 'ln3_w', 'ln3_b', 'qkv_w', 'sa_out_w', 'q_w', 'k_w', 'v_w', 'ca_out_w', 'ffn_w1', 'ffn_b1', 'ffn_w2', 'ffn_b2')}
    del _L0_xcond_all

    def _L1_xcond_setup():
        import jax, jax.numpy as jnp
        import numpy as np
        EPS = 1e-05

        def _ada_ln(x, c, W_ss, b_ss):
            mu = jnp.mean(x, axis=-1, keepdims=True)
            var = jnp.mean((x - mu) ** 2, axis=-1, keepdims=True)
            h = (x - mu) / jnp.sqrt(var + EPS)
            ss = jax.nn.silu(c) @ W_ss + b_ss
            scale, bias = jnp.split(ss, 2, axis=-1)
            return (1.0 + scale)[:, None, :] * h + bias[:, None, :]
        key = jax.random.key(seed)
        ks = jax.random.split(key, 12)
        B, Lq, Lkv, H = (8, 512, 128, 256)
        s = 0.02
        return {'x_q': jax.random.normal(ks[0], (B, Lq, H), jnp.float32), 'x_kv': jax.random.normal(ks[1], (B, Lkv, H), jnp.float32), 't_vec': jax.random.normal(ks[2], (B, H), jnp.float32), 'Wq': jax.random.normal(ks[3], (H, H), jnp.float32) * s, 'bq': jnp.zeros((H,), jnp.float32), 'Wkv': jax.random.normal(ks[4], (H, 2 * H), jnp.float32) * s, 'bkv': jnp.zeros((2 * H,), jnp.float32), 'Wp': jax.random.normal(ks[5], (H, H), jnp.float32) * s, 'bp': jnp.zeros((H,), jnp.float32), 'Wss_q': jax.random.normal(ks[6], (H, 2 * H), jnp.float32) * s, 'bss_q': jnp.zeros((2 * H,), jnp.float32), 'Wss_kv': jax.random.normal(ks[7], (H, 2 * H), jnp.float32) * s, 'bss_kv': jnp.zeros((2 * H,), jnp.float32)}
    _L1_xcond_all = _L1_xcond_setup()
    _L1_xcond_in = {k: v for k, v in _L1_xcond_all.items() if k in ('Wq', 'bq', 'Wkv', 'bkv', 'Wp', 'bp', 'Wss_q', 'bss_q', 'Wss_kv', 'bss_kv')}
    del _L1_xcond_all

    def _L2_xcond_setup():
        import jax, jax.numpy as jnp
        import numpy as np
        H = 256
        RH = 2 * H
        E = 3
        B, T, P = (8, 512, 64)
        LN_EPS = 1e-05

        def _layer_norm(x, gamma, beta):
            mu = jnp.mean(x, axis=-1, keepdims=True)
            var = jnp.mean(jnp.square(x - mu), axis=-1, keepdims=True)
            return (x - mu) * jax.lax.rsqrt(var + LN_EPS) * gamma + beta
        key = jax.random.key(seed)
        ks = jax.random.split(key, 24)
        s = lambda fan_in: 1.0 / np.sqrt(fan_in)
        inp = {'mix_hidden_states': jax.random.normal(ks[0], (B, T, H), jnp.float32), 'global_anchor': jax.random.normal(ks[1], (B, H), jnp.float32), 'prototype_bank': jax.random.normal(ks[2], (B, P, H), jnp.float32), 'ln_gamma': jnp.ones((H,), jnp.float32), 'ln_beta': jnp.zeros((H,), jnp.float32), 'Wq': jax.random.normal(ks[3], (H, H), jnp.float32) * s(H), 'Wk': jax.random.normal(ks[4], (H, H), jnp.float32) * s(H), 'Wv': jax.random.normal(ks[5], (H, H), jnp.float32) * s(H), 'router_W': jax.random.normal(ks[6], (3 * H, E), jnp.float32) * s(3 * H), 'router_b': jnp.zeros((E,), jnp.float32), 'e_w1': jax.random.normal(ks[7], (E, 3 * H, RH), jnp.float32) * s(3 * H), 'e_b1': jnp.zeros((E, RH), jnp.float32), 'e_w2': jax.random.normal(ks[8], (E, RH, H), jnp.float32) * s(RH), 'e_b2': jnp.zeros((E, H), jnp.float32), 'gate_w1': jax.random.normal(ks[9], (3 * H, H), jnp.float32) * s(3 * H), 'gate_b1': jnp.zeros((H,), jnp.float32), 'gate_w2': jax.random.normal(ks[10], (H, H), jnp.float32) * s(H), 'gate_b2': jnp.zeros((H,), jnp.float32), 'out_w': jax.random.normal(ks[11], (H, H), jnp.float32) * s(H), 'out_b': jnp.zeros((H,), jnp.float32)}
        return inp
    _L2_xcond_all = _L2_xcond_setup()
    _L2_xcond_in = {k: v for k, v in _L2_xcond_all.items() if k in ('ln_gamma', 'ln_beta', 'Wq', 'Wk', 'Wv', 'router_W', 'router_b', 'e_w1', 'e_b1', 'e_w2', 'e_b2', 'gate_w1', 'gate_b1', 'gate_w2', 'gate_b2', 'out_w', 'out_b')}
    del _L2_xcond_all

    def _L3_xcond_setup():
        import jax, jax.numpy as jnp
        import numpy as np
        D, H, B, N, S = (256, 16, 4, 256, 77)
        HD = D // H
        DF = 4 * D
        EPS = 1e-06
        SCALE = HD ** (-0.5)

        def _ln(x):
            m = jnp.mean(x, axis=-1, keepdims=True)
            v = jnp.mean((x - m) ** 2, axis=-1, keepdims=True)
            return (x - m) / jnp.sqrt(v + EPS)
        key = jax.random.key(seed)
        ks = jax.random.split(key, 24)
        s = 0.02
        inp = {'x': jax.random.normal(ks[0], (B, N, D), jnp.float32), 't_emb': jax.random.normal(ks[1], (B, D), jnp.float32), 'context': jax.random.normal(ks[2], (B, S, D), jnp.float32), 'context_mask': jnp.zeros((B, S), jnp.bool_), 'ada_w': jax.random.normal(ks[3], (D, 6 * D), jnp.float32) * s, 'ada_b': jnp.zeros((6 * D,), jnp.float32), 'qkv_w': jax.random.normal(ks[4], (D, 3 * D), jnp.float32) * s, 'qkv_b': jnp.zeros((3 * D,), jnp.float32), 'sa_proj_w': jax.random.normal(ks[5], (D, D), jnp.float32) * s, 'sa_proj_b': jnp.zeros((D,), jnp.float32), 'q_w': jax.random.normal(ks[6], (D, D), jnp.float32) * s, 'q_b': jnp.zeros((D,), jnp.float32), 'kv_w': jax.random.normal(ks[7], (D, 2 * D), jnp.float32) * s, 'kv_b': jnp.zeros((2 * D,), jnp.float32), 'ca_proj_w': jax.random.normal(ks[8], (D, D), jnp.float32) * s, 'ca_proj_b': jnp.zeros((D,), jnp.float32), 'fc1_w': jax.random.normal(ks[9], (D, DF), jnp.float32) * s, 'fc1_b': jnp.zeros((DF,), jnp.float32), 'fc2_w': jax.random.normal(ks[10], (DF, D), jnp.float32) * s, 'fc2_b': jnp.zeros((D,), jnp.float32)}
        return inp
    _L3_xcond_all = _L3_xcond_setup()
    _L3_xcond_in = {k: v for k, v in _L3_xcond_all.items() if k in ('ada_w', 'ada_b', 'qkv_w', 'qkv_b', 'sa_proj_w', 'sa_proj_b', 'q_w', 'q_b', 'kv_w', 'kv_b', 'ca_proj_w', 'ca_proj_b', 'fc1_w', 'fc1_b', 'fc2_w', 'fc2_b')}
    del _L3_xcond_all
    return {'x': x, 'cond_1024': cond_1024, 'ctx_1024': ctx_1024, 'mask_BxS2_bf0': mask_BxS2_bf0, 'L0_xcond_ln1_w': _L0_xcond_in['ln1_w'], 'L0_xcond_ln1_b': _L0_xcond_in['ln1_b'], 'L0_xcond_ln2_w': _L0_xcond_in['ln2_w'], 'L0_xcond_ln2_b': _L0_xcond_in['ln2_b'], 'L0_xcond_ln3_w': _L0_xcond_in['ln3_w'], 'L0_xcond_ln3_b': _L0_xcond_in['ln3_b'], 'L0_xcond_qkv_w': _L0_xcond_in['qkv_w'], 'L0_xcond_sa_out_w': _L0_xcond_in['sa_out_w'], 'L0_xcond_q_w': _L0_xcond_in['q_w'], 'L0_xcond_k_w': _L0_xcond_in['k_w'], 'L0_xcond_v_w': _L0_xcond_in['v_w'], 'L0_xcond_ca_out_w': _L0_xcond_in['ca_out_w'], 'L0_xcond_ffn_w1': _L0_xcond_in['ffn_w1'], 'L0_xcond_ffn_b1': _L0_xcond_in['ffn_b1'], 'L0_xcond_ffn_w2': _L0_xcond_in['ffn_w2'], 'L0_xcond_ffn_b2': _L0_xcond_in['ffn_b2'], 'L1_xcond_Wq': _L1_xcond_in['Wq'], 'L1_xcond_bq': _L1_xcond_in['bq'], 'L1_xcond_Wkv': _L1_xcond_in['Wkv'], 'L1_xcond_bkv': _L1_xcond_in['bkv'], 'L1_xcond_Wp': _L1_xcond_in['Wp'], 'L1_xcond_bp': _L1_xcond_in['bp'], 'L1_xcond_Wss_q': _L1_xcond_in['Wss_q'], 'L1_xcond_bss_q': _L1_xcond_in['bss_q'], 'L1_xcond_Wss_kv': _L1_xcond_in['Wss_kv'], 'L1_xcond_bss_kv': _L1_xcond_in['bss_kv'], 'L2_xcond_ln_gamma': _L2_xcond_in['ln_gamma'], 'L2_xcond_ln_beta': _L2_xcond_in['ln_beta'], 'L2_xcond_Wq': _L2_xcond_in['Wq'], 'L2_xcond_Wk': _L2_xcond_in['Wk'], 'L2_xcond_Wv': _L2_xcond_in['Wv'], 'L2_xcond_router_W': _L2_xcond_in['router_W'], 'L2_xcond_router_b': _L2_xcond_in['router_b'], 'L2_xcond_e_w1': _L2_xcond_in['e_w1'], 'L2_xcond_e_b1': _L2_xcond_in['e_b1'], 'L2_xcond_e_w2': _L2_xcond_in['e_w2'], 'L2_xcond_e_b2': _L2_xcond_in['e_b2'], 'L2_xcond_gate_w1': _L2_xcond_in['gate_w1'], 'L2_xcond_gate_b1': _L2_xcond_in['gate_b1'], 'L2_xcond_gate_w2': _L2_xcond_in['gate_w2'], 'L2_xcond_gate_b2': _L2_xcond_in['gate_b2'], 'L2_xcond_out_w': _L2_xcond_in['out_w'], 'L2_xcond_out_b': _L2_xcond_in['out_b'], 'L3_xcond_ada_w': _L3_xcond_in['ada_w'], 'L3_xcond_ada_b': _L3_xcond_in['ada_b'], 'L3_xcond_qkv_w': _L3_xcond_in['qkv_w'], 'L3_xcond_qkv_b': _L3_xcond_in['qkv_b'], 'L3_xcond_sa_proj_w': _L3_xcond_in['sa_proj_w'], 'L3_xcond_sa_proj_b': _L3_xcond_in['sa_proj_b'], 'L3_xcond_q_w': _L3_xcond_in['q_w'], 'L3_xcond_q_b': _L3_xcond_in['q_b'], 'L3_xcond_kv_w': _L3_xcond_in['kv_w'], 'L3_xcond_kv_b': _L3_xcond_in['kv_b'], 'L3_xcond_ca_proj_w': _L3_xcond_in['ca_proj_w'], 'L3_xcond_ca_proj_b': _L3_xcond_in['ca_proj_b'], 'L3_xcond_fc1_w': _L3_xcond_in['fc1_w'], 'L3_xcond_fc1_b': _L3_xcond_in['fc1_b'], 'L3_xcond_fc2_w': _L3_xcond_in['fc2_w'], 'L3_xcond_fc2_b': _L3_xcond_in['fc2_b']}

def reference(x, cond_1024, ctx_1024, mask_BxS2_bf0, L0_xcond_ln1_w, L0_xcond_ln1_b, L0_xcond_ln2_w, L0_xcond_ln2_b, L0_xcond_ln3_w, L0_xcond_ln3_b, L0_xcond_qkv_w, L0_xcond_sa_out_w, L0_xcond_q_w, L0_xcond_k_w, L0_xcond_v_w, L0_xcond_ca_out_w, L0_xcond_ffn_w1, L0_xcond_ffn_b1, L0_xcond_ffn_w2, L0_xcond_ffn_b2, L1_xcond_Wq, L1_xcond_bq, L1_xcond_Wkv, L1_xcond_bkv, L1_xcond_Wp, L1_xcond_bp, L1_xcond_Wss_q, L1_xcond_bss_q, L1_xcond_Wss_kv, L1_xcond_bss_kv, L2_xcond_ln_gamma, L2_xcond_ln_beta, L2_xcond_Wq, L2_xcond_Wk, L2_xcond_Wv, L2_xcond_router_W, L2_xcond_router_b, L2_xcond_e_w1, L2_xcond_e_b1, L2_xcond_e_w2, L2_xcond_e_b2, L2_xcond_gate_w1, L2_xcond_gate_b1, L2_xcond_gate_w2, L2_xcond_gate_b2, L2_xcond_out_w, L2_xcond_out_b, L3_xcond_ada_w, L3_xcond_ada_b, L3_xcond_qkv_w, L3_xcond_qkv_b, L3_xcond_sa_proj_w, L3_xcond_sa_proj_b, L3_xcond_q_w, L3_xcond_q_b, L3_xcond_kv_w, L3_xcond_kv_b, L3_xcond_ca_proj_w, L3_xcond_ca_proj_b, L3_xcond_fc1_w, L3_xcond_fc1_b, L3_xcond_fc2_w, L3_xcond_fc2_b):
    import jax
    import jax.numpy as jnp

    def _L0_xcond_ref(x, noise_emb, context, ln1_w, ln1_b, ln2_w, ln2_b, ln3_w, ln3_b, qkv_w, sa_out_w, q_w, k_w, v_w, ca_out_w, ffn_w1, ffn_b1, ffn_w2, ffn_b2):
        import jax, jax.numpy as jnp
        import numpy as np
        import math
        D_MODEL = 256
        N_HEADS = 16
        HEAD_DIM = D_MODEL // N_HEADS
        D_FF = 1024
        EPS = 1e-05
        ROPE_BASE = 10000.0

        def _rope(t):
            L, Dh = (t.shape[1], t.shape[-1])
            half = Dh // 2
            inv_freq = 1.0 / ROPE_BASE ** (jnp.arange(half, dtype=t.dtype) / half)
            ang = jnp.arange(L, dtype=t.dtype)[:, None] * inv_freq[None, :]
            cos = jnp.cos(ang)[None, :, None, :]
            sin = jnp.sin(ang)[None, :, None, :]
            t1, t2 = (t[..., :half], t[..., half:])
            return jnp.concatenate([t1 * cos - t2 * sin, t2 * cos + t1 * sin], axis=-1)

        def _adaln(x, emb, w, b):
            e = emb[:, 0, :]
            gb = e @ w.T + b
            gamma, beta = jnp.split(gb, 2, axis=-1)
            mu = x.mean(-1, keepdims=True)
            var = x.var(-1, keepdims=True)
            xn = (x - mu) * jax.lax.rsqrt(var + EPS)
            return xn * (1.0 + gamma[:, None, :]) + beta[:, None, :]

        def _attn(q, k, v):
            scale = 1.0 / math.sqrt(HEAD_DIM)
            scores = jnp.einsum('bqhd,bkhd->bhqk', q, k) * scale
            w = jax.nn.softmax(scores, axis=-1)
            out = jnp.einsum('bhqk,bkhd->bqhd', w, v)
            B, Lq = (out.shape[0], out.shape[1])
            return out.reshape(B, Lq, D_MODEL)
        B, L, D = x.shape
        L_ctx = context.shape[1]
        res = x
        xn = _adaln(x, noise_emb, ln1_w, ln1_b)
        qkv = xn @ qkv_w.T
        q, k, v = jnp.split(qkv, 3, axis=-1)
        q = _rope(q.reshape(B, L, N_HEADS, HEAD_DIM))
        k = _rope(k.reshape(B, L, N_HEADS, HEAD_DIM))
        v = v.reshape(B, L, N_HEADS, HEAD_DIM)
        sa = _attn(q, k, v) @ sa_out_w.T
        x = res + sa
        res = x
        xn = _adaln(x, noise_emb, ln2_w, ln2_b)
        q = _rope((xn @ q_w.T).reshape(B, L, N_HEADS, HEAD_DIM))
        k = _rope((context @ k_w.T).reshape(B, L_ctx, N_HEADS, HEAD_DIM))
        v = (context @ v_w.T).reshape(B, L_ctx, N_HEADS, HEAD_DIM)
        ca = _attn(q, k, v) @ ca_out_w.T
        x = res + ca
        res = x
        xn = _adaln(x, noise_emb, ln3_w, ln3_b)
        h = jax.nn.gelu(xn @ ffn_w1.T + ffn_b1, approximate=False)
        x = res + (h @ ffn_w2.T + ffn_b2)
        return x

    def _L1_xcond_ref(x_q, x_kv, t_vec, Wq, bq, Wkv, bkv, Wp, bp, Wss_q, bss_q, Wss_kv, bss_kv):
        import jax, jax.numpy as jnp
        import numpy as np
        EPS = 1e-05

        def _ada_ln(x, c, W_ss, b_ss):
            mu = jnp.mean(x, axis=-1, keepdims=True)
            var = jnp.mean((x - mu) ** 2, axis=-1, keepdims=True)
            h = (x - mu) / jnp.sqrt(var + EPS)
            ss = jax.nn.silu(c) @ W_ss + b_ss
            scale, bias = jnp.split(ss, 2, axis=-1)
            return (1.0 + scale)[:, None, :] * h + bias[:, None, :]
        B, Lq, H = x_q.shape
        Lkv = x_kv.shape[1]
        nh = 16
        dh = H // nh
        xq = _ada_ln(x_q, t_vec, Wss_q, bss_q)
        xkv = _ada_ln(x_kv, t_vec, Wss_kv, bss_kv)
        q = (xq @ Wq + bq).reshape(B, Lq, nh, dh)
        kv = (xkv @ Wkv + bkv).reshape(B, Lkv, 2, nh, dh)
        k = kv[:, :, 0]
        v = kv[:, :, 1]
        scores = jnp.einsum('bqhd,bkhd->bhqk', q, k) / jnp.sqrt(jnp.float32(dh))
        attn = jax.nn.softmax(scores, axis=-1)
        out = jnp.einsum('bhqk,bkhd->bqhd', attn, v).reshape(B, Lq, H)
        return x_q + (out @ Wp + bp)

    def _L2_xcond_ref(mix_hidden_states, global_anchor, prototype_bank, ln_gamma, ln_beta, Wq, Wk, Wv, router_W, router_b, e_w1, e_b1, e_w2, e_b2, gate_w1, gate_b1, gate_w2, gate_b2, out_w, out_b):
        import jax, jax.numpy as jnp
        import numpy as np
        H = 256
        RH = 2 * H
        E = 3
        B, T, P = (8, 512, 64)
        LN_EPS = 1e-05

        def _layer_norm(x, gamma, beta):
            mu = jnp.mean(x, axis=-1, keepdims=True)
            var = jnp.mean(jnp.square(x - mu), axis=-1, keepdims=True)
            return (x - mu) * jax.lax.rsqrt(var + LN_EPS) * gamma + beta
        x = mix_hidden_states
        nx = _layer_norm(x, ln_gamma, ln_beta)
        q = nx @ Wq
        k = prototype_bank @ Wk
        v = prototype_bank @ Wv
        scores = jnp.einsum('bth,bph->btp', q, k) * H ** (-0.5)
        weights = jax.nn.softmax(scores, axis=-1)
        evidence = jnp.einsum('btp,bph->bth', weights, v)
        anchor = jnp.broadcast_to(global_anchor[:, None, :], nx.shape)
        combined = jnp.concatenate([nx, evidence, anchor], axis=-1)
        router_logits = combined @ router_W + router_b
        router_probs = jax.nn.softmax(router_logits, axis=-1)
        h = jax.nn.silu(jnp.einsum('btc,ecr->bter', combined, e_w1) + e_b1)
        expert_out = jnp.einsum('bter,erh->bteh', h, e_w2) + e_b2
        routed = jnp.sum(expert_out * router_probs[..., None], axis=-2)
        g = jax.nn.sigmoid(jax.nn.silu(combined @ gate_w1 + gate_b1) @ gate_w2 + gate_b2)
        refined_delta = g * (routed @ out_w + out_b)
        return x + refined_delta

    def _L3_xcond_ref(x, t_emb, context, context_mask, ada_w, ada_b, qkv_w, qkv_b, sa_proj_w, sa_proj_b, q_w, q_b, kv_w, kv_b, ca_proj_w, ca_proj_b, fc1_w, fc1_b, fc2_w, fc2_b):
        import jax, jax.numpy as jnp
        import numpy as np
        D, H, B, N, S = (256, 16, 4, 256, 77)
        HD = D // H
        DF = 4 * D
        EPS = 1e-06
        SCALE = HD ** (-0.5)

        def _ln(x):
            m = jnp.mean(x, axis=-1, keepdims=True)
            v = jnp.mean((x - m) ** 2, axis=-1, keepdims=True)
            return (x - m) / jnp.sqrt(v + EPS)
        Bx, Nx, C = x.shape
        Sx = context.shape[1]
        mod = jax.nn.silu(t_emb) @ ada_w + ada_b
        shift_sa, scale_sa, gate_sa, shift_ff, scale_ff, gate_ff = [m[:, None, :] for m in jnp.split(mod, 6, axis=-1)]
        xm1 = _ln(x) * (1 + scale_sa) + shift_sa
        qkv = (xm1 @ qkv_w + qkv_b).reshape(Bx, Nx, 3, H, HD)
        q, k, v = (qkv[:, :, 0], qkv[:, :, 1], qkv[:, :, 2])
        attn = jnp.einsum('bnhd,bmhd->bhnm', q, k) * SCALE
        attn = jax.nn.softmax(attn, axis=-1)
        sa = jnp.einsum('bhnm,bmhd->bnhd', attn, v).reshape(Bx, Nx, C)
        sa = sa @ sa_proj_w + sa_proj_b
        x = x + gate_sa * sa
        xn2 = _ln(x)
        qc = (xn2 @ q_w + q_b).reshape(Bx, Nx, H, HD)
        kvc = (context @ kv_w + kv_b).reshape(Bx, Sx, 2, H, HD)
        kc, vc = (kvc[:, :, 0], kvc[:, :, 1])
        attn_c = jnp.einsum('bnhd,bshd->bhns', qc, kc) * SCALE
        attn_c = jnp.where(context_mask[:, None, None, :], -jnp.inf, attn_c)
        attn_c = jax.nn.softmax(attn_c, axis=-1)
        ca = jnp.einsum('bhns,bshd->bnhd', attn_c, vc).reshape(Bx, Nx, C)
        ca = ca @ ca_proj_w + ca_proj_b
        x = x + ca
        xm3 = _ln(x) * (1 + scale_ff) + shift_ff
        h = jax.nn.gelu(xm3 @ fc1_w + fc1_b, approximate=False)
        ff = h @ fc2_w + fc2_b
        x = x + gate_ff * ff
        return x
    x = _L0_xcond_ref(x, cond_1024[:, None, :], ctx_1024, L0_xcond_ln1_w, L0_xcond_ln1_b, L0_xcond_ln2_w, L0_xcond_ln2_b, L0_xcond_ln3_w, L0_xcond_ln3_b, L0_xcond_qkv_w, L0_xcond_sa_out_w, L0_xcond_q_w, L0_xcond_k_w, L0_xcond_v_w, L0_xcond_ca_out_w, L0_xcond_ffn_w1, L0_xcond_ffn_b1, L0_xcond_ffn_w2, L0_xcond_ffn_b2)
    x = _L1_xcond_ref(x, ctx_1024, cond_1024, L1_xcond_Wq, L1_xcond_bq, L1_xcond_Wkv, L1_xcond_bkv, L1_xcond_Wp, L1_xcond_bp, L1_xcond_Wss_q, L1_xcond_bss_q, L1_xcond_Wss_kv, L1_xcond_bss_kv)
    x = _L2_xcond_ref(x, cond_1024, ctx_1024, L2_xcond_ln_gamma, L2_xcond_ln_beta, L2_xcond_Wq, L2_xcond_Wk, L2_xcond_Wv, L2_xcond_router_W, L2_xcond_router_b, L2_xcond_e_w1, L2_xcond_e_b1, L2_xcond_e_w2, L2_xcond_e_b2, L2_xcond_gate_w1, L2_xcond_gate_b1, L2_xcond_gate_w2, L2_xcond_gate_b2, L2_xcond_out_w, L2_xcond_out_b)
    x = _L3_xcond_ref(x, cond_1024, ctx_1024, mask_BxS2_bf0, L3_xcond_ada_w, L3_xcond_ada_b, L3_xcond_qkv_w, L3_xcond_qkv_b, L3_xcond_sa_proj_w, L3_xcond_sa_proj_b, L3_xcond_q_w, L3_xcond_q_b, L3_xcond_kv_w, L3_xcond_kv_b, L3_xcond_ca_proj_w, L3_xcond_ca_proj_b, L3_xcond_fc1_w, L3_xcond_fc1_b, L3_xcond_fc2_w, L3_xcond_fc2_b)
    return x

_drawn_inputs = setup_inputs


def setup_inputs(seed=0):
    import zlib

    import numpy as np

    out = dict(_drawn_inputs(seed))
    spreads = {'L1_xcond_bq': (0.0, 2.0),
     'L1_xcond_bkv': (0.0, 0.1),
     'L1_xcond_bp': (0.0, 0.1),
     'L1_xcond_bss_q': (0.0, 0.8),
     'L1_xcond_bss_kv': (0.0, 0.765),
     'L2_xcond_ln_gamma': (1.0, 0.6),
     'L2_xcond_ln_beta': (0.0, 0.702),
     'L2_xcond_router_b': (0.0, 0.8),
     'L2_xcond_e_b1': (0.0, 0.429),
     'L2_xcond_e_b2': (0.0, 0.1),
     'L2_xcond_gate_b1': (0.0, 0.8),
     'L2_xcond_gate_b2': (0.0, 0.8),
     'L2_xcond_out_b': (0.0, 0.1),
     'L3_xcond_ada_b': (0.0, 0.47),
     'L3_xcond_qkv_b': (0.0, 0.8),
     'L3_xcond_sa_proj_b': (0.0, 0.37),
     'L3_xcond_q_b': (0.0, 2.0),
     'L3_xcond_kv_b': (0.0, 0.726),
     'L3_xcond_ca_proj_b': (0.0, 0.1),
     'L3_xcond_fc1_b': (0.0, 0.8),
     'L3_xcond_fc2_b': (0.0, 0.447)}
    factors = {'L0_xcond_ln1_b': 8.0,
     'L0_xcond_ln2_w': 8.0,
     'L0_xcond_ln2_b': 8.0,
     'L0_xcond_ln3_b': 8.0,
     'L0_xcond_q_w': 8.0,
     'L0_xcond_k_w': 8.0,
     'L0_xcond_ffn_b1': 7.801,
     'L0_xcond_ffn_b2': 2.939,
     'L1_xcond_Wq': 8.0,
     'L1_xcond_Wss_q': 8.0,
     'L3_xcond_qkv_w': 8.0,
     'L3_xcond_sa_proj_w': 5.738,
     'L3_xcond_q_w': 64.0,
     'L3_xcond_fc1_w': 2.688,
     'L3_xcond_kv_w': 3.016}
    for name, (base, spread) in spreads.items():
        noise = np.random.default_rng([zlib.crc32(name.encode()), seed]).standard_normal(out[name].shape)
        drawn = base * np.exp(spread * noise) if base else spread * noise
        out[name] = jnp.asarray(drawn.astype(out[name].dtype))
    for name, factor in factors.items():
        out[name] = (out[name] * factor).astype(out[name].dtype)
    return out
```

```python
from contextlib import ExitStack

import concourse.bass as bass
from concourse import mybir

F32 = mybir.dt.float32
BF16 = mybir.dt.bfloat16
U8 = mybir.dt.uint8
ALU = mybir.AluOpType
ACT = mybir.ActivationFunctionType
AX = mybir.AxisListType.X

P = 128
T = 2048
D = 256
NH = 16
DH = D // NH
NT = T // P
NS2 = 1601
NC2 = -(-NS2 // P)
CH = 512
NCH = T // CH
KD = D // P
FF = 1024
NE = 3
RH = 512
HG = 4
NG = NH // HG
PARTS = 3
Q_PART = (0, 1, 2, 0, 1, 0)
K_PART = (0, 0, 0, 1, 1, 2)
PAIR_ROWS = DH * len(Q_PART)
MASK_ROW = PAIR_ROWS
MAX_ROW = MASK_ROW + 1
KROWS = MAX_ROW + PARTS
CREDIT = 8
MASK_BIAS = -1.0e30


def tile_rows(n, i):
    return min(P, n - i * P)


class Signal:

    def __init__(self, sem):
        self.sem = sem
        self.start = CREDIT

    def at(self, n):
        return self.start + n

    def advance(self, n):
        self.start += n


class Machine:
    pass


def cols(ap, k):
    return ap[:, k:k + 1]


def setup_phase(nc, m, d):
    s_load, s_w, s_cond, s_mod, s_modv, s_st, s_rs, s_n, s_tr, s_ev = (
        m.sig[n] for n in ("load", "weights", "cond_ready", "mod_ready", "mod_saved", "stats",
                           "rstd", "normed", "turned", "turn_saved"))
    with ExitStack() as ctx:
        sb = lambda n, s, t=F32: ctx.enter_context(nc.sbuf_tensor("su_" + n, s, t))
        lnw = sb("lnw", [P, 3, KD, 2 * D])
        l1w = sb("l1w", [P, 2, KD, 2 * D])
        adaw = sb("adaw", [P, KD, 6 * D])
        ew1c = sb("ew1c", [P, NE, KD, RH])
        gw1c = sb("gw1c", [P, KD, D])
        rwc = sb("rwc", [P, KD, NE])
        bias_cols = sb("bias_cols", [P, m.NCOL])
        gate_b = sb("gate_b", [P, 2, D])
        rb = sb("rb", [P, NE])
        cond = sb("cond", [P, KD])
        silu_cond = sb("silu_cond", [P, KD])
        cond_bc = sb("cond_bc", [P, 2, KD, P])
        ones = sb("ones", [P, P])
        ct = sb("ct", [P, NC2, D])
        cn = sb("cn", [P, NC2, D])
        st = sb("st", [P, NC2, 6])
        mv = sb("mv", [P, NC2, 2])
        var = sb("var", [P, NC2])
        std = sb("std", [P, NC2])
        rstd = sb("rstd", [P, NC2])
        ps = ctx.enter_context(nc.psum_tensor("su_ps", [P, 8, CH], F32))
        L = m.L
        col = m.col
        jobs = []
        for i in range(3):
            for j in range(4):
                jobs.append((col["l0"] + 4 * i + j, [lnw[:, i, k, j * P:(j + 1) * P] for k in range(KD)], 0))
        for i in range(2):
            for j in range(4):
                jobs.append((col["l1"] + 4 * i + j, [l1w[:, i, k, j * P:(j + 1) * P] for k in range(KD)], 1))
        for j in range(12):
            jobs.append((col["l3"] + j, [adaw[:, k, j * P:(j + 1) * P] for k in range(KD)], 1))
        for e in range(NE):
            for j in range(RH // P):
                jobs.append((col["eb1"] + 4 * e + j, [ew1c[:, e, k, j * P:(j + 1) * P] for k in range(KD)], 0))
        for j in range(KD):
            jobs.append((col["gb1"] + j, [gw1c[:, k, j * P:(j + 1) * P] for k in range(KD)], 0))
        assert [j[0] for j in jobs] == list(range(len(jobs)))
        NJ = len(jobs)
        plus_one = [col["l0"] + 4 * i for i in range(3)] + [col["l1"], col["l1"] + 4, col["l3"] + 2, col["l3"] + 8]
        NLOAD = 0

        block = ctx.enter_context(nc.Block())

        @block.sync
        def _(sp):
            nonlocal NLOAD
            loads = [(cond, d["cond"]),
                     (m.ident, d["ident"])]
            for i in range(3):
                loads.append((lnw[:, i], d["l0_ln_wT"][i].rearrange("(k p) n -> p k n", p=P)))
            loads.append((l1w[:, 0], d["L1_xcond_Wss_q"].rearrange("(k p) n -> p k n", p=P)))
            loads.append((l1w[:, 1], d["L1_xcond_Wss_kv"].rearrange("(k p) n -> p k n", p=P)))
            loads.append((adaw, d["L3_xcond_ada_w"].rearrange("(k p) n -> p k n", p=P)))
            for e in range(NE):
                loads.append((ew1c[:, e], d["L2_xcond_e_w1"][e, 2 * D:3 * D, :].rearrange("(k p) n -> p k n", p=P)))
            loads.append((gw1c, d["L2_xcond_gate_w1"][2 * D:3 * D, :].rearrange("(k p) n -> p k n", p=P)))
            loads.append((rwc, d["L2_xcond_router_W"][2 * D:3 * D, :].rearrange("(k p) n -> p k n", p=P)))
            loads.append((bias_cols, d["bias_cols"]))
            for i in range(2):
                j = (2, 5)[i]
                loads.append((gate_b[:, i], d["L3_xcond_ada_b"][j * D:(j + 1) * D].partition_broadcast(P)))
            loads.append((rb, d["L2_xcond_router_b"].partition_broadcast(P)))
            NLOAD = len(loads)
            for dst, src in loads:
                sp.dma_start(dst[:] if hasattr(dst, "name") else dst, src).then_inc(s_w.sem, 16)

        @block.gpsimd
        def _(pool):
            nc.gpsimd.memset(ones[:, :], 1.0).then_inc(m.sig["ones"].sem, 1)

        @block.scalar
        def _(act):
            act.dma_start(ct[:, 0:NC2 - 1, :], d["ctx"][0:(NC2 - 1) * P, :].rearrange("(t p) n -> p t n", p=P)
                          ).then_inc(s_load.sem, 16)
            act.dma_start(ct[0:L, NC2 - 1, :], d["ctx"][(NC2 - 1) * P:NS2, :]).then_inc(s_load.sem, 16)
            act.dma_start(m.x[:, :, :], d["x"].rearrange("(t p) n -> p t n", p=P)).then_inc(s_load.sem, 16)
            act.wait_ge(s_w.sem, s_w.at(16 * NLOAD))
            nc.scalar.activation(silu_cond[:, :], cond[:, :], ACT.Silu).then_inc(s_cond.sem, 1)
            act.wait_ge(s_st.sem, s_st.at(1))
            nc.scalar.activation(std[:, :], var[:, :], ACT.Sqrt).then_inc(s_rs.sem, 1)
            turn = 0
            for src in range(2):
                for t4 in range(4):
                    for k in range(KD):
                        n = min(4 * P, NS2 - t4 * 4 * P)
                        act.wait_ge(s_tr.sem, s_tr.at(turn + 1))
                        dst = (m.ctxT, m.ctxnT)[src][:, k, t4 * CH:t4 * CH + n]
                        if src == 0:
                            nc.scalar.copy(dst, ps[:, 2 + turn % 4, 0:n]).then_inc(s_ev.sem, 1)
                        else:
                            if t4 == 0 and k == 0:
                                act.wait_ge(m.sig["cols_ready"].sem, m.sig["cols_ready"].at(1))
                            c = col["l1"] + 4
                            nc.scalar.activation(dst, ps[:, 2 + turn % 4, 0:n], ACT.Identity,
                                                 scale=cols(m.mod, c + k), bias=cols(m.mod, c + 2 + k)
                                                 ).then_inc(s_ev.sem, 1)
                        turn += 1

        @block.vector
        def _(dve):
            dve.wait_ge(s_w.sem, s_w.at(16 * NLOAD))
            dve.wait_ge(m.sig["ones"].sem, m.sig["ones"].at(1))
            dve.wait_ge(s_cond.sem, s_cond.at(1))
            for i, c in enumerate((cond, silu_cond)):
                for k in range(KD):
                    last = nc.vector.tensor_scalar(cond_bc[:, i, k, :], ones[:, :], cols(c, k), None, ALU.mult)
            last.then_inc(m.sig["cond_bc"].sem, 1)
            dve.wait_ge(s_load.sem, s_load.at(48))
            for t in range(NC2):
                r = tile_rows(NS2, t)
                nc.vector.bn_stats(st[0:r, t, :], ct[0:r, t, :]).then_inc(m.sig["dve"].sem, 1)
            nc.vector.memset(var[:, :], 1.0).then_inc(m.sig["dve"].sem, 1)
            dve.wait_ge(m.sig["dve"].sem, m.sig["dve"].at(NC2 + 1))
            for t in range(NC2):
                r = tile_rows(NS2, t)
                nc.vector.bn_aggr(mv[0:r, t, :], st[0:r, t, :]).then_inc(m.sig["dve"].sem, 1)
            dve.wait_ge(m.sig["dve"].sem, m.sig["dve"].at(2 * NC2 + 1))
            nc.vector.tensor_scalar(var[:, 0:NC2 - 1], mv[:, 0:NC2 - 1, 1], 1e-5, None, ALU.add)
            nc.vector.tensor_scalar(var[0:L, NC2 - 1:NC2], mv[0:L, NC2 - 1, 1:2], 1e-5, None, ALU.add
                                    ).then_inc(s_st.sem, 1)
            dve.wait_ge(s_rs.sem, s_rs.at(1))
            nc.vector.reciprocal(rstd[:, :], std[:, :]).then_inc(m.sig["dve"].sem, 1)
            dve.wait_ge(m.sig["dve"].sem, m.sig["dve"].at(2 * NC2 + 2))
            for t in range(NC2):
                r = tile_rows(NS2, t)
                nc.vector.tensor_scalar(cn[0:r, t, :], ct[0:r, t, :], mv[0:r, t, 0:1], rstd[0:r, t:t + 1],
                                        ALU.subtract, ALU.mult).then_inc(s_n.sem, 1)
            dve.wait_ge(s_mod.sem, s_mod.at(1))
            nc.vector.tensor_tensor(m.mod[:, 0:NJ], ps[:, 0, 0:NJ], bias_cols[:, 0:NJ], ALU.add
                                    ).then_inc(m.sig["dve"].sem, 1)
            nc.vector.tensor_copy(m.mod[:, NJ:m.NCOL], bias_cols[:, NJ:m.NCOL]).then_inc(m.sig["dve"].sem, 1)
            dve.wait_ge(m.sig["dve"].sem, m.sig["dve"].at(2 * NC2 + 4))
            for c in plus_one:
                last = nc.vector.tensor_scalar(m.mod[:, c:c + 2], m.mod[:, c:c + 2], 1.0, None, ALU.add)
            last.then_inc(m.sig["cols_ready"].sem, 1)
            dve.wait_ge(s_mod.sem, s_mod.at(2))
            nc.vector.tensor_tensor(m.gates[:, :, :], ps[:, 1, :].rearrange("p (a b) -> p a b", a=2),
                                    gate_b[:, :, :], ALU.add).then_inc(s_modv.sem, 1)
            nc.vector.tensor_tensor(m.router_bias[:, :], ps[:, 0, NJ:NJ + NE], rb[:, :], ALU.add
                                    ).then_inc(s_modv.sem, 1)

        @block.tensor
        def _(pe):
            pe.wait_ge(s_w.sem, s_w.at(16 * NLOAD))
            pe.wait_ge(s_load.sem, s_load.at(48))
            turn = 0
            def turn_tiles(src, ready):
                nonlocal turn
                for t4 in range(4):
                    for k in range(KD):
                        if turn >= 4:
                            pe.wait_ge(s_ev.sem, s_ev.at(turn - 3))
                        tiles = range(4 * t4, min(4 * t4 + 4, NC2))
                        if ready:
                            pe.wait_ge(s_n.sem, s_n.at(tiles[-1] + 1))
                        for t in tiles:
                            r = tile_rows(NS2, t)
                            last = pe.transpose(ps[:, 2 + turn % 4, (t % 4) * P:(t % 4) * P + r],
                                                src[0:r, t, k * P:(k + 1) * P], m.ident[0:r, 0:r])
                        last.then_inc(s_tr.sem, 1)
                        turn += 1
            turn_tiles(ct, False)
            pe.wait_ge(s_cond.sem, s_cond.at(1))
            for c, w, which in jobs:
                v = (cond, silu_cond)[which]
                for k in range(KD):
                    last = pe.matmul(ps[:, 0, c:c + 1], w[k], cols(v, k), start=(k == 0), stop=(k == KD - 1))
            pe.wait_ge(m.sig["cond_bc"].sem, m.sig["cond_bc"].at(1))
            for k in range(KD):
                last = pe.matmul(ps[:, 0, NJ:NJ + NE], cond_bc[:, 0, k, :], rwc[:, k, :],
                                 start=(k == 0), stop=(k == KD - 1))
            last.then_inc(s_mod.sem, 1)
            for i in range(2):
                j = (2, 5)[i]
                for k in range(KD):
                    last = pe.matmul(ps[:, 1, i * D:(i + 1) * D], cond_bc[:, 1, k, :],
                                     adaw[:, k, j * D:(j + 1) * D], start=(k == 0), stop=(k == KD - 1))
            last.then_inc(s_mod.sem, 1)
            turn_tiles(cn, True)

    for n, k in (("load", 48), ("weights", 16 * NLOAD), ("cond_ready", 1), ("mod_ready", 2), ("mod_saved", 2),
                 ("stats", 1), ("rstd", 1), ("normed", NC2), ("turned", 16), ("turn_saved", 16), ("ones", 1),
                 ("cond_bc", 1), ("dve", 2 * NC2 + 4), ("cols_ready", 1)):
        m.sig[n].advance(k)


def norm_phase(nc, m, hT, eps, scale, shift):
    s_st, s_rs, s_n, s_tr, s_ev, s_d = (m.sig[n] for n in ("stats", "rstd", "normed", "turned", "turn_saved", "dve"))
    with ExitStack() as ctx:
        m.uid += 1
        sb = lambda n, s, t=F32: ctx.enter_context(nc.sbuf_tensor(f"nm{m.uid}_" + n, s, t))
        st = sb("st", [P, NT, 6])
        mv = sb("mv", [P, NT, 2])
        var = sb("var", [P, NT])
        std = sb("std", [P, NT])
        rstd = sb("rstd", [P, NT])
        xn = sb("xn", [P, NT, D])
        ps = ctx.enter_context(nc.psum_tensor(f"nm{m.uid}_ps", [P, 4, CH], F32))
        block = ctx.enter_context(nc.Block())

        @block.vector
        def _(dve):
            for t in range(NT):
                nc.vector.bn_stats(st[:, t, :], m.x[:, t, :]).then_inc(s_d.sem, 1)
            dve.wait_ge(s_d.sem, s_d.at(NT))
            for t in range(NT):
                nc.vector.bn_aggr(mv[:, t, :], st[:, t, :]).then_inc(s_d.sem, 1)
            dve.wait_ge(s_d.sem, s_d.at(2 * NT))
            nc.vector.tensor_scalar(var[:, :], mv[:, :, 1], eps, None, ALU.add).then_inc(s_st.sem, 1)
            dve.wait_ge(s_rs.sem, s_rs.at(1))
            nc.vector.reciprocal(rstd[:, :], std[:, :]).then_inc(s_d.sem, 1)
            dve.wait_ge(s_d.sem, s_d.at(2 * NT + 1))
            for t in range(NT):
                nc.vector.tensor_scalar(xn[:, t, :], m.x[:, t, :], mv[:, t, 0:1], rstd[:, t:t + 1],
                                        ALU.subtract, ALU.mult).then_inc(s_n.sem, 1)

        @block.scalar
        def _(act):
            act.wait_ge(s_st.sem, s_st.at(1))
            nc.scalar.activation(std[:, :], var[:, :], ACT.Sqrt).then_inc(s_rs.sem, 1)
            for i in range(NCH * KD):
                c, k = divmod(i, KD)
                act.wait_ge(s_tr.sem, s_tr.at(i + 1))
                dst = hT[:, k, c * CH:(c + 1) * CH]
                if scale is None:
                    nc.scalar.copy(dst, ps[:, i % 4, :]).then_inc(s_ev.sem, 1)
                else:
                    nc.scalar.activation(dst, ps[:, i % 4, :], ACT.Identity, scale=cols(m.mod, scale + k),
                                         bias=cols(m.mod, shift + k)).then_inc(s_ev.sem, 1)

        @block.tensor
        def _(pe):
            for i in range(NCH * KD):
                c, k = divmod(i, KD)
                pe.wait_ge(s_n.sem, s_n.at(4 * c + 4))
                if i >= 4:
                    pe.wait_ge(s_ev.sem, s_ev.at(i - 3))
                for t in range(4):
                    last = pe.transpose(ps[:, i % 4, t * P:(t + 1) * P], xn[:, 4 * c + t, k * P:(k + 1) * P],
                                        m.ident[:, :])
                last.then_inc(s_tr.sem, 1)

    for n, k in (("stats", 1), ("rstd", 1), ("normed", NT), ("turned", NCH * KD), ("turn_saved", NCH * KD),
                 ("dve", 2 * NT + 1)):
        m.sig[n].advance(k)


def projection_phase(nc, m, loads, feature_jobs, token_jobs, rope):
    s_w, s_pr, s_tk, s_rot, s_rv, s_f2, s_p1, s_r, s_p2, s_sp, s_d = (
        m.sig[n] for n in ("weights", "proj_ready", "proj_taken", "rot_ready", "rot_taken",
                           "feat_final", "part1", "rest", "part2", "parts_ready", "dve"))
    s_slot = [m.sig[f"stored{i}"] for i in range(4)]
    NF, NJ = len(feature_jobs), len(feature_jobs) + len(token_jobs)
    R = 4
    with ExitStack() as ctx:
        m.uid += 1
        sb = lambda n, s, t=F32: ctx.enter_context(nc.sbuf_tensor(f"pj{m.uid}_" + n, s, t))
        feat = sb("feat", [P, R, CH])
        turned = sb("turned", [P, R, CH])
        final = sb("final", [P, R, CH]) if rope else feat
        rest = sb("rest", [P, R, CH])
        parts = sb("parts", [P, R, PARTS, CH], BF16)
        ps = ctx.enter_context(nc.psum_tensor(f"pj{m.uid}_ps", [P, 4, CH], F32))
        pr = ctx.enter_context(nc.psum_tensor(f"pj{m.uid}_pr", [P, 2, CH], F32))
        block = ctx.enter_context(nc.Block())
        split = [f for f in range(NF) if feature_jobs[f][4] is not None]
        assert not split or split == list(range(NF))
        stored = len(split) > 0

        @block.sync
        def _(sp):
            for dst, src in loads:
                sp.dma_start(dst, src).then_inc(s_w.sem, 16)
            for f in split:
                n = feature_jobs[f][2]
                sp.wait_ge(s_sp.sem, s_sp.at(f + 1))
                sp.dma_start(feature_jobs[f][4], parts[:, f % R, :, 0:n]).then_inc(s_slot[f % R].sem, 16)
            for r in range(min(R, len(split))):
                sp.wait_ge(s_slot[r].sem, s_slot[r].at(16 * len(range(r, len(split), R))))

        @block.tensor
        def _(pe):
            pe.wait_ge(s_w.sem, s_w.at(16 * len(loads)))

            def rotate(f):
                n = feature_jobs[f][2]
                pe.wait_ge(s_tk.sem, s_tk.at(f + 1))
                pe.wait_ge(s_rv.sem, s_rv.at(f - 1))
                pe.matmul(pr[:, f % 2, 0:n], m.swap[:, :], feat[:, f % R, 0:n], start=True, stop=True
                          ).then_inc(s_rot.sem, 1)

            for i in range(NJ):
                pe.wait_ge(s_tk.sem, s_tk.at(i - 3))
                if i < NF:
                    w, x, n = feature_jobs[i][:3]
                    for k in range(KD):
                        last = pe.matmul(ps[:, i % 4, 0:n], w[k], x[k], start=(k == 0), stop=(k == KD - 1))
                else:
                    x, r, w = token_jobs[i - NF][:3]
                    for k in range(KD):
                        last = pe.matmul(ps[0:r, i % 4, 0:D], x[k], w[k], start=(k == 0), stop=(k == KD - 1))
                last.then_inc(s_pr.sem, 1)
                if rope and 1 <= i <= NF:
                    rotate(i - 1)

        @block.vector
        def _(dve):
            dve.wait_ge(s_w.sem, s_w.at(16 * len(loads)))
            done = 0

            def rotated(f):
                nonlocal done
                n, (c0,) = feature_jobs[f][2], feature_jobs[f][6:7]
                dve.wait_ge(s_rot.sem, s_rot.at(f + 1))
                nc.vector.tensor_tensor(turned[:, f % R, 0:n], pr[:, f % 2, 0:n], m.sin[:, c0:c0 + n], ALU.mult
                                        ).then_inc(s_rv.sem, 1)
                dve.wait_ge(s_rv.sem, s_rv.at(f + 1))
                dve.wait_ge(s_d.sem, s_d.at(f + 1))
                nc.vector.tensor_tensor(final[:, f % R, 0:n], final[:, f % R, 0:n], turned[:, f % R, 0:n], ALU.add
                                        ).then_inc(s_f2.sem, 1)

            for i in range(NJ):
                dve.wait_ge(s_pr.sem, s_pr.at(i + 1))
                if i < NF:
                    n, bias, _, kept = feature_jobs[i][2:6]
                    dst = feat[:, i % R, 0:n] if kept is None else kept
                    if stored:
                        dve.wait_ge(s_sp.sem, s_sp.at(i - R + 1))
                    if bias is None:
                        op = nc.vector.tensor_copy(dst, ps[:, i % 4, 0:n])
                    else:
                        op = nc.vector.tensor_scalar(dst, ps[:, i % 4, 0:n], cols(m.mod, bias), None, ALU.add)
                    op.then_inc(s_tk.sem, 1)
                    if rope:
                        c0 = feature_jobs[i][6]
                        dve.wait_ge(s_tk.sem, s_tk.at(i + 1))
                        nc.vector.tensor_tensor(final[:, i % R, 0:n], feat[:, i % R, 0:n],
                                                m.cos[:, c0:c0 + n], ALU.mult).then_inc(s_d.sem, 1)
                        if i >= 1:
                            rotated(i - 1)
                else:
                    _, r, _, bias, dst = token_jobs[i - NF]
                    if rope and i == NF:
                        rotated(NF - 1)
                    if bias is None:
                        nc.vector.tensor_copy(dst, ps[0:r, i % 4, 0:D]).then_inc(s_tk.sem, 1)
                    else:
                        nc.vector.tensor_tensor(dst, ps[0:r, i % 4, 0:D], bias[0:r, :], ALU.add
                                                ).then_inc(s_tk.sem, 1)

        whole = s_f2 if rope else s_tk

        @block.scalar
        def _(act):
            for f in split:
                n = feature_jobs[f][2]
                act.wait_ge(whole.sem, whole.at(f + 1))
                if f >= R:
                    act.wait_ge(s_slot[f % R].sem, s_slot[f % R].at(16 * (f // R)))
                nc.scalar.copy(parts[:, f % R, 0, 0:n], final[:, f % R, 0:n]).then_inc(s_p1.sem, 1)
                act.wait_ge(s_r.sem, s_r.at(f + 1))
                nc.scalar.copy(parts[:, f % R, 1, 0:n], rest[:, f % R, 0:n]).then_inc(s_p2.sem, 1)

        @block.gpsimd
        def _(pool):
            for f in split:
                n = feature_jobs[f][2]
                pool.wait_ge(s_p1.sem, s_p1.at(f + 1))
                nc.gpsimd.tensor_tensor(rest[:, f % R, 0:n], final[:, f % R, 0:n], parts[:, f % R, 0, 0:n],
                                        ALU.subtract).then_inc(s_r.sem, 1)
                pool.wait_ge(s_p2.sem, s_p2.at(f + 1))
                nc.gpsimd.tensor_tensor(parts[:, f % R, 2, 0:n], rest[:, f % R, 0:n], parts[:, f % R, 1, 0:n],
                                        ALU.subtract).then_inc(s_sp.sem, 1)

    s_w.advance(16 * len(loads))
    for s in (s_pr, s_tk):
        s.advance(NJ)
    if rope:
        for s in (s_rot, s_rv, s_f2, s_d):
            s.advance(NF)
    if stored:
        for s in (s_p1, s_r, s_p2, s_sp):
            s.advance(NF)
        for r in range(R):
            s_slot[r].advance(16 * len(range(r, NF, R)))


def max_pieces(nk, items, bank, turn_after):
    out = []
    for it in items:
        for key in range(0, nk, CH):
            out.append(((it, key, min(CH, nk - key)), bank))
            bank = (bank + 1) % 3
            if len(out) == turn_after:
                out.append(("turn", bank))
                bank = (bank + 1) % 3
    return out, bank


def attention_phase(nc, m, nk, masked):
    s_kq = [m.sig["kq0"], m.sig["kq1"]]
    s_st, s_p, s_av, s_acc, s_mx, s_mt, s_nm, s_m1, s_mr, s_m2, s_ones, s_ms, s_mo, s_mi, s_v, s_init = (
        m.sig[n] for n in ("scores_ready", "probs_ready", "av_done", "acc_saved", "max_ready", "max_taken",
                           "maxes_ready", "m_part1", "m_rest", "m_part2", "ones_set", "m_parts",
                           "m_out", "m_in", "v_staged", "rows_ready"))
    KT = -(-nk // P)
    items = HG * (CH // P)
    NP = -(-nk // CH)
    LEAD = 4
    this = [(0, q) for q in range(LEAD, items)]
    ahead = [(1, q) for q in range(LEAD)]
    TURN_AT = len(this) * NP + 3
    full, end = max_pieces(nk, this + ahead, 0, TURN_AT)
    skip = -end % 3
    first_items = [(0, q) for q in range(items)] + ahead
    first, end = max_pieces(nk, first_items, -(len(first_items) * NP + 1 + skip) % 3, items * NP + 3)
    assert (end + skip) % 3 == 0 and [x[1:] for x in first[-6:]] == [x[1:] for x in full[-6:]]
    short, _ = max_pieces(nk, this, 0, len(this) * NP)

    def with_needs(stream):
        last = {b: q + 1 - len(full) for q, (_, b) in enumerate(full)}
        out = []
        for q, (piece, b) in enumerate(stream):
            out.append((piece, b, last[b]))
            last[b] = q + 1
        return out

    NFIRST, NFULL, NSHORT = len(first), len(full), len(short)
    streams = {"first": [x[:2] + (max(x[2], 0),) for x in with_needs(first)], "full": with_needs(full),
               "short": with_needs(short), "none": []}
    UB = 2 * NCH
    NU = NG * NCH
    NB = NU // UB
    assert NB == 2
    NCONST = 3 * 2 * HG
    SLOTS, HELD = 4, 2
    KQ = 16 * 2 * len(Q_PART)

    with ExitStack() as ctx:
        m.uid += 1
        sb = lambda n, s, t=F32: ctx.enter_context(nc.sbuf_tensor(f"at{m.uid}_" + n, s, t))
        kst = sb("kst", [P, 2, HG, T], BF16)
        qst = sb("qst", [P, 2, HG, T], BF16)
        probs = sb("probs", [P, 2, HG, CH])
        vst = sb("vst", [P, 2, NT, HG, 2 * DH])
        mpart = sb("mpart", [P, 2, items, NP])
        mmax = sb("mmax", [P, 2, items])
        neg = sb("neg", [items, P])
        mrest = sb("mrest", [items, P])
        zero = sb("zero", [items, P])
        mparts = sb("mparts", [items, PARTS, P], BF16)
        scores = ctx.enter_context(nc.psum_tensor(f"at{m.uid}_scores", [P, 4, CH], F32))
        acc = ctx.enter_context(nc.psum_tensor(f"at{m.uid}_acc", [P, CH], F32))
        mxp = ctx.enter_context(nc.psum_tensor(f"at{m.uid}_mxp", [P, 3, CH], F32))
        block = ctx.enter_context(nc.Block())

        def taken_before(U):
            return NFIRST + U * NFULL

        @block.sync
        def _(sp):
            def load_group(par, g):
                for c in range(len(Q_PART)):
                    rows = slice(DH * c, DH * (c + 1))
                    sp.dma_start(qst[rows, par, :, :],
                                 m.q_parts[Q_PART[c], bass.ds(g * HG * DH, HG * DH), :].rearrange(
                                     "(h d) t -> d h t", d=DH)).then_inc(s_kq[par].sem, 16)
                    sp.dma_start(kst[rows, par, :, 0:nk],
                                 m.k_parts[K_PART[c], bass.ds(g * HG * DH, HG * DH), 0:nk].rearrange(
                                     "(h d) t -> d h t", d=DH)).then_inc(s_kq[par].sem, 16)

            def spread_max(par, c, n):
                sp.wait_ge(s_ms.sem, s_ms.at(n + 1))
                sp.dma_start(m.m_scratch.rearrange("a i q -> i a q"), mparts[:, :, :]).then_inc(s_mo.sem, 16)
                sp.wait_ge(s_mo.sem, s_mo.at(16 * (n + 1)))
                sp.dma_start(qst[MAX_ROW:MAX_ROW + PARTS, par, :, c * CH:(c + 1) * CH],
                             m.m_scratch.rearrange("a (h i) q -> a h (i q)", h=HG)).then_inc(s_mi.sem, 16)

            load_group(0, 0)
            spread_max(0, 0, 0)
            with sp.Fori(0, NB) as i:
                for u in range(UB):
                    U = i * UB + u
                    if u == 0:
                        with sp.If(i < NB - 1):
                            load_group(1, 1)
                        with sp.Else():
                            sp.wait_ge(s_st.sem, s_st.at(U * 2 * KT))
                            load_group(1, 3)
                    if u == NCH:
                        with sp.If(i < NB - 1):
                            sp.wait_ge(s_st.sem, s_st.at(U * 2 * KT))
                            load_group(0, 2)
                    nxt = (u + 1) % UB
                    if u < UB - 1:
                        spread_max(nxt // NCH, nxt % NCH, U + 1)
                    else:
                        with sp.If(i < NB - 1):
                            spread_max(0, 0, U + 1)
            sp.wait_ge(s_mi.sem, s_mi.at(16 * NU))

        @block.tensor
        def _(pe):
            def take_pieces(stream, lo, hi, before, unit_of, turned):
                for piece, b, need in streams[stream][lo:hi]:
                    pe.wait_ge(s_mt.sem, s_mt.at(before + need))
                    if piece == "turn":
                        pe.wait_ge(s_nm.sem, s_nm.at(turned[1]))
                        last = pe.transpose(mxp[0:items, b, 0:P], mmax[:, turned[0], :], m.ident[:, :])
                    else:
                        (which, q), key, n = piece
                        par, c = unit_of[which]
                        h, qt = divmod(q, CH // P)
                        last = pe.matmul(mxp[:, b, 0:n],
                                         qst[0:MAX_ROW, par, h, c * CH + qt * P:c * CH + (qt + 1) * P],
                                         kst[0:MAX_ROW, par, h, key:key + n], start=True, stop=True)
                    last.then_inc(s_mx.sem, 1)

            def unit(i, u, stream):
                U = i * UB + u
                par, c = divmod(u, NCH)
                total = len(streams[stream])
                unit_of = [divmod((u + x) % UB, NCH) for x in (1, 2)]
                done = [0]

                def some(upto):
                    if done[0] <= AHEAD_AT < upto and (u + 2) % NCH == 0 and stream == "full":
                        tpar = unit_of[1][0]
                        take_pieces(stream, done[0], AHEAD_AT, taken_before(U), unit_of, ((u + 1) % 2, U + 2))
                        done[0] = AHEAD_AT
                        pe.wait_ge(s_kq[tpar].sem, s_kq[tpar].at(KQ * (i + 1) + (KQ if tpar == 0 else 0)))
                    take_pieces(stream, done[0], upto, taken_before(U), unit_of, ((u + 1) % 2, U + 2))
                    done[0] = upto

                def weigh(s):
                    pe.wait_ge(s_p.sem, s_p.at((U * KT + s) * 2 + 2))
                    if s == 0:
                        pe.wait_ge(s_acc.sem, s_acc.at(U))
                    r = tile_rows(nk, s)
                    for j in range(HG):
                        last = pe.matmul(acc[32 * j:32 * j + 2 * DH, :], vst[0:r, par, s, j, :],
                                         probs[0:r, s % 2, j, :], start=(s == 0), stop=(s == KT - 1))
                    last.then_inc(s_av.sem, 1)

                pe.wait_ge(s_mi.sem, s_mi.at(16 * (U + 1)))
                if u % NCH == 0:
                    pe.wait_ge(s_v.sem, s_v.at(1 + i * 2 + u // NCH))
                held = HELD if total > HELD else 0
                slots, at = SLOTS * KT, 0
                for s in range(KT):
                    r = tile_rows(nk, s)
                    for j in range(HG):
                        if j % 2 == 0:
                            pe.wait_ge(s_p.sem, s_p.at((U * KT + s) * 2 + j // 2 - 1))
                        last = pe.matmul(scores[0:r, j, :], kst[0:KROWS, par, j, s * P:s * P + r],
                                         qst[0:KROWS, par, j, c * CH:(c + 1) * CH], start=True, stop=True)
                        if j % 2:
                            last.then_inc(s_st.sem, 1)
                        if SLOTS == 4 or j % 2:
                            at += 1
                            some((total - held) * at // slots)
                    if s:
                        weigh(s - 1)
                some(total)
                weigh(KT - 1)

            AHEAD_AT = [n for n, (pc, _) in enumerate(full) if pc != "turn" and pc[0][0] == 1][0]
            pe.wait_ge(s_kq[0].sem, s_kq[0].at(KQ))
            pe.wait_ge(s_init.sem, s_init.at(16 * NCONST))
            take_pieces("first", 0, NFIRST, 0, [(0, 0), (0, 1)], (0, 1))
            with pe.Fori(0, NB) as i:
                for u in range(UB - 2):
                    unit(i, u, "full")
                with pe.If(i < NB - 1):
                    unit(i, UB - 2, "full")
                    unit(i, UB - 1, "full")
                with pe.Else():
                    unit(i, UB - 2, "short")
                    unit(i, UB - 1, "none")

        @block.scalar
        def _(act):
            for par in range(2):
                for h in range(HG):
                    mask = m.mask_row if masked else m.const_rows
                    act.dma_start(kst[MASK_ROW:MAX_ROW, par, h, 0:nk], mask[0:1, 0:nk]).then_inc(s_init.sem, 16)
                    act.dma_start(kst[MAX_ROW:KROWS, par, h, 0:nk], m.const_rows[1:KROWS - MASK_ROW, 0:nk]
                                  ).then_inc(s_init.sem, 16)
                    act.dma_start(qst[MASK_ROW:MAX_ROW, par, h, :], m.const_rows[1:2, :]).then_inc(s_init.sem, 16)
            with act.Fori(0, NB) as i:
                for u in range(UB):
                    U = i * UB + u
                    g, c = divmod(u, NCH)
                    for s in range(KT):
                        r = tile_rows(nk, s)
                        act.wait_ge(s_av.sem, s_av.at(U * KT + s - 1))
                        for half in range(2):
                            act.wait_ge(s_st.sem, s_st.at((U * KT + s) * 2 + half + 1))
                            nc.scalar.activation(probs[0:r, s % 2, 2 * half:2 * half + 2, :],
                                                 scores[0:r, 2 * half:2 * half + 2, :], ACT.Exp,
                                                 scale=1.0 / DH ** 0.5).then_inc(s_p.sem, 1)
                    act.wait_ge(s_av.sem, s_av.at((U + 1) * KT))
                    nc.scalar.copy(m.attn[:, bass.ds((i * 2 + g) * T + c * CH, CH)], acc[:, :]
                                   ).then_inc(s_acc.sem, 1)

        @block.vector
        def _(dve):
            def take(stream, before, next_unit, slot):
                for q, (piece, b, _) in enumerate(streams[stream]):
                    if piece == "turn":
                        dve.wait_ge(s_m1.sem, s_m1.at(next_unit))
                        dve.wait_ge(s_mr.sem, s_mr.at(next_unit))
                        dve.wait_ge(s_mx.sem, s_mx.at(before + q + 1))
                        nc.vector.tensor_scalar(neg[:, :], mxp[0:items, b, 0:P], -1.0, None, ALU.mult
                                                ).then_inc(s_mt.sem, 1)
                        continue
                    (which, item), key, n = piece
                    if item == 0 and key == 0 and which == 1:
                        dve.wait_ge(s_nm.sem, s_nm.at(next_unit))
                    dve.wait_ge(s_mx.sem, s_mx.at(before + q + 1))
                    part = key // CH
                    nc.vector.reduce_max(mpart[:, (slot + which) % 2, item, part:part + 1], mxp[:, b, 0:n], AX
                                         ).then_inc(s_mt.sem, 1)
                    if which == 0 and item == items - 1 and key + n == nk:
                        dve.wait_ge(s_mt.sem, s_mt.at(before + q + 1))
                        nc.vector.reduce_max(mmax[:, slot, :], mpart[:, slot, :, :], AX).then_inc(s_nm.sem, 1)

            take("first", 0, 0, 0)
            with dve.Fori(0, NB) as i:
                for u in range(UB - 2):
                    take("full", taken_before(i * UB + u), i * UB + u + 1, (u + 1) % 2)
                with dve.If(i < NB - 1):
                    for u in (UB - 2, UB - 1):
                        take("full", taken_before(i * UB + u), i * UB + u + 1, (u + 1) % 2)
                with dve.Else():
                    take("short", taken_before(i * UB + UB - 2), i * UB + UB - 1, 1)

        @block.gpsimd
        def _(pool):
            def stage_v(par, g):
                whole = nk // P
                for kt in range(0, whole, 4):
                    e = min(kt + 4, whole)
                    last = nc.gpsimd.tensor_copy(vst[:, par, kt:e, :, 0:DH],
                                                 m.v[:, kt:e, bass.ds(g * HG * DH, HG * DH)].rearrange(
                                                     "p t (h e) -> p t h e", e=DH))
                if nk % P:
                    r = nk % P
                    last = nc.gpsimd.tensor_copy(vst[0:r, par, whole, :, 0:DH],
                                                 m.v[0:r, whole, bass.ds(g * HG * DH, HG * DH)].rearrange(
                                                     "p (h e) -> p h e", e=DH))
                last.then_inc(s_v.sem, 1)

            def cut_max(turn_at, n):
                pool.wait_ge(s_mt.sem, s_mt.at(turn_at))
                pool.wait_ge(s_mo.sem, s_mo.at(16 * n))
                pool.wait_ge(s_mi.sem, s_mi.at(16 * n))
                nc.gpsimd.tensor_tensor(mparts[:, 0, :], neg[:, :], zero[:, :], ALU.add).then_inc(s_m1.sem, 1)
                pool.wait_ge(s_m1.sem, s_m1.at(n + 1))
                nc.gpsimd.tensor_tensor(mrest[:, :], neg[:, :], mparts[:, 0, :], ALU.subtract).then_inc(s_mr.sem, 1)
                pool.wait_ge(s_mr.sem, s_mr.at(n + 1))
                nc.gpsimd.tensor_tensor(mparts[:, 1, :], mrest[:, :], zero[:, :], ALU.add).then_inc(s_m2.sem, 1)
                pool.wait_ge(s_m2.sem, s_m2.at(n + 1))
                nc.gpsimd.tensor_tensor(mparts[:, 2, :], mrest[:, :], mparts[:, 1, :], ALU.subtract
                                        ).then_inc(s_ms.sem, 1)

            nc.gpsimd.memset(zero[:, :], 0.0)
            nc.gpsimd.memset(vst[:, :, :, :, :], 1.0).then_inc(s_ones.sem, 1)
            pool.wait_ge(s_ones.sem, s_ones.at(1))
            stage_v(0, 0)
            cut_max(items * NP + 3 + 1, 0)
            with pool.Fori(0, NB) as i:
                for u in range(UB):
                    U = i * UB + u
                    if u == 0:
                        pool.wait_ge(s_av.sem, s_av.at(U * KT))
                        stage_v(1, i * 2 + 1)
                    if u == NCH:
                        with pool.If(i < NB - 1):
                            pool.wait_ge(s_av.sem, s_av.at(U * KT))
                            stage_v(0, i + 2)   
                    if u < UB - 2:
                        cut_max(taken_before(U) + TURN_AT + 1, U + 1)
                with pool.If(i < NB - 1):
                    for u in (UB - 2, UB - 1):
                        U = i * UB + u
                        cut_max(taken_before(U) + TURN_AT + 1, U + 1)
                with pool.Else():
                    cut_max(taken_before(i * UB + UB - 2) + NSHORT, i * UB + UB - 1)

    s_kq[0].advance(2 * KQ)
    s_kq[1].advance(2 * KQ)
    s_st.advance(NU * 2 * KT)
    s_p.advance(NU * 2 * KT)
    s_av.advance(NU * KT)
    s_acc.advance(NU)
    for s in (s_mx, s_mt):
        s.advance(taken_before(NU - 2) + NSHORT)
    for s in (s_nm, s_m1, s_mr, s_m2, s_ms):
        s.advance(NU)
    s_init.advance(16 * NCONST)
    s_ones.advance(1)
    s_mo.advance(16 * NU)
    s_mi.advance(16 * NU)
    s_v.advance(NG)


def output_phase(nc, m, weight, bias, gate, extra=None):
    s_w, s_o, s_rd, s_a, s_at, s_as, s_y, s_x, s_wf, s_xb = (
        m.sig[n] for n in ("weights", "o_turned", "recip", "normalised", "a_turned", "a_saved", "y_ready",
                           "x_added", "w_folded", "x_biased"))
    nload = 1 + (bias is not None)
    with ExitStack() as ctx:
        m.uid += 1
        sb = lambda n, s, t=F32: ctx.enter_context(nc.sbuf_tensor(f"op{m.uid}_" + n, s, t))
        w = sb("w", [P, KD, D])
        bb = sb("bb", [P, D])
        rd = sb("rd", [P, 2, NH])
        a = sb("a", [P, 2, NH, DH])
        aT = sb("aT", [P, 2, KD, P])
        po = ctx.enter_context(nc.psum_tensor(f"op{m.uid}_po", [P, 2, CH], F32))
        pt = ctx.enter_context(nc.psum_tensor(f"op{m.uid}_pt", [P, 2, CH], F32))
        py = ctx.enter_context(nc.psum_tensor(f"op{m.uid}_py", [P, 2, CH], F32))
        block = ctx.enter_context(nc.Block())

        @block.sync
        def _(sp):
            sp.dma_start(w[:, :, :], weight.rearrange("(k p) n -> p k n", p=P)).then_inc(s_w.sem, 16)
            if bias is not None:
                sp.dma_start(bb[:, :], bias.partition_broadcast(P)).then_inc(s_w.sem, 16)

        @block.gpsimd
        def _(pool):
            pool.wait_ge(s_w.sem, s_w.at(16 * nload))
            if gate is not None:
                for k in range(KD):
                    last = nc.gpsimd.tensor_tensor(w[:, k, :], w[:, k, :], m.gates[:, gate, :], ALU.mult)
                last.then_inc(s_wf.sem, 1)
                nc.gpsimd.tensor_tensor(bb[:, :], bb[:, :], m.gates[:, gate, :], ALU.mult).then_inc(s_wf.sem, 1)
                pool.wait_ge(s_wf.sem, s_wf.at(2))
            if extra is not None:
                nc.gpsimd.tensor_scalar(bb[:, :], bb[:, :], extra[:, :], None, ALU.add).then_inc(s_wf.sem, 1)
                pool.wait_ge(s_wf.sem, s_wf.at(1))
            if bias is not None:
                for t in range(NT):
                    nc.gpsimd.tensor_tensor(m.x[:, t, :], m.x[:, t, :], bb[:, :], ALU.add).then_inc(s_xb.sem, 1)

        @block.tensor
        def _(pe):
            def open_heads(t):
                pe.wait_ge(s_a.sem, s_a.at(t - 1))
                for g in range(NG):
                    last = pe.transpose(po[:, t % 2, g * P:(g + 1) * P],
                                        m.attn[:, g * T + t * P:g * T + (t + 1) * P], m.ident[:, :])
                last.then_inc(s_o.sem, 1)

            def turn_back(t):
                pe.wait_ge(s_a.sem, s_a.at(t + 1))
                pe.wait_ge(s_as.sem, s_as.at(t - 1))
                for k in range(KD):
                    last = pe.transpose(pt[:, t % 2, k * P:(k + 1) * P],
                                        a[:, t % 2, k * (NH // KD):(k + 1) * (NH // KD), :].rearrange(
                                            "p h e -> p (h e)"), m.ident[:, :])
                last.then_inc(s_at.sem, 1)

            def project(t):
                pe.wait_ge(s_as.sem, s_as.at(t + 1))
                pe.wait_ge(s_x.sem, s_x.at(t - 1))
                for k in range(KD):
                    last = pe.matmul(py[:, t % 2, 0:D], aT[:, t % 2, k, :], w[:, k, :],
                                     start=(k == 0), stop=(k == KD - 1))
                last.then_inc(s_y.sem, 1)

            pe.wait_ge(s_w.sem, s_w.at(16 * nload))
            if gate is not None:
                pe.wait_ge(s_wf.sem, s_wf.at(2))
            for t in range(NT + 2):
                if t < NT:
                    open_heads(t)
                if 1 <= t <= NT:
                    turn_back(t - 1)
                if t >= 2:
                    project(t - 2)

        @block.scalar
        def _(act):
            for t in range(NT):
                act.wait_ge(s_at.sem, s_at.at(t + 1))
                act.wait_ge(s_y.sem, s_y.at(t - 1))
                nc.scalar.copy(aT[:, t % 2, :, :].rearrange("p k n -> p (k n)"), pt[:, t % 2, 0:D]
                               ).then_inc(s_as.sem, 1)

        @block.vector
        def _(dve):
            for t in range(NT + 2):
                if t < NT:
                    heads = po[:, t % 2, :].rearrange("p (h e) -> p h e", e=2 * DH)
                    dve.wait_ge(s_o.sem, s_o.at(t + 1))
                    nc.vector.reciprocal(rd[:, t % 2, :], heads[:, :, DH]).then_inc(s_rd.sem, 1)
                    dve.wait_ge(s_rd.sem, s_rd.at(t + 1))
                    dve.wait_ge(s_at.sem, s_at.at(t - 1))
                    nc.vector.tensor_tensor(a[:, t % 2, :, :], heads[:, :, 0:DH],
                                            rd[:, t % 2, :].unsqueeze(2).broadcast_to([P, NH, DH]), ALU.mult
                                            ).then_inc(s_a.sem, 1)
                if t >= 2:
                    y = t - 2
                    dve.wait_ge(s_y.sem, s_y.at(y + 1))
                    if bias is not None:
                        dve.wait_ge(s_xb.sem, s_xb.at(y + 1))
                    nc.vector.tensor_tensor(m.x[:, y, :], py[:, y % 2, 0:D], m.x[:, y, :], ALU.add
                                            ).then_inc(s_x.sem, 1)

    s_w.advance(16 * nload)
    for s in (s_o, s_rd, s_a, s_at, s_as, s_y, s_x):
        s.advance(NT)
    if gate is not None:
        s_wf.advance(2)
    if extra is not None:
        s_wf.advance(1)
    if bias is not None:
        s_xb.advance(NT)


def ffn_phase(nc, m, hT, w1, b1_col, w2, b2, gate, out):
    s_w, s_u, s_g, s_y, s_x, s_wf, s_xb, s_out = (m.sig[n] for n in (
        "weights", "up_ready", "gelu_ready", "y_ready", "x_added", "w_folded", "x_biased", "stored0"))
    NF = FF // P
    with ExitStack() as ctx:
        m.uid += 1
        sb = lambda n, s, t=F32: ctx.enter_context(nc.sbuf_tensor(f"ff{m.uid}_" + n, s, t))
        w1s = sb("w1", [P, KD, FF])
        w2s = sb("w2", [P, NF, D])
        bb = sb("bb", [P, D])
        hid = sb("hid", [P, 2, NF, CH])
        pu = ctx.enter_context(nc.psum_tensor(f"ff{m.uid}_pu", [P, 4, CH], F32))
        py = ctx.enter_context(nc.psum_tensor(f"ff{m.uid}_py", [P, 2, CH], F32))
        block = ctx.enter_context(nc.Block())

        @block.sync
        def _(sp):
            sp.dma_start(w1s[:, :, :], w1.rearrange("(k p) n -> p k n", p=P)).then_inc(s_w.sem, 16)
            sp.dma_start(w2s[:, :, :], w2.rearrange("(k p) n -> p k n", p=P)).then_inc(s_w.sem, 16)
            sp.dma_start(bb[:, :], b2.partition_broadcast(P)).then_inc(s_w.sem, 16)
            if out is not None:
                for c in range(NCH):
                    sp.wait_ge(s_x.sem, s_x.at(4 * c + 4))
                    sp.dma_start(out[c * CH:(c + 1) * CH, :].rearrange("(t p) n -> p t n", p=P),
                                 m.x[:, 4 * c:4 * c + 4, :]).then_inc(s_out.sem, 16)
                sp.wait_ge(s_out.sem, s_out.at(16 * NCH))

        @block.gpsimd
        def _(pool):
            pool.wait_ge(s_w.sem, s_w.at(48))
            if gate is not None:
                for k in range(NF):
                    last = nc.gpsimd.tensor_tensor(w2s[:, k, :], w2s[:, k, :], m.gates[:, gate, :], ALU.mult)
                last.then_inc(s_wf.sem, 1)
                nc.gpsimd.tensor_tensor(bb[:, :], bb[:, :], m.gates[:, gate, :], ALU.mult).then_inc(s_wf.sem, 1)
                pool.wait_ge(s_wf.sem, s_wf.at(2))
            for t in range(NT):
                nc.gpsimd.tensor_tensor(m.x[:, t, :], m.x[:, t, :], bb[:, :], ALU.add).then_inc(s_xb.sem, 1)

        @block.tensor
        def _(pe):
            def up(c):
                for f in range(NF):
                    i = c * NF + f
                    pe.wait_ge(s_g.sem, s_g.at(i - 3))
                    for k in range(KD):
                        last = pe.matmul(pu[:, i % 4, :], w1s[:, k, f * P:(f + 1) * P],
                                         hT[:, k, c * CH:(c + 1) * CH], start=(k == 0), stop=(k == KD - 1))
                    last.then_inc(s_u.sem, 1)

            def down(c):
                pe.wait_ge(s_g.sem, s_g.at((c + 1) * NF))
                for q in range(4):
                    t = 4 * c + q
                    pe.wait_ge(s_x.sem, s_x.at(t - 1))
                    for f in range(NF):
                        last = pe.matmul(py[:, t % 2, 0:D], hid[:, c % 2, f, q * P:(q + 1) * P], w2s[:, f, :],
                                         start=(f == 0), stop=(f == NF - 1))
                    last.then_inc(s_y.sem, 1)

            pe.wait_ge(s_w.sem, s_w.at(48))
            up(0)
            if gate is not None:
                pe.wait_ge(s_wf.sem, s_wf.at(2))
            for c in range(NCH):
                if c + 1 < NCH:
                    up(c + 1)
                down(c)

        @block.scalar
        def _(act):
            for i in range(NCH * NF):
                c, f = divmod(i, NF)
                act.wait_ge(s_u.sem, s_u.at(i + 1))
                if c >= 2 and f == 0:
                    act.wait_ge(s_y.sem, s_y.at(4 * (c - 1)))
                nc.scalar.activation(hid[:, c % 2, f, :], pu[:, i % 4, :], ACT.Gelu, bias=cols(m.mod, b1_col + f)
                                     ).then_inc(s_g.sem, 1)

        @block.vector
        def _(dve):
            for t in range(NT):
                dve.wait_ge(s_y.sem, s_y.at(t + 1))
                dve.wait_ge(s_xb.sem, s_xb.at(t + 1))
                nc.vector.tensor_tensor(m.x[:, t, :], py[:, t % 2, 0:D], m.x[:, t, :], ALU.add
                                        ).then_inc(s_x.sem, 1)

    s_w.advance(48)
    s_u.advance(NCH * NF)
    s_g.advance(NCH * NF)
    for s in (s_y, s_x, s_xb):
        s.advance(NT)
    if gate is not None:
        s_wf.advance(2)
    if out is not None:
        s_out.advance(16 * NCH)


def evidence_phase(nc, m, qT, kT, evT):
    s_sc, s_mx, s_nb, s_e, s_rd, s_pn, s_tr, s_ts, s_ev, s_es = (m.sig[n] for n in (
        "scores_ready", "max_ready", "neg_ready", "probs_ready", "recip", "normalised", "turned", "turn_saved",
        "av_done", "acc_saved"))
    GROUPS = [(g, min(g + 4, NC2)) for g in range(0, NC2, 4)]
    NGR = len(GROUPS)
    SC = 1.0 / D ** 0.5
    with ExitStack() as ctx:
        m.uid += 1
        sb = lambda n, s, t=F32: ctx.enter_context(nc.sbuf_tensor(f"ev{m.uid}_" + n, s, t))
        probs = sb("probs", [P, 2, NS2])
        probsT = sb("probsT", [P, NC2, CH])
        mx = sb("mx", [P, NT])
        nb = sb("nb", [P, NT])
        den = sb("den", [P, NT])
        rden = sb("rden", [P, NT])
        ps = ctx.enter_context(nc.psum_tensor(f"ev{m.uid}_ps", [P, 4, CH], F32))
        pt = ctx.enter_context(nc.psum_tensor(f"ev{m.uid}_pt", [P, 2, CH], F32))
        po = ctx.enter_context(nc.psum_tensor(f"ev{m.uid}_po", [P, 2, CH], F32))
        allkeys = ps[:, :, :].rearrange("p a b -> p (a b)")[:, 0:NS2]
        block = ctx.enter_context(nc.Block())

        @block.tensor
        def _(pe):
            def score(t):
                pe.wait_ge(s_e.sem, s_e.at(t))
                for b in range(4):
                    n = min(CH, NS2 - b * CH)
                    for k in range(KD):
                        last = pe.matmul(ps[:, b, 0:n], qT[:, k, t * P:(t + 1) * P], kT[:, k, b * CH:b * CH + n],
                                         start=(k == 0), stop=(k == KD - 1))
                last.then_inc(s_sc.sem, 1)

            def turn(t):
                pe.wait_ge(s_pn.sem, s_pn.at(t + 1))
                for g, (a, b) in enumerate(GROUPS):
                    i = t * NGR + g
                    pe.wait_ge(s_ts.sem, s_ts.at(i - 1))
                    for kt in range(a, b):
                        r = tile_rows(NS2, kt)
                        last = pe.transpose(pt[0:r, i % 2, (kt - a) * P:(kt - a + 1) * P],
                                            probs[:, t % 2, kt * P:kt * P + r], m.ident[:, :])
                    last.then_inc(s_tr.sem, 1)

            def weigh(c):
                pe.wait_ge(s_ts.sem, s_ts.at(NGR * 4 * (c + 1)))
                for k in range(KD):
                    pe.wait_ge(s_es.sem, s_es.at(KD * c + k - 1))
                    for kt in range(NC2):
                        r = tile_rows(NS2, kt)
                        last = pe.matmul(po[:, k, :], m.v[0:r, kt, k * P:(k + 1) * P], probsT[0:r, kt, :],
                                         start=(kt == 0), stop=(kt == NC2 - 1))
                    last.then_inc(s_ev.sem, 1)

            for t in range(NT + 1):
                if t < NT:
                    score(t)
                if t >= 1:
                    turn(t - 1)
                    if t % 4 == 0:
                        weigh(t // 4 - 1)

        @block.vector
        def _(dve):
            def save(c):
                for k in range(KD):
                    dve.wait_ge(s_ev.sem, s_ev.at(KD * c + k + 1))
                    nc.vector.tensor_copy(evT[:, k, c * CH:(c + 1) * CH], po[:, k, :]).then_inc(s_es.sem, 1)

            for t in range(NT + 1):
                if t < NT:
                    dve.wait_ge(s_sc.sem, s_sc.at(t + 1))
                    nc.vector.reduce_max(cols(mx, t), allkeys, AX).then_inc(s_mx.sem, 1)
                    dve.wait_ge(s_mx.sem, s_mx.at(t + 1))
                    nc.vector.tensor_scalar(cols(nb, t), cols(mx, t), -SC, None, ALU.mult).then_inc(s_nb.sem, 1)
                    dve.wait_ge(s_e.sem, s_e.at(t + 1))
                    nc.vector.reciprocal(cols(rden, t), cols(den, t)).then_inc(s_rd.sem, 1)
                    dve.wait_ge(s_rd.sem, s_rd.at(t + 1))
                    nc.vector.tensor_scalar(probs[:, t % 2, :], probs[:, t % 2, :], cols(rden, t), None, ALU.mult
                                            ).then_inc(s_pn.sem, 1)
                    if t % 4 == 0 and t:
                        save(t // 4 - 1)
            save(NCH - 1)

        @block.scalar
        def _(act):
            def save_turned(t):
                for g, (a, b) in enumerate(GROUPS):
                    i = t * NGR + g
                    r = tile_rows(NS2, a)
                    act.wait_ge(s_tr.sem, s_tr.at(i + 1))
                    if t % 4 == 0 and g == 0 and t:
                        act.wait_ge(s_ev.sem, s_ev.at(KD * (t // 4)))
                    nc.scalar.copy(probsT[0:r, a:b, (t % 4) * P:(t % 4 + 1) * P],
                                   pt[0:r, i % 2, 0:(b - a) * P].rearrange("p (a b) -> p a b", b=P)
                                   ).then_inc(s_ts.sem, 1)

            for t in range(NT + 1):
                if t < NT:
                    act.wait_ge(s_nb.sem, s_nb.at(t + 1))
                    act.wait_ge(s_tr.sem, s_tr.at(NGR * (t - 1)) if t else s_tr.at(0))
                    nc.scalar.activation(probs[:, t % 2, :], allkeys, ACT.Exp, bias=cols(nb, t), scale=SC,
                                         accum_out=cols(den, t)).then_inc(s_e.sem, 1)
                if t >= 1:
                    save_turned(t - 1)

    for s in (s_sc, s_mx, s_nb, s_e, s_rd, s_pn):
        s.advance(NT)
    for s in (s_tr, s_ts):
        s.advance(NT * NGR)
    for s in (s_ev, s_es):
        s.advance(NCH * KD)


def fold_phase(nc, m, d, w2o, b2o):
    s_w, s_pr, s_tk, s_o, s_bc = (m.sig[n] for n in ("weights", "proj_ready", "proj_taken", "ones", "cond_bc"))
    RT = RH // P
    with ExitStack() as ctx:
        m.uid += 1
        sb = lambda n, s, t=F32: ctx.enter_context(nc.sbuf_tensor(f"fo{m.uid}_" + n, s, t))
        w2T = sb("w2T", [P, NE, KD, RH])
        ow = sb("ow", [P, KD, D])
        ob = sb("ob", [P, D])
        b2 = sb("b2", [P, NE, KD])
        b2bc = sb("b2bc", [P, NE, KD, P])
        ones = sb("ones", [P, P])
        ps = ctx.enter_context(nc.psum_tensor(f"fo{m.uid}_ps", [P, 4, CH], F32))
        block = ctx.enter_context(nc.Block())

        @block.sync
        def _(sp):
            for e in range(NE):
                sp.dma_start(w2T[:, e], d["e_w2T"][e].rearrange("(k p) r -> p k r", p=P)).then_inc(s_w.sem, 16)
            sp.dma_start(ow[:, :, :], d["L2_xcond_out_w"].rearrange("(k p) n -> p k n", p=P)).then_inc(s_w.sem, 16)
            sp.dma_start(ob[:, :], d["L2_xcond_out_b"].partition_broadcast(P)).then_inc(s_w.sem, 16)
            sp.dma_start(b2[:, :, :], d["e_b2_cols"].rearrange("p (e k) -> p e k", e=NE)).then_inc(s_w.sem, 16)

        @block.gpsimd
        def _(pool):
            nc.gpsimd.memset(ones[:, :], 1.0).then_inc(s_o.sem, 1)

        @block.tensor
        def _(pe):
            pe.wait_ge(s_w.sem, s_w.at(96))
            pe.wait_ge(s_bc.sem, s_bc.at(1))
            for i in range(NE * (RT + 1)):
                e, r = divmod(i, RT + 1)
                pe.wait_ge(s_tk.sem, s_tk.at(i - 3))
                for k in range(KD):
                    lhs = w2T[:, e, k, r * P:(r + 1) * P] if r < RT else b2bc[:, e, k, :]
                    last = pe.matmul(ps[:, i % 4, 0:D], lhs, ow[:, k, :], start=(k == 0), stop=(k == KD - 1))
                last.then_inc(s_pr.sem, 1)

        @block.vector
        def _(dve):
            dve.wait_ge(s_w.sem, s_w.at(96))
            dve.wait_ge(s_o.sem, s_o.at(1))
            for e in range(NE):
                for k in range(KD):
                    last = nc.vector.tensor_scalar(b2bc[:, e, k, :], ones[:, :], b2[:, e, k:k + 1], None, ALU.mult)
            last.then_inc(s_bc.sem, 1)
            for i in range(NE * (RT + 1)):
                e, r = divmod(i, RT + 1)
                dve.wait_ge(s_pr.sem, s_pr.at(i + 1))
                if r < RT:
                    nc.vector.tensor_copy(w2o[:, e, r, :], ps[:, i % 4, 0:D]).then_inc(s_tk.sem, 1)
                else:
                    nc.vector.tensor_tensor(b2o[:, e, :], ps[:, i % 4, 0:D], ob[:, :], ALU.add).then_inc(s_tk.sem, 1)

    s_w.advance(96)
    s_o.advance(1)
    s_bc.advance(1)
    for s in (s_pr, s_tk):
        s.advance(NE * (RT + 1))


def expert_phase(nc, m, d, nxT, evT, w2o, b2o):
    (s_w, s_u, s_g, s_r, s_rl, s_rm, s_rs, s_re, s_rt, s_rr, s_pb, s_gz, s_gp, s_gs, s_y, s_yt, s_ya, s_gy, s_x) = (
        m.sig[n] for n in ("weights", "up_ready", "gelu_ready", "r_ready", "r_logits", "r_max", "r_shifted",
                           "r_exp", "r_sum", "r_recip", "r_probs", "gate_ready", "gate_biased", "gate_open",
                           "y_ready", "y_biased", "y_summed", "y_gated", "x_added"))
    RT = RH // P
    KC = 2 * KD
    NU = KD + NE * RT
    with ExitStack() as ctx:
        m.uid += 1
        sb = lambda n, s, t=F32: ctx.enter_context(nc.sbuf_tensor(f"ex{m.uid}_" + n, s, t))
        w1 = sb("w1", [P, NE, KC, RH])
        gw1 = sb("gw1", [P, KC, D])
        gw2 = sb("gw2", [P, KD, D])
        gb2 = sb("gb2", [P, D])
        rw = sb("rw", [P, KC, NE])
        hid = sb("hid", [P, 2, NU, CH])
        logit = sb("logit", [P, 4, NE])
        rmax = sb("rmax", [P, 4])
        rexp = sb("rexp", [P, 4, NE])
        rsum = sb("rsum", [P, 4])
        prob = sb("prob", [P, 4, NE])
        gate = sb("gate", [P, 4, D])
        biased = sb("biased", [P, NE, D])
        summed = sb("summed", [P, D])
        pu = ctx.enter_context(nc.psum_tensor(f"ex{m.uid}_pu", [P, 2, CH], F32))
        pr = ctx.enter_context(nc.psum_tensor(f"ex{m.uid}_pr", [P, CH], F32))
        pg = ctx.enter_context(nc.psum_tensor(f"ex{m.uid}_pg", [P, 2, CH], F32))
        py = ctx.enter_context(nc.psum_tensor(f"ex{m.uid}_py", [P, NE, CH], F32))
        block = ctx.enter_context(nc.Block())
        NL = NE + 4
        moving = lambda k, c: (nxT if k < KD else evT)[:, k % KD, c * CH:(c + 1) * CH]
        stationary = lambda k, t: (nxT if k < KD else evT)[:, k % KD, t * P:(t + 1) * P]

        @block.sync
        def _(sp):
            for e in range(NE):
                sp.dma_start(w1[:, e], d["L2_xcond_e_w1"][e, 0:2 * D, :].rearrange("(k p) n -> p k n", p=P)
                             ).then_inc(s_w.sem, 16)
            sp.dma_start(gw1[:, :, :], d["L2_xcond_gate_w1"][0:2 * D, :].rearrange("(k p) n -> p k n", p=P)
                         ).then_inc(s_w.sem, 16)
            sp.dma_start(gw2[:, :, :], d["L2_xcond_gate_w2"].rearrange("(k p) n -> p k n", p=P)
                         ).then_inc(s_w.sem, 16)
            sp.dma_start(gb2[:, :], d["L2_xcond_gate_b2"].partition_broadcast(P)).then_inc(s_w.sem, 16)
            sp.dma_start(rw[:, :, :], d["L2_xcond_router_W"][0:2 * D, :].rearrange("(k p) n -> p k n", p=P)
                         ).then_inc(s_w.sem, 16)

        @block.tensor
        def _(pe):
            def up(c):
                for f in range(NU):
                    i = c * NU + f
                    pe.wait_ge(s_g.sem, s_g.at(i - 1))
                    for k in range(KC):
                        if f < KD:
                            w = gw1[:, k, f * P:(f + 1) * P]
                        else:
                            e, r = divmod(f - KD, RT)
                            w = w1[:, e, k, r * P:(r + 1) * P]
                        last = pe.matmul(pu[:, i % 2, :], w, moving(k, c), start=(k == 0), stop=(k == KC - 1))
                    last.then_inc(s_u.sem, 1)

            def route(c):
                pe.wait_ge(s_rl.sem, s_rl.at(c))
                for q in range(4):
                    for k in range(KC):
                        last = pe.matmul(pr[:, q * NE:(q + 1) * NE], stationary(k, 4 * c + q), rw[:, k, :],
                                         start=(k == 0), stop=(k == KC - 1))
                last.then_inc(s_r.sem, 1)

            def open_gate(c):
                pe.wait_ge(s_g.sem, s_g.at(c * NU + KD))
                pe.wait_ge(s_gp.sem, s_gp.at(c))
                for q in range(4):
                    for k in range(KD):
                        last = pe.matmul(pg[:, q // 2, (q % 2) * D:(q % 2 + 1) * D],
                                         hid[:, c % 2, k, q * P:(q + 1) * P], gw2[:, k, :],
                                         start=(k == 0), stop=(k == KD - 1))
                last.then_inc(s_gz.sem, 1)

            def down(c):
                pe.wait_ge(s_g.sem, s_g.at((c + 1) * NU))
                for q in range(4):
                    for e in range(NE):
                        i = (4 * c + q) * NE + e
                        pe.wait_ge(s_yt.sem, s_yt.at(i - NE + 1))
                        for r in range(RT):
                            last = pe.matmul(py[:, e, 0:D], hid[:, c % 2, KD + e * RT + r, q * P:(q + 1) * P],
                                             w2o[:, e, r, :], start=(r == 0), stop=(r == RT - 1))
                        last.then_inc(s_y.sem, 1)

            pe.wait_ge(s_w.sem, s_w.at(16 * NL))
            up(0)
            for c in range(NCH):
                route(c)
                open_gate(c)
                if c + 1 < NCH:
                    up(c + 1)
                down(c)

        @block.scalar
        def _(act):
            def silus(c):
                for f in range(NU):
                    i = c * NU + f
                    act.wait_ge(s_u.sem, s_u.at(i + 1))
                    if f == 0 and c >= 2:
                        act.wait_ge(s_y.sem, s_y.at(4 * NE * (c - 1)))
                    b = m.col["gb1"] + f if f < KD else m.col["eb1"] + f - KD
                    nc.scalar.activation(hid[:, c % 2, f, :], pu[:, i % 2, :], ACT.Silu, bias=cols(m.mod, b)
                                         ).then_inc(s_g.sem, 1)

            silus(0)
            for c in range(NCH):
                act.wait_ge(s_rs.sem, s_rs.at(c + 1))
                nc.scalar.activation(rexp[:, :, :], logit[:, :, :], ACT.Exp).then_inc(s_re.sem, 1)
                act.wait_ge(s_gp.sem, s_gp.at(c + 1))
                nc.scalar.activation(gate[:, :, :], gate[:, :, :], ACT.Sigmoid).then_inc(s_gs.sem, 1)
                if c + 1 < NCH:
                    silus(c + 1)

        @block.vector
        def _(dve):
            dve.wait_ge(s_w.sem, s_w.at(16 * NL))
            for c in range(NCH):
                dve.wait_ge(s_r.sem, s_r.at(c + 1))
                nc.vector.tensor_tensor(logit[:, :, :], pr[:, 0:4 * NE].rearrange("p (q e) -> p q e", e=NE),
                                        m.router_bias[:, :].unsqueeze(1).broadcast_to([P, 4, NE]), ALU.add
                                        ).then_inc(s_rl.sem, 1)
                dve.wait_ge(s_rl.sem, s_rl.at(c + 1))
                nc.vector.reduce_max(rmax[:, :], logit[:, :, :], AX).then_inc(s_rm.sem, 1)
                dve.wait_ge(s_rm.sem, s_rm.at(c + 1))
                nc.vector.tensor_tensor(logit[:, :, :], logit[:, :, :],
                                        rmax[:, :].unsqueeze(2).broadcast_to([P, 4, NE]), ALU.subtract
                                        ).then_inc(s_rs.sem, 1)
                dve.wait_ge(s_gz.sem, s_gz.at(c + 1))
                nc.vector.tensor_tensor(gate[:, :, :], pg[:, :, :].rearrange("p a (b n) -> p (a b) n", n=D),
                                        gb2[:, :].unsqueeze(1).broadcast_to([P, 4, D]), ALU.add
                                        ).then_inc(s_gp.sem, 1)
                dve.wait_ge(s_re.sem, s_re.at(c + 1))
                nc.vector.reduce_sum(rsum[:, :], rexp[:, :, :], AX).then_inc(s_rt.sem, 1)
                dve.wait_ge(s_rt.sem, s_rt.at(c + 1))
                nc.vector.reciprocal(rmax[:, :], rsum[:, :]).then_inc(s_rr.sem, 1)
                dve.wait_ge(s_rr.sem, s_rr.at(c + 1))
                nc.vector.tensor_tensor(prob[:, :, :], rexp[:, :, :],
                                        rmax[:, :].unsqueeze(2).broadcast_to([P, 4, NE]), ALU.mult
                                        ).then_inc(s_pb.sem, 1)
                dve.wait_ge(s_pb.sem, s_pb.at(c + 1))
                dve.wait_ge(s_gs.sem, s_gs.at(c + 1))
                for q in range(4):
                    t = 4 * c + q
                    for e in range(NE):
                        i = t * NE + e
                        dve.wait_ge(s_y.sem, s_y.at(i + 1))
                        nc.vector.tensor_tensor(biased[:, e, :], py[:, e, 0:D], b2o[:, e, :], ALU.add
                                                ).then_inc(s_yt.sem, 1)
                        dve.wait_ge(s_yt.sem, s_yt.at(i + 1))
                        p = prob[:, q, e:e + 1]
                        if e == 0:
                            op = nc.vector.tensor_scalar(summed[:, :], biased[:, e, :], p, None, ALU.mult)
                        else:
                            dve.wait_ge(s_ya.sem, s_ya.at(i))
                            op = nc.vector.scalar_tensor_tensor(out=summed[:, :], in0=biased[:, e, :], scalar=p,
                                                                in1=summed[:, :], op0=ALU.mult, op1=ALU.add)
                        op.then_inc(s_ya.sem, 1)
                    dve.wait_ge(s_ya.sem, s_ya.at((t + 1) * NE))
                    nc.vector.tensor_tensor(summed[:, :], summed[:, :], gate[:, q, :], ALU.mult).then_inc(s_gy.sem, 1)
                    dve.wait_ge(s_gy.sem, s_gy.at(t + 1))
                    nc.vector.tensor_tensor(m.x[:, t, :], m.x[:, t, :], summed[:, :], ALU.add).then_inc(s_x.sem, 1)

    s_w.advance(16 * NL)
    for s in (s_u, s_g):
        s.advance(NCH * NU)
    for s in (s_r, s_rl, s_rm, s_rs, s_re, s_rt, s_rr, s_pb, s_gz, s_gp, s_gs):
        s.advance(NCH)
    for s in (s_y, s_yt, s_ya):
        s.advance(NT * NE)
    for s in (s_gy, s_x):
        s.advance(NT)


def mask_phase(nc, m, d):
    s_w, s_d, s_o = (m.sig[n] for n in ("weights", "dve", "stored0"))
    with ExitStack() as ctx:
        sb = lambda n, s, t=F32: ctx.enter_context(nc.sbuf_tensor("mk_" + n, s, t))
        raw = sb("raw", [P, -(-NS2 // 4)], mybir.dt.int32)
        as_f = sb("as_f", [P, NS2])
        row = sb("row", [1, NS2], BF16)
        const = sb("const", [1, 2, T], BF16)
        left = sb("left", [P, 1])
        inv = sb("inv", [P, 1])
        block = ctx.enter_context(nc.Block())

        @block.sync
        def _(sp):
            sp.dma_start(raw[:, :], d["mask"].rearrange("a n -> (a n)").partition_broadcast(P)).then_inc(s_w.sem, 16)
            sp.wait_ge(s_d.sem, s_d.at(2))
            sp.dma_start(m.mask_row[:, :], row[:, :]).then_inc(s_o.sem, 16)
            sp.wait_ge(m.sig["ones"].sem, m.sig["ones"].at(2))
            for r in range(KROWS - MASK_ROW):
                sp.dma_start(m.const_rows[r:r + 1, :], const[:, min(r, 1), :]).then_inc(s_o.sem, 16)
            sp.wait_ge(s_o.sem, s_o.at(16 * (1 + KROWS - MASK_ROW)))

        @block.gpsimd
        def _(pool):
            nc.gpsimd.memset(const[:, 0, :], 0.0).then_inc(m.sig["ones"].sem, 1)
            nc.gpsimd.memset(const[:, 1, :], 1.0).then_inc(m.sig["ones"].sem, 1)

        @block.vector
        def _(dve):
            dve.wait_ge(s_w.sem, s_w.at(16))
            nc.vector.tensor_copy(as_f[:, :], raw[:, :].bitcast(U8)[:, 0:NS2]).then_inc(s_d.sem, 1)
            dve.wait_ge(s_d.sem, s_d.at(1))
            nc.vector.tensor_scalar(row[:, :], as_f[0:1, :], MASK_BIAS, None, ALU.mult).then_inc(s_d.sem, 1)
            nc.vector.reduce_sum(left[:, :], as_f[:, :], AX).then_inc(s_d.sem, 1)
            dve.wait_ge(s_d.sem, s_d.at(3))
            nc.vector.tensor_scalar(left[:, :], left[:, :], -1.0, float(NS2), ALU.mult, ALU.add).then_inc(s_d.sem, 1)
            dve.wait_ge(s_d.sem, s_d.at(4))
            nc.vector.reciprocal(inv[:, :], left[:, :]).then_inc(s_d.sem, 1)
            dve.wait_ge(s_d.sem, s_d.at(5))
            nc.vector.tensor_scalar(m.none_left[:, :], inv[:, :], 0.0, None, ALU.mult).then_inc(s_d.sem, 1)

    s_w.advance(16)
    s_d.advance(6)
    s_o.advance(16 * (1 + KROWS - MASK_ROW))
    m.sig["ones"].advance(2)


SIGNALS = """load weights cond_ready mod_ready mod_saved stats rstd normed turned turn_saved ones cond_bc dve
cols_ready proj_ready proj_taken rot_ready rot_taken feat_final part1 rest part2 parts_ready stored0 stored1
stored2 stored3 kq0 kq1 scores_ready probs_ready av_done acc_saved max_ready max_taken maxes_ready neg_ready
m_part1 m_rest m_part2 ones_set m_parts m_out m_in v_staged rows_ready o_turned recip normalised
a_turned a_saved y_ready x_added w_folded x_biased up_ready gelu_ready r_ready r_logits r_max r_shifted r_exp
r_sum r_recip r_probs gate_ready gate_biased gate_open y_biased y_summed y_gated""".split()


def build(nc, d, out):
    m = Machine()
    m.uid = 0
    m.L = NS2 - (NC2 - 1) * P
    m.col, at = {}, 0
    for name, n in (("l0", 12), ("l1", 8), ("l3", 12), ("eb1", NE * RH // P), ("gb1", KD), ("ln2g", KD), ("ln2b", KD),
                    ("l0b1", FF // P), ("l3b1", FF // P), ("l1q", KD), ("l1k", KD), ("l3q", KD), ("l3k", KD),
                    ("l3cq", KD), ("l3ck", KD)):
        m.col[name] = at
        at += n
    m.NCOL = at
    with ExitStack() as ctx:
        sb = lambda n, s, t=F32: ctx.enter_context(nc.sbuf_tensor(n, s, t))
        m.sig = {n: Signal(ctx.enter_context(nc.semaphore(n))) for n in SIGNALS}
        m.x = sb("x_sb", [P, NT, D])
        m.v = sb("v_sb", [P, NT, D])
        m.attn = sb("attn", [P, NG * T])
        m.ctxT = sb("ctxT", [P, KD, NS2])
        m.ctxnT = sb("ctxnT", [P, KD, NS2])
        m.ident = sb("ident_sb", [P, P])
        m.mod = sb("mod", [P, m.NCOL])
        m.gates = sb("gates", [P, 2, D])
        m.router_bias = sb("router_bias", [P, NE])
        m.none_left = sb("none_left", [P, 1])
        dram = lambda n, s, t: nc.dram_tensor(n, s, t, kind="Internal").ap()
        m.q_parts = dram("q_parts", (PARTS, D, T), BF16)
        m.k_parts = dram("k_parts", (PARTS, D, T), BF16)
        m.m_scratch = dram("m_scratch", (PARTS, HG * CH // P, P), BF16)
        m.mask_row = dram("mask_row", (1, NS2), BF16)
        m.const_rows = dram("const_rows", (KROWS - MASK_ROW, T), BF16)
        hT = m.attn[:, 0:KD * T].rearrange("p (k t) -> p k t", k=KD)
        evT = m.attn[:, KD * T:2 * KD * T].rearrange("p (k t) -> p k t", k=KD)
        c = m.col

        with nc.Block() as block:
            @block.sync
            def _(sp):
                for s in m.sig.values():
                    sp.sem_inc(s.sem, CREDIT)

        setup_phase(nc, m, d)
        mask_phase(nc, m, d)

        def feature(w, wcol, src, n_src, bias, parts, keep=None):
            jobs = []
            for c0 in range(0, n_src, CH):
                n = min(CH, n_src - c0)
                for f in range(KD):
                    lhs = [w[:, k, wcol + f * P:wcol + (f + 1) * P] for k in range(KD)]
                    rhs = [src[:, k, c0:c0 + n] for k in range(KD)]
                    store = None if parts is None else parts[:, f * P:(f + 1) * P, c0:c0 + n].rearrange("a p t -> p a t")
                    kept = None if keep is None else keep[:, f, c0:c0 + n]
                    jobs.append((lhs, rhs, n, None if bias is None else bias + f, store, kept, c0))
            return jobs

        def token(w, wcol, src, n_src, bias_bc):
            jobs = []
            for t in range(-(-n_src // P)):
                r = tile_rows(n_src, t)
                jobs.append(([src[:, k, t * P:t * P + r] for k in range(KD)], r,
                             [w[:, k, wcol:wcol + D] for k in range(KD)], bias_bc, m.v[0:r, t, :]))
            return jobs

        def view(name):
            return d[name].rearrange("(k p) n -> p k n", p=P)

        def qkv(name, q, k, v, rope, k_src, nk, keep=None):
            with ExitStack() as cx:
                m.uid += 1
                tiles, loads = {}, []
                for w, _, _ in (q, k, v):
                    if w not in tiles:
                        n = d[w].shape[1]
                        tiles[w] = cx.enter_context(nc.sbuf_tensor(f"w{m.uid}_{len(tiles)}", [P, KD, n], F32))
                        loads.append((tiles[w][:, :, :], view(w)))
                if rope:
                    m.swap = cx.enter_context(nc.sbuf_tensor(f"swap{m.uid}", [P, P], F32))
                    m.cos = cx.enter_context(nc.sbuf_tensor(f"cos{m.uid}", [P, T], F32))
                    m.sin = cx.enter_context(nc.sbuf_tensor(f"sin{m.uid}", [P, T], F32))
                    for a, b in ((m.swap, "swap"), (m.cos, "cos"), (m.sin, "sin")):
                        loads.append((a[:, :], d[b]))
                bias = None
                if v[2] is not None:
                    bias = cx.enter_context(nc.sbuf_tensor(f"vb{m.uid}", [P, D], F32))
                    loads.append((bias[:, :], v[2].partition_broadcast(P)))
                store = keep is None
                fj = feature(tiles[k[0]], k[1], k_src, nk, k[2], m.k_parts if store else None,
                             None if store else keep[1])
                fj += feature(tiles[q[0]], q[1], hT, T, q[2], m.q_parts if store else None,
                              None if store else keep[0])
                projection_phase(nc, m, loads, fj, token(tiles[v[0]], v[1], k_src, nk, bias), rope)

        norm_phase(nc, m, hT, 1e-5, c["l0"], c["l0"] + 2)
        qkv("l0s", ("l0_qkv_wT", 0, None), ("l0_qkv_wT", D, None), ("l0_qkv_wT", 2 * D, None), True, hT, T)
        attention_phase(nc, m, T, False)
        output_phase(nc, m, d["l0_sa_wT"], None, None)
        norm_phase(nc, m, hT, 1e-5, c["l0"] + 4, c["l0"] + 6)
        qkv("l0c", ("l0_q_wT", 0, None), ("l0_k_wT", 0, None), ("l0_v_wT", 0, None), True, m.ctxT, NS2)
        attention_phase(nc, m, NS2, False)
        output_phase(nc, m, d["l0_ca_wT"], None, None)
        norm_phase(nc, m, hT, 1e-5, c["l0"] + 8, c["l0"] + 10)
        ffn_phase(nc, m, hT, d["l0_w1T"], c["l0b1"], d["l0_w2T"], d["L0_xcond_ffn_b2"], None, None)
        norm_phase(nc, m, hT, 1e-5, c["l1"], c["l1"] + 2)
        qkv("l1", ("L1_xcond_Wq", 0, c["l1q"]), ("L1_xcond_Wkv", 0, c["l1k"]),
            ("L1_xcond_Wkv", D, d["L1_xcond_bkv"][D:2 * D]), False, m.ctxnT, NS2)
        attention_phase(nc, m, NS2, False)
        output_phase(nc, m, d["L1_xcond_Wp"], d["L1_xcond_bp"], None)
        norm_phase(nc, m, hT, 1e-5, c["ln2g"], c["ln2b"])
        with ExitStack() as cx:
            q2T = cx.enter_context(nc.sbuf_tensor("q2T", [P, KD, T], F32))
            k2T = cx.enter_context(nc.sbuf_tensor("k2T", [P, KD, NS2], F32))
            qkv("l2", ("L2_xcond_Wq", 0, None), ("L2_xcond_Wk", 0, None), ("L2_xcond_Wv", 0, None), False,
                m.ctxT, NS2, keep=(q2T, k2T))
            evidence_phase(nc, m, q2T, k2T, evT)
        with ExitStack() as cx:
            w2o = cx.enter_context(nc.sbuf_tensor("w2o", [P, NE, RH // P, D], F32))
            b2o = cx.enter_context(nc.sbuf_tensor("b2o", [P, NE, D], F32))
            fold_phase(nc, m, d, w2o, b2o)
            expert_phase(nc, m, d, hT, evT, w2o, b2o)
        norm_phase(nc, m, hT, 1e-6, c["l3"] + 2, c["l3"])
        qkv("l3s", ("L3_xcond_qkv_w", 0, c["l3q"]), ("L3_xcond_qkv_w", D, c["l3k"]),
            ("L3_xcond_qkv_w", 2 * D, d["L3_xcond_qkv_b"][2 * D:3 * D]), False, hT, T)
        attention_phase(nc, m, T, False)
        output_phase(nc, m, d["L3_xcond_sa_proj_w"], d["L3_xcond_sa_proj_b"], 0)
        norm_phase(nc, m, hT, 1e-6, None, None)
        qkv("l3c", ("L3_xcond_q_w", 0, c["l3cq"]), ("L3_xcond_kv_w", 0, c["l3ck"]),
            ("L3_xcond_kv_w", D, d["L3_xcond_kv_b"][D:2 * D]), False, m.ctxT, NS2)
        attention_phase(nc, m, NS2, True)
        output_phase(nc, m, d["L3_xcond_ca_proj_w"], d["L3_xcond_ca_proj_b"], None, m.none_left)
        norm_phase(nc, m, hT, 1e-6, c["l3"] + 8, c["l3"] + 6)
        ffn_phase(nc, m, hT, d["L3_xcond_fc1_w"], c["l3b1"], d["L3_xcond_fc2_w"], d["L3_xcond_fc2_b"], 1, out)


def kernel(**inputs):
    import numpy as np
    import concourse.bacc as bacc
    from concourse.bass_utils import run_bass_kernel_spmd

    a = {n: np.ascontiguousarray(v) for n, v in inputs.items()}
    columns = lambda v: np.asarray(v).reshape(-1, P).T
    arrays = {
        "x": a["x"][0], "ctx": a["ctx_1024"][0], "cond": columns(a["cond_1024"]),
        "mask": np.pad(a["mask_BxS2_bf0"], ((0, 0), (0, -NS2 % 4))).view(np.int32),
        "ident": np.eye(P, dtype=np.float32),
        "l0_ln_wT": np.stack([a[f"L0_xcond_ln{i}_w"].T for i in (1, 2, 3)]),
        "l0_qkv_wT": a["L0_xcond_qkv_w"].T, "l0_sa_wT": a["L0_xcond_sa_out_w"].T,
        "l0_q_wT": a["L0_xcond_q_w"].T, "l0_k_wT": a["L0_xcond_k_w"].T, "l0_v_wT": a["L0_xcond_v_w"].T,
        "l0_ca_wT": a["L0_xcond_ca_out_w"].T, "l0_w1T": a["L0_xcond_ffn_w1"].T, "l0_w2T": a["L0_xcond_ffn_w2"].T,
        "e_w2T": a["L2_xcond_e_w2"].transpose(0, 2, 1),
        "e_b2_cols": columns(a["L2_xcond_e_b2"]),
        "bias_cols": np.concatenate([columns(a[n]) for n in (
            "L0_xcond_ln1_b", "L0_xcond_ln2_b", "L0_xcond_ln3_b", "L1_xcond_bss_q", "L1_xcond_bss_kv",
            "L3_xcond_ada_b", "L2_xcond_e_b1", "L2_xcond_gate_b1", "L2_xcond_ln_gamma", "L2_xcond_ln_beta",
            "L0_xcond_ffn_b1", "L3_xcond_fc1_b", "L1_xcond_bq")]
            + [columns(a["L1_xcond_bkv"][0:D])]
            + [columns(a["L3_xcond_qkv_b"][0:2 * D]), columns(a["L3_xcond_q_b"]), columns(a["L3_xcond_kv_b"][0:D])],
            axis=1),
    }
    half = DH // 2
    freq = (np.float32(1.0) / np.power(np.float32(10000.0), np.arange(half, dtype=np.float32) / np.float32(half))
            ).astype(np.float32)
    angle = np.arange(T, dtype=np.float32)[None, :] * freq[:, None]
    arrays["cos"] = np.tile(np.cos(angle), (P // half, 1)).astype(np.float32)
    arrays["sin"] = np.tile(np.concatenate([-np.sin(angle), np.sin(angle)]), (P // DH, 1)).astype(np.float32)
    swap = np.zeros((P, P), np.float32)
    swap[np.arange(P), np.arange(P) ^ half] = 1.0
    arrays["swap"] = swap
    for n in ("L1_xcond_Wss_q", "L1_xcond_Wss_kv", "L1_xcond_Wq", "L1_xcond_Wkv", "L1_xcond_bkv", "L1_xcond_Wp",
              "L1_xcond_bp", "L0_xcond_ffn_b2", "L2_xcond_Wq", "L2_xcond_Wk", "L2_xcond_Wv", "L2_xcond_router_W",
              "L2_xcond_router_b", "L2_xcond_e_w1", "L2_xcond_gate_w1", "L2_xcond_gate_w2", "L2_xcond_gate_b2",
              "L2_xcond_out_w", "L2_xcond_out_b", "L3_xcond_ada_w", "L3_xcond_ada_b", "L3_xcond_qkv_w",
              "L3_xcond_qkv_b", "L3_xcond_sa_proj_w", "L3_xcond_sa_proj_b", "L3_xcond_q_w", "L3_xcond_kv_w",
              "L3_xcond_kv_b", "L3_xcond_ca_proj_w", "L3_xcond_ca_proj_b", "L3_xcond_fc1_w", "L3_xcond_fc2_w",
              "L3_xcond_fc2_b"):
        arrays[n] = a[n]
    arrays = {"in_" + n: np.ascontiguousarray(v) for n, v in arrays.items()}
    nc = bacc.Bacc("TRN2", target_bir_lowering=False, num_devices=1)
    d = {n[3:]: nc.dram_tensor(n, v.shape, mybir.dt.from_np(v.dtype), kind="ExternalInput").ap()
         for n, v in arrays.items()}
    out = nc.dram_tensor("out_x", (T, D), F32, kind="ExternalOutput").ap()
    build(nc, d, out)
    r = run_bass_kernel_spmd(nc, [arrays], core_ids=[0])
    return r.results[0]["out_x"].reshape(1, T, D)
```

```python
from contextlib import ExitStack

import concourse.bass as bass
from concourse import mybir

F32 = mybir.dt.float32
BF16 = mybir.dt.bfloat16
U8 = mybir.dt.uint8
ALU = mybir.AluOpType
ACT = mybir.ActivationFunctionType
AX = mybir.AxisListType.X

P = 128
T = 2048
D = 256
NH = 16
DH = D // NH
NT = T // P
NS2 = 1601
NC2 = -(-NS2 // P)
CH = 512
NCH = T // CH
KD = D // P
FF = 1024
NE = 3
RH = 512
HG = 4
NG = NH // HG
PARTS = 3
Q_PART = (0, 1, 2, 0, 1, 0)
K_PART = (0, 0, 0, 1, 1, 2)
PAIR_ROWS = DH * len(Q_PART)
MASK_ROW = PAIR_ROWS
MAX_ROW = MASK_ROW + 1
KROWS = MAX_ROW + PARTS
CREDIT = 8
MASK_BIAS = -1.0e30


def tile_rows(n, i):
    return min(P, n - i * P)


class Signal:

    def __init__(self, sem):
        self.sem = sem
        self.start = CREDIT

    def at(self, n):
        return self.start + n

    def advance(self, n):
        self.start += n


class Machine:
    pass


def cols(ap, k):
    return ap[:, k:k + 1]


def setup_phase(nc, m, d):
    s_in, s_load, s_w, s_cond, s_bc, s_row, s_rowv, s_mod, s_gate, s_modv, s_cols = (m.sig[n] for n in (
        "cond_in", "load", "weights", "cond_ready", "cond_bc", "rows_ready", "rows_saved", "mod_ready",
        "gate_ready", "mod_saved", "cols_ready"))
    s_st, s_rs, s_n, s_tr, s_ev, s_ones, s_d = (m.sig[n] for n in (
        "stats", "rstd", "normed", "turned", "turn_saved", "ones", "dve"))
    s_mk, s_mkd, s_const, s_out = (m.sig[n] for n in ("mask_in", "mask_step", "const_set", "stored0"))
    with ExitStack() as ctx:
        sb = lambda n, s, t=F32: ctx.enter_context(nc.sbuf_tensor("su_" + n, s, t))
        lnw = sb("lnw", [P, 3, KD, 2 * D])
        l1w = sb("l1w", [P, 2, KD, 2 * D])
        adaw = sb("adaw", [P, KD, 6 * D])
        ew1c = sb("ew1c", [P, NE, KD, RH])
        gw1c = sb("gw1c", [P, KD, D])
        rwc = sb("rwc", [P, KD, NE])
        bias_cols = sb("bias_cols", [P, m.NCOL])
        gate_b = sb("gate_b", [P, 2, D])
        rb = sb("rb", [P, NE])
        cond = sb("cond", [P, KD])
        silu_cond = sb("silu_cond", [P, KD])
        cond_bc = sb("cond_bc", [P, 2, KD, P])
        ones = sb("ones", [P, P])
        rows = sb("rows", [P, 3, CH])
        ct = sb("ct", [P, NC2, D])
        cn = sb("cn", [P, NC2, D])
        st = sb("st", [P, NC2, 6])
        mv = sb("mv", [P, NC2, 2])
        var = sb("var", [P, NC2])
        std = sb("std", [P, NC2])
        rstd = sb("rstd", [P, NC2])
        raw = sb("raw", [P, -(-NS2 // 4)], mybir.dt.int32)
        as_f = sb("as_f", [P, NS2])
        mask_bias = sb("mask_bias", [1, NS2], BF16)
        const = sb("const", [1, 2, T], BF16)
        left = sb("left", [P, 1])
        inv = sb("inv", [P, 1])
        ps = ctx.enter_context(nc.psum_tensor("su_ps", [P, 8, CH], F32))
        L = m.L
        chunks = [(lnw[:, i], 0, CH) for i in range(3)] + [(l1w[:, i], 1, CH) for i in range(2)]
        chunks += [(adaw[:, :, i * CH:(i + 1) * CH], 1, CH) for i in range(3)]
        chunks += [(ew1c[:, e], 0, CH) for e in range(NE)] + [(gw1c, 0, D)]
        assert [m.col[n] for n in ("l0", "l1", "l3", "eb1", "gb1")] == [0, 12, 20, 32, 44]
        NCHUNK = len(chunks)
        NROW = -(-NCHUNK // 4)
        NJ = sum(w for _, _, w in chunks) // P
        plus_one = [m.col["l0"] + 4 * i for i in range(3)]
        plus_one += [m.col["l1"], m.col["l1"] + 4, m.col["l3"] + 2, m.col["l3"] + 8]
        NSTORE = 1 + KROWS - MASK_ROW
        loads = [(lnw[:, i], d["l0_ln_wT"][i].rearrange("(k p) n -> p k n", p=P)) for i in range(3)]
        loads += [(l1w[:, i], d[n].rearrange("(k p) n -> p k n", p=P))
                  for i, n in enumerate(("L1_xcond_Wss_q", "L1_xcond_Wss_kv"))]
        loads += [(adaw[:, :, :], d["L3_xcond_ada_w"].rearrange("(k p) n -> p k n", p=P))]
        loads += [(ew1c[:, e], d["L2_xcond_e_w1"][e, 2 * D:3 * D, :].rearrange("(k p) n -> p k n", p=P))
                  for e in range(NE)]
        loads += [(gw1c[:, :, :], d["L2_xcond_gate_w1"][2 * D:3 * D, :].rearrange("(k p) n -> p k n", p=P)),
                  (rwc[:, :, :], d["L2_xcond_router_W"][2 * D:3 * D, :].rearrange("(k p) n -> p k n", p=P)),
                  (bias_cols[:, :], d["bias_cols"]),
                  (rb[:, :], d["L2_xcond_router_b"].partition_broadcast(P))]
        loads += [(gate_b[:, i], d["L3_xcond_ada_b"][j * D:(j + 1) * D].partition_broadcast(P))
                  for i, j in enumerate((2, 5))]
        NLOAD = len(loads)

        block = ctx.enter_context(nc.Block())

        @block.sync
        def _(sp):
            sp.dma_start(raw[:, :], d["mask"].rearrange("a n -> (a n)").partition_broadcast(P)).then_inc(s_mk.sem, 16)
            for dst, src in loads:
                sp.dma_start(dst, src).then_inc(s_w.sem, 16)
            sp.wait_ge(s_const.sem, s_const.at(2))
            for r in range(KROWS - MASK_ROW):
                sp.dma_start(m.const_rows[r:r + 1, :], const[:, min(r, 1), :]).then_inc(s_out.sem, 16)
            sp.wait_ge(s_mkd.sem, s_mkd.at(2))
            sp.dma_start(m.mask_row[:, :], mask_bias[:, :]).then_inc(s_out.sem, 16)
            sp.wait_ge(s_out.sem, s_out.at(16 * NSTORE))

        @block.gpsimd
        def _(pool):
            nc.gpsimd.memset(ones[:, :], 1.0).then_inc(s_ones.sem, 1)
            nc.gpsimd.memset(const[:, 0, :], 0.0).then_inc(s_const.sem, 1)
            nc.gpsimd.memset(const[:, 1, :], 1.0).then_inc(s_const.sem, 1)

        @block.scalar
        def _(act):
            act.dma_start(cond[:, :], d["cond"]).then_inc(s_in.sem, 16)
            act.dma_start(m.ident[:, :], d["ident"]).then_inc(s_in.sem, 16)
            act.dma_start(ct[:, 0:NC2 - 1, :], d["ctx"][0:(NC2 - 1) * P, :].rearrange("(t p) n -> p t n", p=P)
                          ).then_inc(s_load.sem, 16)
            act.dma_start(ct[0:L, NC2 - 1, :], d["ctx"][(NC2 - 1) * P:NS2, :]).then_inc(s_load.sem, 16)
            act.dma_start(m.x[:, :, :], d["x"].rearrange("(t p) n -> p t n", p=P)).then_inc(m.sig["x_in"].sem, 16)
            act.wait_ge(s_in.sem, s_in.at(32))
            nc.scalar.activation(silu_cond[:, :], cond[:, :], ACT.Silu).then_inc(s_cond.sem, 1)
            act.wait_ge(s_st.sem, s_st.at(1))
            nc.scalar.activation(std[:, :], var[:, :], ACT.Sqrt).then_inc(s_rs.sem, 1)
            turn = 0
            for src in range(2):
                if src == 1:
                    act.wait_ge(s_row.sem, s_row.at(1))
                    nc.scalar.copy(rows[:, 0:NROW - 1, :], ps[:, 0:NROW - 1, :]).then_inc(s_rowv.sem, 1)
                    nc.scalar.copy(rows[:, NROW - 1, 0:D], ps[:, NROW - 1, 0:D]).then_inc(s_rowv.sem, 1)
                    nc.scalar.copy(rows[0:96, NROW - 1, D:CH], ps[0:96, NROW - 1, D:CH]).then_inc(s_rowv.sem, 1)
                    act.wait_ge(s_cols.sem, s_cols.at(1))
                for t4 in range(4):
                    for k in range(KD):
                        n = min(4 * P, NS2 - t4 * 4 * P)
                        act.wait_ge(s_tr.sem, s_tr.at(turn + 1))
                        dst = (m.ctxT, m.ctxnT)[src][:, k, t4 * CH:t4 * CH + n]
                        if src == 0:
                            nc.scalar.copy(dst, ps[:, 4 + turn % 4, 0:n]).then_inc(s_ev.sem, 1)
                        else:
                            c = m.col["l1"] + 4
                            nc.scalar.activation(dst, ps[:, 4 + turn % 4, 0:n], ACT.Identity,
                                                 scale=cols(m.mod, c + k), bias=cols(m.mod, c + 2 + k)
                                                 ).then_inc(s_ev.sem, 1)
                        turn += 1

        @block.vector
        def _(dve):
            dve.wait_ge(s_in.sem, s_in.at(32))
            dve.wait_ge(s_ones.sem, s_ones.at(1))
            dve.wait_ge(s_cond.sem, s_cond.at(1))
            for i, c in enumerate((cond, silu_cond)):
                for k in range(KD):
                    last = nc.vector.tensor_scalar(cond_bc[:, i, k, :], ones[:, :], cols(c, k), None, ALU.mult)
            last.then_inc(s_bc.sem, 1)
            dve.wait_ge(s_load.sem, s_load.at(32))
            for t in range(NC2):
                r = tile_rows(NS2, t)
                nc.vector.bn_stats(st[0:r, t, :], ct[0:r, t, :]).then_inc(s_d.sem, 1)
            nc.vector.memset(var[:, :], 1.0).then_inc(s_d.sem, 1)
            dve.wait_ge(s_d.sem, s_d.at(NC2 + 1))
            for t in range(NC2):
                r = tile_rows(NS2, t)
                nc.vector.bn_aggr(mv[0:r, t, :], st[0:r, t, :]).then_inc(s_d.sem, 1)
            dve.wait_ge(s_d.sem, s_d.at(2 * NC2 + 1))
            nc.vector.tensor_scalar(var[:, 0:NC2 - 1], mv[:, 0:NC2 - 1, 1], 1e-5, None, ALU.add)
            nc.vector.tensor_scalar(var[0:L, NC2 - 1:NC2], mv[0:L, NC2 - 1, 1:2], 1e-5, None, ALU.add
                                    ).then_inc(s_st.sem, 1)
            dve.wait_ge(s_rs.sem, s_rs.at(1))
            nc.vector.reciprocal(rstd[:, :], std[:, :]).then_inc(s_d.sem, 1)
            dve.wait_ge(s_d.sem, s_d.at(2 * NC2 + 2))
            for t in range(NC2):
                r = tile_rows(NS2, t)
                nc.vector.tensor_scalar(cn[0:r, t, :], ct[0:r, t, :], mv[0:r, t, 0:1], rstd[0:r, t:t + 1],
                                        ALU.subtract, ALU.mult).then_inc(s_n.sem, 1)
            dve.wait_ge(s_mk.sem, s_mk.at(16))
            nc.vector.tensor_copy(as_f[:, :], raw[:, :].bitcast(U8)[:, 0:NS2]).then_inc(s_mkd.sem, 1)
            dve.wait_ge(s_mkd.sem, s_mkd.at(1))
            nc.vector.tensor_scalar(mask_bias[:, :], as_f[0:1, :], MASK_BIAS, None, ALU.mult).then_inc(s_mkd.sem, 1)
            nc.vector.reduce_sum(left[:, :], as_f[:, :], AX).then_inc(s_mkd.sem, 1)
            dve.wait_ge(s_mkd.sem, s_mkd.at(3))
            nc.vector.tensor_scalar(left[:, :], left[:, :], -1.0, float(NS2), ALU.mult, ALU.add
                                    ).then_inc(s_mkd.sem, 1)
            dve.wait_ge(s_mkd.sem, s_mkd.at(4))
            nc.vector.reciprocal(inv[:, :], left[:, :]).then_inc(s_mkd.sem, 1)
            dve.wait_ge(s_mkd.sem, s_mkd.at(5))
            nc.vector.tensor_scalar(m.none_left[:, :], inv[:, :], 0.0, None, ALU.mult).then_inc(s_mkd.sem, 1)
            dve.wait_ge(m.sig["x_in"].sem, m.sig["x_in"].at(16))
            for t in range(NT):
                nc.vector.bn_stats(m.x_stats[:, t, :], m.x[:, t, :]).then_inc(m.sig["x_stats"].sem, 1)
            dve.wait_ge(m.sig["x_stats"].sem, m.sig["x_stats"].at(NT))
            for t in range(NT):
                nc.vector.bn_aggr(m.x_mean_var[:, t, :], m.x_stats[:, t, :])
            dve.wait_ge(s_w.sem, s_w.at(16 * NLOAD))
            dve.wait_ge(s_mod.sem, s_mod.at(1))
            for b in range(NROW):
                columns = ps[:, b, :].rearrange("p (q j r) -> p j q r", q=4, j=4)
                for j in range(4):
                    c = 16 * b + 4 * j
                    w = min(4, NJ - c)
                    last = nc.vector.tensor_tensor(m.mod[:, c:c + w], columns[:, j, 0:w, 0],
                                                   bias_cols[:, c:c + w], ALU.add)
            last.then_inc(s_d.sem, 1)
            nc.vector.tensor_copy(m.mod[:, NJ:m.NCOL], bias_cols[:, NJ:m.NCOL]).then_inc(s_d.sem, 1)
            dve.wait_ge(s_d.sem, s_d.at(2 * NC2 + 4))
            for c in plus_one:
                last = nc.vector.tensor_scalar(m.mod[:, c:c + 2], m.mod[:, c:c + 2], 1.0, None, ALU.add)
            last.then_inc(s_cols.sem, 1)
            dve.wait_ge(s_gate.sem, s_gate.at(1))
            nc.vector.tensor_tensor(m.gates[:, :, :], ps[:, 3, :].rearrange("p (a b) -> p a b", a=2),
                                    gate_b[:, :, :], ALU.add)
            dve.wait_ge(s_gate.sem, s_gate.at(2))
            nc.vector.tensor_tensor(m.router_bias[:, :], ps[:, 4, 0:NE], rb[:, :], ALU.add).then_inc(s_modv.sem, 1)

        @block.tensor
        def _(pe):
            pe.wait_ge(s_in.sem, s_in.at(32))
            pe.wait_ge(s_load.sem, s_load.at(32))
            turn = 0
            def turn_tiles(src, ready):
                nonlocal turn
                for t4 in range(4):
                    for k in range(KD):
                        if turn >= 4:
                            pe.wait_ge(s_ev.sem, s_ev.at(turn - 3))
                        tiles = range(4 * t4, min(4 * t4 + 4, NC2))
                        if ready:
                            pe.wait_ge(s_n.sem, s_n.at(tiles[-1] + 1))
                        for t in tiles:
                            r = tile_rows(NS2, t)
                            last = pe.transpose(ps[:, 4 + turn % 4, (t % 4) * P:(t % 4) * P + r],
                                                src[0:r, t, k * P:(k + 1) * P], m.ident[0:r, 0:r])
                        last.then_inc(s_tr.sem, 1)
                        turn += 1
            turn_tiles(ct, False)
            pe.wait_ge(s_bc.sem, s_bc.at(1))
            pe.wait_ge(s_w.sem, s_w.at(16 * NLOAD))
            for b in range(NROW):
                for k in range(KD):
                    for j in range(4):
                        w, which, n = chunks[4 * b + j]
                        last = pe.matmul(ps[32 * j:32 * j + 32, b, 0:n], cond_bc[:, which, k, 0:32], w[:, k, 0:n],
                                         start=(k == 0), stop=(k == KD - 1))
            last.then_inc(s_row.sem, 1)
            for i in range(2):
                j = (2, 5)[i]
                for k in range(KD):
                    last = pe.matmul(ps[:, 3, i * D:(i + 1) * D], cond_bc[:, 1, k, :],
                                     adaw[:, k, j * D:(j + 1) * D], start=(k == 0), stop=(k == KD - 1))
            last.then_inc(s_gate.sem, 1)
            pe.wait_ge(s_rowv.sem, s_rowv.at(3))
            for b in range(NROW):
                for q in range(4):
                    r = P if 16 * b + 4 * 3 + q < NJ else 96
                    last = pe.transpose(ps[:, b, q * P:q * P + r], rows[0:r, b, q * P:(q + 1) * P],
                                        m.ident[0:r, 0:r])
            last.then_inc(s_mod.sem, 1)
            turn_tiles(cn, True)
            pe.wait_ge(s_ev.sem, s_ev.at(turn - 3))
            for k in range(KD):
                last = pe.matmul(ps[:, 4, 0:NE], cond_bc[:, 0, k, :], rwc[:, k, :],
                                 start=(k == 0), stop=(k == KD - 1))
            last.then_inc(s_gate.sem, 1)

    for s, k in ((s_in, 32), (s_load, 32), (m.sig["x_in"], 16), (m.sig["x_stats"], NT), (s_w, 16 * NLOAD), (s_cond, 1), (s_bc, 1), (s_row, 1),
                 (s_rowv, 3), (s_mod, 1), (s_gate, 2), (s_modv, 1), (s_cols, 1), (s_st, 1), (s_rs, 1), (s_n, NC2),
                 (s_tr, 16), (s_ev, 16), (s_ones, 1), (s_d, 2 * NC2 + 4), (s_mk, 16), (s_mkd, 6), (s_const, 2),
                 (s_out, 16 * NSTORE)):
        s.advance(k)


def row_statistics(nc, m, dve, final, t):
    s_xs = m.sig["x_stats"]
    if t < NT:
        dve.wait_ge(final.sem, final.at(t + 1))
        nc.vector.bn_stats(m.x_stats[:, t, :], m.x[:, t, :]).then_inc(s_xs.sem, 1)
    if t >= 1:
        dve.wait_ge(s_xs.sem, s_xs.at(t))
        nc.vector.bn_aggr(m.x_mean_var[:, t - 1, :], m.x_stats[:, t - 1, :])


def norm_phase(nc, m, hT, eps, scale, shift):
    s_st, s_rs, s_rec, s_n, s_np, s_tr = (m.sig[n] for n in ("stats", "rstd", "recip", "normed", "normed_pool", "turned"))
    PER = CH // P
    with ExitStack() as ctx:
        m.uid += 1
        sb = lambda n, s, t=F32: ctx.enter_context(nc.sbuf_tensor(f"nm{m.uid}_" + n, s, t))
        var = sb("var", [P, NT])
        std = sb("std", [P, NT])
        rstd = sb("rstd", [P, NT])
        xn = sb("xn", [P, NT, D])
        ps = ctx.enter_context(nc.psum_tensor(f"nm{m.uid}_ps", [P, NCH * KD, CH], F32))
        block = ctx.enter_context(nc.Block())

        @block.vector
        def _(dve):
            nc.vector.tensor_scalar(var[:, :], m.x_mean_var[:, :, 1], eps, None, ALU.add).then_inc(s_st.sem, 1)
            dve.wait_ge(s_rs.sem, s_rs.at(1))
            nc.vector.reciprocal(rstd[:, :], std[:, :]).then_inc(s_rec.sem, 1)
            dve.wait_ge(s_rec.sem, s_rec.at(1))
            for t in range(NT):
                if t % PER < PER - 1:
                    nc.vector.tensor_scalar(xn[:, t, :], m.x[:, t, :], m.x_mean_var[:, t, 0:1], rstd[:, t:t + 1],
                                            ALU.subtract, ALU.mult).then_inc(s_n.sem, 1)
            for c in range(NCH):
                dve.wait_ge(s_tr.sem, s_tr.at(c * KD + 2))
                src, dst = ps[:, c * KD + 1, :], hT[:, 1, c * CH:(c + 1) * CH]
                if scale is None:
                    nc.vector.tensor_copy(dst, src)
                else:
                    nc.vector.tensor_scalar(dst, src, cols(m.mod, scale + 1), cols(m.mod, shift + 1),
                                            ALU.mult, ALU.add)

        @block.gpsimd
        def _(pool):
            pool.wait_ge(s_rec.sem, s_rec.at(1))
            for t in range(PER - 1, NT, PER):
                nc.gpsimd.tensor_scalar(xn[:, t, :], m.x[:, t, :], m.x_mean_var[:, t, 0:1], rstd[:, t:t + 1],
                                        ALU.subtract, ALU.mult).then_inc(s_np.sem, 1)

        @block.scalar
        def _(act):
            act.wait_ge(s_st.sem, s_st.at(1))
            nc.scalar.activation(std[:, :], var[:, :], ACT.Sqrt).then_inc(s_rs.sem, 1)
            for c in range(NCH):
                act.wait_ge(s_tr.sem, s_tr.at(c * KD + 1))
                src, dst = ps[:, c * KD, :], hT[:, 0, c * CH:(c + 1) * CH]
                if scale is None:
                    nc.scalar.copy(dst, src)
                else:
                    nc.scalar.activation(dst, src, ACT.Identity, scale=cols(m.mod, scale), bias=cols(m.mod, shift))

        @block.tensor
        def _(pe):
            for c in range(NCH):
                pe.wait_ge(s_n.sem, s_n.at((PER - 1) * (c + 1)))
                pe.wait_ge(s_np.sem, s_np.at(c + 1))
                for k in range(KD):
                    for t in range(PER):
                        last = pe.transpose(ps[:, c * KD + k, t * P:(t + 1) * P],
                                            xn[:, PER * c + t, k * P:(k + 1) * P], m.ident[:, :])
                    last.then_inc(s_tr.sem, 1)

    for s, k in ((s_st, 1), (s_rs, 1), (s_rec, 1), (s_n, NCH * (PER - 1)), (s_np, NCH), (s_tr, NCH * KD)):
        s.advance(k)


def projection_phase(nc, m, loads, feature_jobs, token_jobs, rope):
    s_w, s_pr, s_tk, s_rot, s_rv, s_f2, s_p1, s_r, s_p2, s_sp, s_d = (
        m.sig[n] for n in ("weights", "proj_ready", "proj_taken", "rot_ready", "rot_taken",
                           "feat_final", "part1", "rest", "part2", "parts_ready", "dve"))
    s_slot = [m.sig[f"stored{i}"] for i in range(4)]
    NF, NJ = len(feature_jobs), len(feature_jobs) + len(token_jobs)
    R = 4
    with ExitStack() as ctx:
        m.uid += 1
        sb = lambda n, s, t=F32: ctx.enter_context(nc.sbuf_tensor(f"pj{m.uid}_" + n, s, t))
        feat = sb("feat", [P, R, CH])
        turned = sb("turned", [P, R, CH])
        final = sb("final", [P, R, CH]) if rope else feat
        rest = sb("rest", [P, R, CH])
        parts = sb("parts", [P, R, PARTS, CH], BF16)
        ps = ctx.enter_context(nc.psum_tensor(f"pj{m.uid}_ps", [P, 4, CH], F32))
        pr = ctx.enter_context(nc.psum_tensor(f"pj{m.uid}_pr", [P, 2, CH], F32))
        block = ctx.enter_context(nc.Block())
        split = [f for f in range(NF) if feature_jobs[f][4] is not None]
        assert not split or split == list(range(NF))
        stored = len(split) > 0

        @block.sync
        def _(sp):
            for dst, src in loads:
                sp.dma_start(dst, src).then_inc(s_w.sem, 16)
            for f in split:
                n = feature_jobs[f][2]
                sp.wait_ge(s_sp.sem, s_sp.at(f + 1))
                sp.dma_start(feature_jobs[f][4], parts[:, f % R, :, 0:n]).then_inc(s_slot[f % R].sem, 16)
            for r in range(min(R, len(split))):
                sp.wait_ge(s_slot[r].sem, s_slot[r].at(16 * len(range(r, len(split), R))))

        @block.tensor
        def _(pe):
            pe.wait_ge(s_w.sem, s_w.at(16 * len(loads)))

            def rotate(f):
                n = feature_jobs[f][2]
                pe.wait_ge(s_tk.sem, s_tk.at(f + 1))
                pe.wait_ge(s_rv.sem, s_rv.at(f - 1))
                pe.matmul(pr[:, f % 2, 0:n], m.swap[:, :], feat[:, f % R, 0:n], start=True, stop=True
                          ).then_inc(s_rot.sem, 1)

            for i in range(NJ):
                pe.wait_ge(s_tk.sem, s_tk.at(i - 3))
                if i < NF:
                    w, x, n = feature_jobs[i][:3]
                    for k in range(KD):
                        last = pe.matmul(ps[:, i % 4, 0:n], w[k], x[k], start=(k == 0), stop=(k == KD - 1))
                else:
                    x, r, w = token_jobs[i - NF][:3]
                    for k in range(KD):
                        last = pe.matmul(ps[0:r, i % 4, 0:D], x[k], w[k], start=(k == 0), stop=(k == KD - 1))
                last.then_inc(s_pr.sem, 1)
                if rope and 1 <= i:
                    rotate(i - 1)
            if rope:
                rotate(NF - 1)

        whole = s_f2 if rope else s_tk

        def take_feature(engine, f):
            n, bias, _, kept = feature_jobs[f][2:6]
            dst = feat[:, f % R, 0:n] if kept is None else kept
            engine.wait_ge(s_pr.sem, s_pr.at(f + 1))
            if f >= R:
                if rope:
                    engine.wait_ge(s_rot.sem, s_rot.at(f - R + 1))
                    engine.wait_ge(s_d.sem, s_d.at(f - R + 1))
                elif stored:
                    engine.wait_ge(s_p1.sem, s_p1.at(f - R + 1))
                    engine.wait_ge(s_r.sem, s_r.at(f - R + 1))
            if rope:
                op = nc.scalar.copy(dst, ps[:, f % 4, 0:n])
            elif bias is None:
                op = nc.vector.tensor_copy(dst, ps[:, f % 4, 0:n])
            else:
                op = nc.vector.tensor_scalar(dst, ps[:, f % 4, 0:n], cols(m.mod, bias), None, ALU.add)
            op.then_inc(s_tk.sem, 1)

        @block.vector
        def _(dve):
            dve.wait_ge(s_w.sem, s_w.at(16 * len(loads)))

            def times_cos(f):
                n, c0 = feature_jobs[f][2], feature_jobs[f][6]
                dve.wait_ge(s_tk.sem, s_tk.at(f + 1))
                if f >= R:
                    dve.wait_ge(s_p1.sem, s_p1.at(f - R + 1))
                    dve.wait_ge(s_r.sem, s_r.at(f - R + 1))
                nc.vector.tensor_tensor(final[:, f % R, 0:n], feat[:, f % R, 0:n], m.cos[:, c0:c0 + n], ALU.mult
                                        ).then_inc(s_d.sem, 1)

            def rotated(f):
                n, c0 = feature_jobs[f][2], feature_jobs[f][6]
                dve.wait_ge(s_rot.sem, s_rot.at(f + 1))
                nc.vector.tensor_tensor(turned[:, f % R, 0:n], pr[:, f % 2, 0:n], m.sin[:, c0:c0 + n], ALU.mult
                                        ).then_inc(s_rv.sem, 1)
                dve.wait_ge(s_rv.sem, s_rv.at(f + 1))
                dve.wait_ge(s_d.sem, s_d.at(f + 1))
                nc.vector.tensor_tensor(final[:, f % R, 0:n], final[:, f % R, 0:n], turned[:, f % R, 0:n], ALU.add
                                        ).then_inc(s_f2.sem, 1)

            def leave_rest(f):
                n = feature_jobs[f][2]
                dve.wait_ge(s_p1.sem, s_p1.at(f + 1))
                if f >= R:
                    dve.wait_ge(s_sp.sem, s_sp.at(f - R + 1))
                nc.vector.tensor_tensor(rest[:, f % R, 0:n], final[:, f % R, 0:n], parts[:, f % R, 0, 0:n],
                                        ALU.subtract).then_inc(s_r.sem, 1)

            lag = 3 if rope else 1
            for i in range(NF + lag):
                if i < NF:
                    if rope:
                        times_cos(i)
                    else:
                        take_feature(dve, i)
                if rope and 1 <= i <= NF:
                    rotated(i - 1)
                if stored and i >= lag:
                    leave_rest(i - lag)
            for i in range(NF, NJ):
                _, r, _, bias, dst = token_jobs[i - NF]
                dve.wait_ge(s_pr.sem, s_pr.at(i + 1))
                if bias is None:
                    op = nc.vector.tensor_copy(dst, ps[0:r, i % 4, 0:D])
                else:
                    op = nc.vector.tensor_tensor(dst, ps[0:r, i % 4, 0:D], bias[0:r, :], ALU.add)
                op.then_inc(s_tk.sem, 1)

        @block.scalar
        def _(act):
            def first_part(f):
                n = feature_jobs[f][2]
                act.wait_ge(whole.sem, whole.at(f + 1))
                if f >= R:
                    act.wait_ge(s_slot[f % R].sem, s_slot[f % R].at(16 * (f // R)))
                nc.scalar.copy(parts[:, f % R, 0, 0:n], final[:, f % R, 0:n]).then_inc(s_p1.sem, 1)

            def second_part(f):
                n = feature_jobs[f][2]
                act.wait_ge(s_r.sem, s_r.at(f + 1))
                nc.scalar.copy(parts[:, f % R, 1, 0:n], rest[:, f % R, 0:n]).then_inc(s_p2.sem, 1)

            lag = (2, 4) if rope else (0, 1)
            for i in range(NF + lag[1]):
                if rope and i < NF:
                    take_feature(act, i)
                if stored and 0 <= i - lag[0] < NF:
                    first_part(i - lag[0])
                if stored and 0 <= i - lag[1]:
                    second_part(i - lag[1])

        @block.gpsimd
        def _(pool):
            for f in split:
                n = feature_jobs[f][2]
                pool.wait_ge(s_p2.sem, s_p2.at(f + 1))
                nc.gpsimd.tensor_tensor(parts[:, f % R, 2, 0:n], rest[:, f % R, 0:n], parts[:, f % R, 1, 0:n],
                                        ALU.subtract).then_inc(s_sp.sem, 1)

    s_w.advance(16 * len(loads))
    for s in (s_pr, s_tk):
        s.advance(NJ)
    if rope:
        for s in (s_rot, s_rv, s_f2, s_d):
            s.advance(NF)
    if stored:
        for s in (s_p1, s_r, s_p2, s_sp):
            s.advance(NF)
        for r in range(R):
            s_slot[r].advance(16 * len(range(r, NF, R)))


def piece_width(nk):
    return -(-nk // -(-nk // CH))


def max_pieces(nk, items, bank, turn_after):
    out = []
    width = piece_width(nk)
    for it in items:
        for key in range(0, nk, width):
            out.append(((it, key, min(width, nk - key)), bank))
            bank = (bank + 1) % 3
            if len(out) == turn_after:
                out.append(("turn", bank))
                bank = (bank + 1) % 3
    return out, bank


def attention_phase(nc, m, nk, masked, values):
    v_src, v_weight, v_bias = values
    s_kq = [m.sig["kq0"], m.sig["kq1"]]
    s_st, s_p, s_av, s_acc, s_mx, s_mt, s_nm, s_m1, s_mr, s_m2, s_ones, s_ms, s_mo, s_mi, s_v, s_init = (
        m.sig[n] for n in ("scores_ready", "probs_ready", "av_done", "acc_saved", "max_ready", "max_taken",
                           "maxes_ready", "m_part1", "m_rest", "m_part2", "ones_set", "m_parts",
                           "m_out", "m_in", "v_staged", "rows_ready"))
    s_w, s_pr, s_tk, s_vb = (m.sig[n] for n in ("weights", "proj_ready", "proj_taken", "v_biased"))
    NVW = 1 + (v_bias is not None)
    KT = -(-nk // P)
    items = HG * (CH // P)
    NP = -(-nk // CH)
    LEAD = 4
    this = [(0, q) for q in range(LEAD, items)]
    ahead = [(1, q) for q in range(LEAD)]
    TURN_AT = len(this) * NP + 3
    full, end = max_pieces(nk, this + ahead, 0, TURN_AT)
    skip = -end % 3
    first_items = [(0, q) for q in range(items)] + ahead
    first, end = max_pieces(nk, first_items, -(len(first_items) * NP + 1 + skip) % 3, items * NP + 3)
    assert (end + skip) % 3 == 0 and [x[1:] for x in first[-6:]] == [x[1:] for x in full[-6:]]
    short, _ = max_pieces(nk, this, 0, len(this) * NP)

    def with_needs(stream):
        last = {b: q + 1 - len(full) for q, (_, b) in enumerate(full)}
        out = []
        for q, (piece, b) in enumerate(stream):
            out.append((piece, b, last[b]))
            last[b] = q + 1
        return out

    NFIRST, NFULL, NSHORT = len(first), len(full), len(short)
    streams = {"first": [x[:2] + (max(x[2], 0),) for x in with_needs(first)], "full": with_needs(full),
               "short": with_needs(short), "none": []}
    UB = 2 * NCH
    NU = NG * NCH
    NB = NU // UB
    assert NB == 2
    NCONST = 3
    SLOTS, HELD = 4, 2
    KQ = 16 * 2 * len(Q_PART)

    with ExitStack() as ctx:
        m.uid += 1
        sb = lambda n, s, t=F32: ctx.enter_context(nc.sbuf_tensor(f"at{m.uid}_" + n, s, t))
        kst = sb("kst", [P, 2, HG, T], BF16)
        qst = sb("qst", [P, 2, HG, T], BF16)
        probs = sb("probs", [P, 2, HG, CH])
        vst = sb("vst", [P, 2, NT, HG, 2 * DH])
        mpart = sb("mpart", [P, 2, items, NP])
        mmax = sb("mmax", [P, 2, items])
        neg = sb("neg", [items, P])
        mrest = sb("mrest", [items, P])
        zero = sb("zero", [items, P])
        vw = sb("vw", [P, KD, D])
        vb = sb("vb", [P, D]) if v_bias is not None else None
        mparts = sb("mparts", [items, PARTS, P], BF16)
        scores = ctx.enter_context(nc.psum_tensor(f"at{m.uid}_scores", [P, 4, CH], F32))
        acc = ctx.enter_context(nc.psum_tensor(f"at{m.uid}_acc", [P, CH], F32))
        mxp = ctx.enter_context(nc.psum_tensor(f"at{m.uid}_mxp", [P, 3, CH], F32))
        block = ctx.enter_context(nc.Block())

        def taken_before(U):
            return NFIRST + U * NFULL

        @block.sync
        def _(sp):
            def load_group(par, g, h0=0, h1=HG, signal=None):
                for c in range(len(Q_PART)):
                    rows = slice(DH * c, DH * (c + 1))
                    heads = slice((g * HG + h0) * DH, (g * HG + h1) * DH)
                    for dst, src in ((qst[rows, par, h0:h1, :], m.q_parts[Q_PART[c], heads, :]),
                                     (kst[rows, par, h0:h1, 0:nk], m.k_parts[K_PART[c], heads, 0:nk])):
                        sp.dma_start(dst, src.rearrange("(h d) t -> d h t", d=DH)
                                     ).then_inc((signal or s_kq[par]).sem, 16)

            def spread_max(par, c, n):
                sp.wait_ge(s_ms.sem, s_ms.at(n + 1))
                sp.dma_start(m.m_scratch.rearrange("a i q -> i a q"), mparts[:, :, :]).then_inc(s_mo.sem, 16)
                sp.wait_ge(s_mo.sem, s_mo.at(16 * (n + 1)))
                sp.dma_start(qst[MAX_ROW:MAX_ROW + PARTS, par, :, c * CH:(c + 1) * CH],
                             m.m_scratch.rearrange("a (h i) q -> a h (i q)", h=HG)).then_inc(s_mi.sem, 16)

            load_group(0, 0, 0, 1, m.sig["head0"])
            load_group(0, 0, 1, HG)
            spread_max(0, 0, 0)
            with sp.Fori(0, NB) as i:
                for u in range(UB):
                    U = i * UB + u
                    if u == 0:
                        with sp.If(i < NB - 1):
                            load_group(1, 1)
                        with sp.Else():
                            sp.wait_ge(s_st.sem, s_st.at(U * 2 * KT))
                            load_group(1, 3)
                    if u == NCH:
                        with sp.If(i < NB - 1):
                            sp.wait_ge(s_st.sem, s_st.at(U * 2 * KT))
                            load_group(0, 2)
                    nxt = (u + 1) % UB
                    if u < UB - 1:
                        spread_max(nxt // NCH, nxt % NCH, U + 1)
                    else:
                        with sp.If(i < NB - 1):
                            spread_max(0, 0, U + 1)
            sp.wait_ge(s_mi.sem, s_mi.at(16 * NU))

        @block.tensor
        def _(pe):
            def take_pieces(stream, lo, hi, before, unit_of, turned):
                for piece, b, need in streams[stream][lo:hi]:
                    pe.wait_ge(s_mt.sem, s_mt.at(before + need))
                    if piece == "turn":
                        pe.wait_ge(s_nm.sem, s_nm.at(turned[1]))
                        last = pe.transpose(mxp[0:items, b, 0:P], mmax[:, turned[0], :], m.ident[:, :])
                    else:
                        (which, q), key, n = piece
                        par, c = unit_of[which]
                        h, qt = divmod(q, CH // P)
                        last = pe.matmul(mxp[:, b, 0:n],
                                         qst[0:MAX_ROW, par, h, c * CH + qt * P:c * CH + (qt + 1) * P],
                                         kst[0:MAX_ROW, par, h, key:key + n], start=True, stop=True)
                    last.then_inc(s_mx.sem, 1)

            def unit(i, u, stream):
                U = i * UB + u
                par, c = divmod(u, NCH)
                total = len(streams[stream])
                unit_of = [divmod((u + x) % UB, NCH) for x in (1, 2)]
                done = [0]

                def some(upto):
                    if done[0] <= AHEAD_AT < upto and (u + 2) % NCH == 0 and stream == "full":
                        tpar = unit_of[1][0]
                        take_pieces(stream, done[0], AHEAD_AT, taken_before(U), unit_of, ((u + 1) % 2, U + 2))
                        done[0] = AHEAD_AT
                        pe.wait_ge(s_kq[tpar].sem, s_kq[tpar].at(KQ * (i + 1) + (KQ if tpar == 0 else 0)))
                    take_pieces(stream, done[0], upto, taken_before(U), unit_of, ((u + 1) % 2, U + 2))
                    done[0] = upto

                def weigh(s):
                    pe.wait_ge(s_p.sem, s_p.at((U * KT + s) * 2 + 2))
                    if s == 0:
                        pe.wait_ge(s_acc.sem, s_acc.at(U))
                    r = tile_rows(nk, s)
                    for j in range(HG):
                        last = pe.matmul(acc[32 * j:32 * j + 2 * DH, :], vst[0:r, par, s, j, :],
                                         probs[0:r, s % 2, j, :], start=(s == 0), stop=(s == KT - 1))
                    last.then_inc(s_av.sem, 1)

                pe.wait_ge(s_mi.sem, s_mi.at(16 * (U + 1)))
                if u % NCH == 0:
                    pe.wait_ge(s_v.sem, s_v.at(1 + i * 2 + u // NCH))
                held = HELD if total > HELD else 0
                slots, at = SLOTS * KT, 0
                for s in range(KT):
                    r = tile_rows(nk, s)
                    for j in range(HG):
                        if j % 2 == 0:
                            pe.wait_ge(s_p.sem, s_p.at((U * KT + s) * 2 + j // 2 - 1))
                        last = pe.matmul(scores[0:r, j, :], kst[0:KROWS, par, j, s * P:s * P + r],
                                         qst[0:KROWS, par, j, c * CH:(c + 1) * CH], start=True, stop=True)
                        if j % 2:
                            last.then_inc(s_st.sem, 1)
                        if SLOTS == 4 or j % 2:
                            at += 1
                            some((total - held) * at // slots)
                    if s:
                        weigh(s - 1)
                some(total)
                weigh(KT - 1)

            AHEAD_AT = [n for n, (pc, _) in enumerate(full) if pc != "turn" and pc[0][0] == 1][0]
            def project_v(t):
                pe.wait_ge(s_tk.sem, s_tk.at(t - 3))
                r = tile_rows(nk, t)
                for k in range(KD):
                    last = pe.matmul(scores[0:r, t % 4, 0:D], v_src[:, k, t * P:t * P + r], vw[:, k, :],
                                     start=(k == 0), stop=(k == KD - 1))
                last.then_inc(s_pr.sem, 1)

            EARLY = 2
            pe.wait_ge(s_w.sem, s_w.at(16 * NVW))
            for t in range(EARLY):
                project_v(t)
            pe.wait_ge(s_init.sem, s_init.at(16 * NCONST))
            pe.wait_ge(m.sig["head0"].sem, m.sig["head0"].at(KQ))
            t = EARLY
            for q in range(NFIRST):
                if q == items // HG * NP:
                    pe.wait_ge(s_kq[0].sem, s_kq[0].at(KQ))
                take_pieces("first", q, q + 1, 0, [(0, 0), (0, 1)], (0, 1))
                if q % 3 == 2 and t < KT:
                    project_v(t)
                    t += 1
            assert t == KT
            pe.wait_ge(s_tk.sem, s_tk.at(KT))
            with pe.Fori(0, NB) as i:
                for u in range(UB - 2):
                    unit(i, u, "full")
                with pe.If(i < NB - 1):
                    unit(i, UB - 2, "full")
                    unit(i, UB - 1, "full")
                with pe.Else():
                    unit(i, UB - 2, "short")
                    unit(i, UB - 1, "none")

        @block.scalar
        def _(act):
            act.dma_start(vw[:, :, :], v_weight).then_inc(s_w.sem, 16)
            if v_bias is not None:
                act.dma_start(vb[:, :], v_bias.partition_broadcast(P)).then_inc(s_w.sem, 16)
            mask = m.mask_row if masked else m.const_rows
            for dst, src in ((kst[MASK_ROW:MAX_ROW, :, :, 0:nk], mask[0:1, 0:nk]),
                             (qst[MASK_ROW:MAX_ROW, :, :, :], m.const_rows[1:2, :]),
                             (kst[MAX_ROW:KROWS, :, :, 0:nk], m.const_rows[1:KROWS - MASK_ROW, 0:nk])):
                rows, n = src.shape
                act.dma_start(dst.rearrange("p a h t -> p (a h) t"),
                              src.unsqueeze(1).broadcast_to([rows, 2 * HG, n])).then_inc(s_init.sem, 16)
            for t in range(KT):
                r = tile_rows(nk, t)
                act.wait_ge(s_pr.sem, s_pr.at(t + 1))
                nc.scalar.copy(m.v[0:r, t, :], scores[0:r, t % 4, 0:D]).then_inc(s_tk.sem, 1)
            with act.Fori(0, NB) as i:
                for u in range(UB):
                    U = i * UB + u
                    g, c = divmod(u, NCH)
                    for s in range(KT):
                        r = tile_rows(nk, s)
                        act.wait_ge(s_av.sem, s_av.at(U * KT + s - 1))
                        for half in range(2):
                            act.wait_ge(s_st.sem, s_st.at((U * KT + s) * 2 + half + 1))
                            nc.scalar.activation(probs[0:r, s % 2, 2 * half:2 * half + 2, :],
                                                 scores[0:r, 2 * half:2 * half + 2, :], ACT.Exp,
                                                 scale=1.0 / DH ** 0.5).then_inc(s_p.sem, 1)
                    act.wait_ge(s_av.sem, s_av.at((U + 1) * KT))
                    nc.scalar.copy(m.attn[:, bass.ds((i * 2 + g) * T + c * CH, CH)], acc[:, :]
                                   ).then_inc(s_acc.sem, 1)

        @block.vector
        def _(dve):
            def take(stream, before, next_unit, slot):
                for q, (piece, b, _) in enumerate(streams[stream]):
                    if piece == "turn":
                        dve.wait_ge(s_m1.sem, s_m1.at(next_unit))
                        dve.wait_ge(s_mr.sem, s_mr.at(next_unit))
                        dve.wait_ge(s_mx.sem, s_mx.at(before + q + 1))
                        nc.vector.tensor_scalar(neg[:, :], mxp[0:items, b, 0:P], -1.0, None, ALU.mult
                                                ).then_inc(s_mt.sem, 1)
                        continue
                    (which, item), key, n = piece
                    if item == 0 and key == 0 and which == 1:
                        dve.wait_ge(s_nm.sem, s_nm.at(next_unit))
                    dve.wait_ge(s_mx.sem, s_mx.at(before + q + 1))
                    part = key // piece_width(nk)
                    nc.vector.reduce_max(mpart[:, (slot + which) % 2, item, part:part + 1], mxp[:, b, 0:n], AX
                                         ).then_inc(s_mt.sem, 1)
                    if which == 0 and item == items - 1 and key + n == nk:
                        dve.wait_ge(s_mt.sem, s_mt.at(before + q + 1))
                        nc.vector.reduce_max(mmax[:, slot, :], mpart[:, slot, :, :], AX).then_inc(s_nm.sem, 1)

            take("first", 0, 0, 0)
            with dve.Fori(0, NB) as i:
                for u in range(UB - 2):
                    take("full", taken_before(i * UB + u), i * UB + u + 1, (u + 1) % 2)
                with dve.If(i < NB - 1):
                    for u in (UB - 2, UB - 1):
                        take("full", taken_before(i * UB + u), i * UB + u + 1, (u + 1) % 2)
                with dve.Else():
                    take("short", taken_before(i * UB + UB - 2), i * UB + UB - 1, 1)

        @block.gpsimd
        def _(pool):
            def stage_v(par, g):
                whole = nk // P
                for kt in range(0, whole, 4):
                    e = min(kt + 4, whole)
                    last = nc.gpsimd.tensor_copy(vst[:, par, kt:e, :, 0:DH],
                                                 m.v[:, kt:e, bass.ds(g * HG * DH, HG * DH)].rearrange(
                                                     "p t (h e) -> p t h e", e=DH))
                if nk % P:
                    r = nk % P
                    last = nc.gpsimd.tensor_copy(vst[0:r, par, whole, :, 0:DH],
                                                 m.v[0:r, whole, bass.ds(g * HG * DH, HG * DH)].rearrange(
                                                     "p (h e) -> p h e", e=DH))
                last.then_inc(s_v.sem, 1)

            def cut_max(turn_at, n):
                pool.wait_ge(s_mt.sem, s_mt.at(turn_at))
                pool.wait_ge(s_mo.sem, s_mo.at(16 * n))
                pool.wait_ge(s_mi.sem, s_mi.at(16 * n))
                nc.gpsimd.tensor_tensor(mparts[:, 0, :], neg[:, :], zero[:, :], ALU.add).then_inc(s_m1.sem, 1)
                pool.wait_ge(s_m1.sem, s_m1.at(n + 1))
                nc.gpsimd.tensor_tensor(mrest[:, :], neg[:, :], mparts[:, 0, :], ALU.subtract).then_inc(s_mr.sem, 1)
                pool.wait_ge(s_mr.sem, s_mr.at(n + 1))
                nc.gpsimd.tensor_tensor(mparts[:, 1, :], mrest[:, :], zero[:, :], ALU.add).then_inc(s_m2.sem, 1)
                pool.wait_ge(s_m2.sem, s_m2.at(n + 1))
                nc.gpsimd.tensor_tensor(mparts[:, 2, :], mrest[:, :], mparts[:, 1, :], ALU.subtract
                                        ).then_inc(s_ms.sem, 1)

            nc.gpsimd.memset(zero[:, :], 0.0)
            nc.gpsimd.memset(vst[:, :, :, :, :], 1.0).then_inc(s_ones.sem, 1)
            pool.wait_ge(s_ones.sem, s_ones.at(1))
            if v_bias is None:
                pool.wait_ge(s_tk.sem, s_tk.at(KT))
            else:
                pool.wait_ge(s_w.sem, s_w.at(16 * NVW))
                for t in range(KT):
                    r = tile_rows(nk, t)
                    pool.wait_ge(s_tk.sem, s_tk.at(t + 1))
                    nc.gpsimd.tensor_tensor(m.v[0:r, t, :], m.v[0:r, t, :], vb[0:r, :], ALU.add
                                            ).then_inc(s_vb.sem, 1)
                pool.wait_ge(s_vb.sem, s_vb.at(KT))
            stage_v(0, 0)
            cut_max(items * NP + 3 + 1, 0)
            with pool.Fori(0, NB) as i:
                for u in range(UB):
                    U = i * UB + u
                    if u == 0:
                        pool.wait_ge(s_av.sem, s_av.at(U * KT))
                        stage_v(1, i * 2 + 1)
                    if u == NCH:
                        with pool.If(i < NB - 1):
                            pool.wait_ge(s_av.sem, s_av.at(U * KT))
                            stage_v(0, i + 2)   
                    if u < UB - 2:
                        cut_max(taken_before(U) + TURN_AT + 1, U + 1)
                with pool.If(i < NB - 1):
                    for u in (UB - 2, UB - 1):
                        U = i * UB + u
                        cut_max(taken_before(U) + TURN_AT + 1, U + 1)
                with pool.Else():
                    cut_max(taken_before(i * UB + UB - 2) + NSHORT, i * UB + UB - 1)

    s_kq[0].advance(2 * KQ)
    m.sig["head0"].advance(KQ)
    s_kq[1].advance(2 * KQ)
    s_st.advance(NU * 2 * KT)
    s_p.advance(NU * 2 * KT)
    s_av.advance(NU * KT)
    s_acc.advance(NU)
    for s in (s_mx, s_mt):
        s.advance(taken_before(NU - 2) + NSHORT)
    for s in (s_nm, s_m1, s_mr, s_m2, s_ms):
        s.advance(NU)
    s_init.advance(16 * NCONST)
    s_ones.advance(1)
    s_mo.advance(16 * NU)
    s_mi.advance(16 * NU)
    s_v.advance(NG)
    s_w.advance(16 * NVW)
    s_pr.advance(KT)
    s_tk.advance(KT)
    if v_bias is not None:
        s_vb.advance(KT)


def output_phase(nc, m, weight, bias, gate, extra=None):
    s_w, s_o, s_rd, s_a, s_at, s_as, s_y, s_x, s_wf, s_xb = (
        m.sig[n] for n in ("weights", "o_turned", "recip", "normalised", "a_turned", "a_saved", "y_ready",
                           "x_added", "w_folded", "x_biased"))
    nload = 1 + (bias is not None)
    with ExitStack() as ctx:
        m.uid += 1
        sb = lambda n, s, t=F32: ctx.enter_context(nc.sbuf_tensor(f"op{m.uid}_" + n, s, t))
        w = sb("w", [P, KD, D])
        bb = sb("bb", [P, D])
        rd = sb("rd", [P, 2, NH])
        a = sb("a", [P, 2, NH, DH])
        aT = sb("aT", [P, 2, KD, P])
        po = ctx.enter_context(nc.psum_tensor(f"op{m.uid}_po", [P, 2, CH], F32))
        pt = ctx.enter_context(nc.psum_tensor(f"op{m.uid}_pt", [P, 2, CH], F32))
        py = ctx.enter_context(nc.psum_tensor(f"op{m.uid}_py", [P, 2, CH], F32))
        block = ctx.enter_context(nc.Block())

        @block.sync
        def _(sp):
            sp.dma_start(w[:, :, :], weight.rearrange("(k p) n -> p k n", p=P)).then_inc(s_w.sem, 16)
            if bias is not None:
                sp.dma_start(bb[:, :], bias.partition_broadcast(P)).then_inc(s_w.sem, 16)

        @block.gpsimd
        def _(pool):
            pool.wait_ge(s_w.sem, s_w.at(16 * nload))
            if gate is not None:
                for k in range(KD):
                    last = nc.gpsimd.tensor_tensor(w[:, k, :], w[:, k, :], m.gates[:, gate, :], ALU.mult)
                last.then_inc(s_wf.sem, 1)
                nc.gpsimd.tensor_tensor(bb[:, :], bb[:, :], m.gates[:, gate, :], ALU.mult).then_inc(s_wf.sem, 1)
                pool.wait_ge(s_wf.sem, s_wf.at(2))
            if extra is not None:
                nc.gpsimd.tensor_scalar(bb[:, :], bb[:, :], extra[:, :], None, ALU.add).then_inc(s_wf.sem, 1)
                pool.wait_ge(s_wf.sem, s_wf.at(1))
            if bias is not None:
                for t in range(NT):
                    nc.gpsimd.tensor_tensor(m.x[:, t, :], m.x[:, t, :], bb[:, :], ALU.add).then_inc(s_xb.sem, 1)

        @block.tensor
        def _(pe):
            def open_heads(t):
                pe.wait_ge(s_a.sem, s_a.at(t - 1))
                for g in range(NG):
                    last = pe.transpose(po[:, t % 2, g * P:(g + 1) * P],
                                        m.attn[:, g * T + t * P:g * T + (t + 1) * P], m.ident[:, :])
                last.then_inc(s_o.sem, 1)

            def turn_back(t):
                pe.wait_ge(s_a.sem, s_a.at(t + 1))
                pe.wait_ge(s_as.sem, s_as.at(t - 1))
                for k in range(KD):
                    last = pe.transpose(pt[:, t % 2, k * P:(k + 1) * P],
                                        a[:, t % 2, k * (NH // KD):(k + 1) * (NH // KD), :].rearrange(
                                            "p h e -> p (h e)"), m.ident[:, :])
                last.then_inc(s_at.sem, 1)

            def project(t):
                pe.wait_ge(s_as.sem, s_as.at(t + 1))
                pe.wait_ge(s_x.sem, s_x.at(t - 1))
                for k in range(KD):
                    last = pe.matmul(py[:, t % 2, 0:D], aT[:, t % 2, k, :], w[:, k, :],
                                     start=(k == 0), stop=(k == KD - 1))
                last.then_inc(s_y.sem, 1)

            pe.wait_ge(s_w.sem, s_w.at(16 * nload))
            if gate is not None:
                pe.wait_ge(s_wf.sem, s_wf.at(2))
            for t in range(NT + 2):
                if t < NT:
                    open_heads(t)
                if 1 <= t <= NT:
                    turn_back(t - 1)
                if t >= 2:
                    project(t - 2)

        @block.scalar
        def _(act):
            for t in range(NT):
                act.wait_ge(s_at.sem, s_at.at(t + 1))
                act.wait_ge(s_y.sem, s_y.at(t - 1))
                nc.scalar.copy(aT[:, t % 2, :, :].rearrange("p k n -> p (k n)"), pt[:, t % 2, 0:D]
                               ).then_inc(s_as.sem, 1)

        @block.vector
        def _(dve):
            for t in range(NT + 2):
                if t < NT:
                    heads = po[:, t % 2, :].rearrange("p (h e) -> p h e", e=2 * DH)
                    dve.wait_ge(s_o.sem, s_o.at(t + 1))
                    nc.vector.reciprocal(rd[:, t % 2, :], heads[:, :, DH]).then_inc(s_rd.sem, 1)
                    dve.wait_ge(s_rd.sem, s_rd.at(t + 1))
                    dve.wait_ge(s_at.sem, s_at.at(t - 1))
                    nc.vector.tensor_tensor(a[:, t % 2, :, :], heads[:, :, 0:DH],
                                            rd[:, t % 2, :].unsqueeze(2).broadcast_to([P, NH, DH]), ALU.mult
                                            ).then_inc(s_a.sem, 1)
                if t >= 2:
                    y = t - 2
                    dve.wait_ge(s_y.sem, s_y.at(y + 1))
                    if bias is not None:
                        dve.wait_ge(s_xb.sem, s_xb.at(y + 1))
                    nc.vector.tensor_tensor(m.x[:, y, :], py[:, y % 2, 0:D], m.x[:, y, :], ALU.add
                                            ).then_inc(s_x.sem, 1)
                if t >= 3:
                    row_statistics(nc, m, dve, s_x, t - 3)
            for t in (NT - 1, NT):
                row_statistics(nc, m, dve, s_x, t)

    s_w.advance(16 * nload)
    for s in (s_o, s_rd, s_a, s_at, s_as, s_y, s_x, m.sig["x_stats"]):
        s.advance(NT)
    if gate is not None:
        s_wf.advance(2)
    if extra is not None:
        s_wf.advance(1)
    if bias is not None:
        s_xb.advance(NT)


def ffn_phase(nc, m, hT, w1, b1_col, w2, b2, gate, out):
    s_w, s_u, s_g, s_y, s_x, s_wf, s_xb, s_out = (m.sig[n] for n in (
        "weights", "up_ready", "gelu_ready", "y_ready", "x_added", "w_folded", "x_biased", "stored0"))
    NF = FF // P
    with ExitStack() as ctx:
        m.uid += 1
        sb = lambda n, s, t=F32: ctx.enter_context(nc.sbuf_tensor(f"ff{m.uid}_" + n, s, t))
        w1s = sb("w1", [P, KD, FF])
        w2s = sb("w2", [P, NF, D])
        bb = sb("bb", [P, D])
        hid = sb("hid", [P, 2, NF, CH])
        pu = ctx.enter_context(nc.psum_tensor(f"ff{m.uid}_pu", [P, 4, CH], F32))
        py = ctx.enter_context(nc.psum_tensor(f"ff{m.uid}_py", [P, 2, CH], F32))
        block = ctx.enter_context(nc.Block())

        @block.sync
        def _(sp):
            sp.dma_start(w1s[:, :, :], w1.rearrange("(k p) n -> p k n", p=P)).then_inc(s_w.sem, 16)
            sp.dma_start(w2s[:, :, :], w2.rearrange("(k p) n -> p k n", p=P)).then_inc(s_w.sem, 16)
            sp.dma_start(bb[:, :], b2.partition_broadcast(P)).then_inc(s_w.sem, 16)
            if out is not None:
                for c in range(NCH):
                    sp.wait_ge(s_x.sem, s_x.at(4 * c + 4))
                    sp.dma_start(out[c * CH:(c + 1) * CH, :].rearrange("(t p) n -> p t n", p=P),
                                 m.x[:, 4 * c:4 * c + 4, :]).then_inc(s_out.sem, 16)
                sp.wait_ge(s_out.sem, s_out.at(16 * NCH))

        @block.gpsimd
        def _(pool):
            pool.wait_ge(s_w.sem, s_w.at(48))
            if gate is not None:
                for k in range(NF):
                    last = nc.gpsimd.tensor_tensor(w2s[:, k, :], w2s[:, k, :], m.gates[:, gate, :], ALU.mult)
                last.then_inc(s_wf.sem, 1)
                nc.gpsimd.tensor_tensor(bb[:, :], bb[:, :], m.gates[:, gate, :], ALU.mult).then_inc(s_wf.sem, 1)
                pool.wait_ge(s_wf.sem, s_wf.at(2))
            for t in range(NT):
                nc.gpsimd.tensor_tensor(m.x[:, t, :], m.x[:, t, :], bb[:, :], ALU.add).then_inc(s_xb.sem, 1)

        @block.tensor
        def _(pe):
            def up(c):
                for f in range(NF):
                    i = c * NF + f
                    pe.wait_ge(s_g.sem, s_g.at(i - 3))
                    for k in range(KD):
                        last = pe.matmul(pu[:, i % 4, :], w1s[:, k, f * P:(f + 1) * P],
                                         hT[:, k, c * CH:(c + 1) * CH], start=(k == 0), stop=(k == KD - 1))
                    last.then_inc(s_u.sem, 1)

            def down(c):
                pe.wait_ge(s_g.sem, s_g.at((c + 1) * NF))
                for q in range(4):
                    t = 4 * c + q
                    pe.wait_ge(s_x.sem, s_x.at(t - 1))
                    for f in range(NF):
                        last = pe.matmul(py[:, t % 2, 0:D], hid[:, c % 2, f, q * P:(q + 1) * P], w2s[:, f, :],
                                         start=(f == 0), stop=(f == NF - 1))
                    last.then_inc(s_y.sem, 1)

            pe.wait_ge(s_w.sem, s_w.at(48))
            up(0)
            if gate is not None:
                pe.wait_ge(s_wf.sem, s_wf.at(2))
            for c in range(NCH):
                if c + 1 < NCH:
                    up(c + 1)
                down(c)

        @block.scalar
        def _(act):
            for i in range(NCH * NF):
                c, f = divmod(i, NF)
                act.wait_ge(s_u.sem, s_u.at(i + 1))
                if c >= 2 and f == 0:
                    act.wait_ge(s_y.sem, s_y.at(4 * (c - 1)))
                nc.scalar.activation(hid[:, c % 2, f, :], pu[:, i % 4, :], ACT.Gelu, bias=cols(m.mod, b1_col + f)
                                     ).then_inc(s_g.sem, 1)

        @block.vector
        def _(dve):
            for t in range(NT):
                dve.wait_ge(s_y.sem, s_y.at(t + 1))
                dve.wait_ge(s_xb.sem, s_xb.at(t + 1))
                nc.vector.tensor_tensor(m.x[:, t, :], py[:, t % 2, 0:D], m.x[:, t, :], ALU.add
                                        ).then_inc(s_x.sem, 1)
                if out is None:
                    row_statistics(nc, m, dve, s_x, t)
            if out is None:
                row_statistics(nc, m, dve, s_x, NT)

    s_w.advance(48)
    s_u.advance(NCH * NF)
    s_g.advance(NCH * NF)
    for s in (s_y, s_x, s_xb):
        s.advance(NT)
    if gate is not None:
        s_wf.advance(2)
    if out is not None:
        s_out.advance(16 * NCH)
    else:
        m.sig["x_stats"].advance(NT)


def evidence_phase(nc, m, qT, kT, evT):
    s_sc, s_mx, s_nb, s_e, s_rd, s_pn, s_tr, s_ts, s_ev, s_es = (m.sig[n] for n in (
        "scores_ready", "max_ready", "neg_ready", "probs_ready", "recip", "normalised", "turned", "turn_saved",
        "av_done", "acc_saved"))
    GROUPS = [(g, min(g + 4, NC2)) for g in range(0, NC2, 4)]
    NGR = len(GROUPS)
    SC = 1.0 / D ** 0.5
    with ExitStack() as ctx:
        m.uid += 1
        sb = lambda n, s, t=F32: ctx.enter_context(nc.sbuf_tensor(f"ev{m.uid}_" + n, s, t))
        probs = sb("probs", [P, 2, NS2])
        probsT = sb("probsT", [P, NC2, CH])
        mx = sb("mx", [P, NT])
        nb = sb("nb", [P, NT])
        den = sb("den", [P, NT])
        rden = sb("rden", [P, NT])
        ps = ctx.enter_context(nc.psum_tensor(f"ev{m.uid}_ps", [P, 4, CH], F32))
        pt = ctx.enter_context(nc.psum_tensor(f"ev{m.uid}_pt", [P, 2, CH], F32))
        po = ctx.enter_context(nc.psum_tensor(f"ev{m.uid}_po", [P, 2, CH], F32))
        allkeys = ps[:, :, :].rearrange("p a b -> p (a b)")[:, 0:NS2]
        block = ctx.enter_context(nc.Block())

        @block.tensor
        def _(pe):
            def score(t):
                pe.wait_ge(s_e.sem, s_e.at(t))
                for b in range(4):
                    n = min(CH, NS2 - b * CH)
                    for k in range(KD):
                        last = pe.matmul(ps[:, b, 0:n], qT[:, k, t * P:(t + 1) * P], kT[:, k, b * CH:b * CH + n],
                                         start=(k == 0), stop=(k == KD - 1))
                last.then_inc(s_sc.sem, 1)

            def turn(t):
                pe.wait_ge(s_pn.sem, s_pn.at(t + 1))
                for g, (a, b) in enumerate(GROUPS):
                    i = t * NGR + g
                    pe.wait_ge(s_ts.sem, s_ts.at(i - 1))
                    for kt in range(a, b):
                        r = tile_rows(NS2, kt)
                        last = pe.transpose(pt[0:r, i % 2, (kt - a) * P:(kt - a + 1) * P],
                                            probs[:, t % 2, kt * P:kt * P + r], m.ident[:, :])
                    last.then_inc(s_tr.sem, 1)

            def weigh(c):
                pe.wait_ge(s_ts.sem, s_ts.at(NGR * 4 * (c + 1)))
                for k in range(KD):
                    pe.wait_ge(s_es.sem, s_es.at(KD * c + k - 1))
                    for kt in range(NC2):
                        r = tile_rows(NS2, kt)
                        last = pe.matmul(po[:, k, :], m.v[0:r, kt, k * P:(k + 1) * P], probsT[0:r, kt, :],
                                         start=(kt == 0), stop=(kt == NC2 - 1))
                    last.then_inc(s_ev.sem, 1)

            for t in range(NT + 1):
                if t < NT:
                    score(t)
                if t >= 1:
                    turn(t - 1)
                    if t % 4 == 0:
                        weigh(t // 4 - 1)

        @block.vector
        def _(dve):
            def save(c):
                for k in range(KD):
                    dve.wait_ge(s_ev.sem, s_ev.at(KD * c + k + 1))
                    nc.vector.tensor_copy(evT[:, k, c * CH:(c + 1) * CH], po[:, k, :]).then_inc(s_es.sem, 1)

            for t in range(NT + 1):
                if t < NT:
                    dve.wait_ge(s_sc.sem, s_sc.at(t + 1))
                    nc.vector.reduce_max(cols(mx, t), allkeys, AX).then_inc(s_mx.sem, 1)
                    dve.wait_ge(s_mx.sem, s_mx.at(t + 1))
                    nc.vector.tensor_scalar(cols(nb, t), cols(mx, t), -SC, None, ALU.mult).then_inc(s_nb.sem, 1)
                    dve.wait_ge(s_e.sem, s_e.at(t + 1))
                    nc.vector.reciprocal(cols(rden, t), cols(den, t)).then_inc(s_rd.sem, 1)
                    dve.wait_ge(s_rd.sem, s_rd.at(t + 1))
                    nc.vector.tensor_scalar(probs[:, t % 2, :], probs[:, t % 2, :], cols(rden, t), None, ALU.mult
                                            ).then_inc(s_pn.sem, 1)
                    if t % 4 == 0 and t:
                        save(t // 4 - 1)
            save(NCH - 1)

        @block.scalar
        def _(act):
            def save_turned(t):
                for g, (a, b) in enumerate(GROUPS):
                    i = t * NGR + g
                    r = tile_rows(NS2, a)
                    act.wait_ge(s_tr.sem, s_tr.at(i + 1))
                    if t % 4 == 0 and g == 0 and t:
                        act.wait_ge(s_ev.sem, s_ev.at(KD * (t // 4)))
                    nc.scalar.copy(probsT[0:r, a:b, (t % 4) * P:(t % 4 + 1) * P],
                                   pt[0:r, i % 2, 0:(b - a) * P].rearrange("p (a b) -> p a b", b=P)
                                   ).then_inc(s_ts.sem, 1)

            for t in range(NT + 1):
                if t < NT:
                    act.wait_ge(s_nb.sem, s_nb.at(t + 1))
                    act.wait_ge(s_tr.sem, s_tr.at(NGR * (t - 1)) if t else s_tr.at(0))
                    nc.scalar.activation(probs[:, t % 2, :], allkeys, ACT.Exp, bias=cols(nb, t), scale=SC,
                                         accum_out=cols(den, t)).then_inc(s_e.sem, 1)
                if t >= 1:
                    save_turned(t - 1)

    for s in (s_sc, s_mx, s_nb, s_e, s_rd, s_pn):
        s.advance(NT)
    for s in (s_tr, s_ts):
        s.advance(NT * NGR)
    for s in (s_ev, s_es):
        s.advance(NCH * KD)


def fold_phase(nc, m, d, w2o, b2o):
    s_w, s_pr, s_tk, s_o, s_bc = (m.sig[n] for n in ("weights", "proj_ready", "proj_taken", "ones", "cond_bc"))
    RT = RH // P
    with ExitStack() as ctx:
        m.uid += 1
        sb = lambda n, s, t=F32: ctx.enter_context(nc.sbuf_tensor(f"fo{m.uid}_" + n, s, t))
        w2T = sb("w2T", [P, NE, KD, RH])
        ow = sb("ow", [P, KD, D])
        ob = sb("ob", [P, D])
        b2 = sb("b2", [P, NE, KD])
        b2bc = sb("b2bc", [P, NE, KD, P])
        ones = sb("ones", [P, P])
        ps = ctx.enter_context(nc.psum_tensor(f"fo{m.uid}_ps", [P, 4, CH], F32))
        block = ctx.enter_context(nc.Block())

        @block.sync
        def _(sp):
            for e in range(NE):
                sp.dma_start(w2T[:, e], d["e_w2T"][e].rearrange("(k p) r -> p k r", p=P)).then_inc(s_w.sem, 16)
            sp.dma_start(ow[:, :, :], d["L2_xcond_out_w"].rearrange("(k p) n -> p k n", p=P)).then_inc(s_w.sem, 16)
            sp.dma_start(ob[:, :], d["L2_xcond_out_b"].partition_broadcast(P)).then_inc(s_w.sem, 16)
            sp.dma_start(b2[:, :, :], d["e_b2_cols"].rearrange("p (e k) -> p e k", e=NE)).then_inc(s_w.sem, 16)

        @block.gpsimd
        def _(pool):
            nc.gpsimd.memset(ones[:, :], 1.0).then_inc(s_o.sem, 1)

        @block.tensor
        def _(pe):
            pe.wait_ge(s_w.sem, s_w.at(96))
            pe.wait_ge(s_bc.sem, s_bc.at(1))
            for i in range(NE * (RT + 1)):
                e, r = divmod(i, RT + 1)
                pe.wait_ge(s_tk.sem, s_tk.at(i - 3))
                for k in range(KD):
                    lhs = w2T[:, e, k, r * P:(r + 1) * P] if r < RT else b2bc[:, e, k, :]
                    last = pe.matmul(ps[:, i % 4, 0:D], lhs, ow[:, k, :], start=(k == 0), stop=(k == KD - 1))
                last.then_inc(s_pr.sem, 1)

        @block.vector
        def _(dve):
            dve.wait_ge(s_w.sem, s_w.at(96))
            dve.wait_ge(s_o.sem, s_o.at(1))
            for e in range(NE):
                for k in range(KD):
                    last = nc.vector.tensor_scalar(b2bc[:, e, k, :], ones[:, :], b2[:, e, k:k + 1], None, ALU.mult)
            last.then_inc(s_bc.sem, 1)
            for i in range(NE * (RT + 1)):
                e, r = divmod(i, RT + 1)
                dve.wait_ge(s_pr.sem, s_pr.at(i + 1))
                if r < RT:
                    nc.vector.tensor_copy(w2o[:, e, r, :], ps[:, i % 4, 0:D]).then_inc(s_tk.sem, 1)
                else:
                    nc.vector.tensor_tensor(b2o[:, e, :], ps[:, i % 4, 0:D], ob[:, :], ALU.add).then_inc(s_tk.sem, 1)

    s_w.advance(96)
    s_o.advance(1)
    s_bc.advance(1)
    for s in (s_pr, s_tk):
        s.advance(NE * (RT + 1))


def expert_phase(nc, m, d, nxT, evT, w2o, b2o):
    (s_w, s_u, s_g, s_r, s_rl, s_rm, s_rs, s_re, s_rt, s_rr, s_pb, s_gz, s_gp, s_gs, s_y, s_yt, s_ya, s_gy, s_x) = (
        m.sig[n] for n in ("weights", "up_ready", "gelu_ready", "r_ready", "r_logits", "r_max", "r_shifted",
                           "r_exp", "r_sum", "r_recip", "r_probs", "gate_ready", "gate_biased", "gate_open",
                           "y_ready", "y_biased", "y_summed", "y_gated", "x_added"))
    RT = RH // P
    KC = 2 * KD
    NU = KD + NE * RT
    with ExitStack() as ctx:
        m.uid += 1
        sb = lambda n, s, t=F32: ctx.enter_context(nc.sbuf_tensor(f"ex{m.uid}_" + n, s, t))
        w1 = sb("w1", [P, NE, KC, RH])
        gw1 = sb("gw1", [P, KC, D])
        gw2 = sb("gw2", [P, KD, D])
        gb2 = sb("gb2", [P, D])
        rw = sb("rw", [P, KC, NE])
        hid = sb("hid", [P, 2, NU, CH])
        logit = sb("logit", [P, 4, NE])
        rmax = sb("rmax", [P, 4])
        rexp = sb("rexp", [P, 4, NE])
        rsum = sb("rsum", [P, 4])
        prob = sb("prob", [P, 4, NE])
        gate = sb("gate", [P, 4, D])
        biased = sb("biased", [P, NE, D])
        summed = sb("summed", [P, D])
        pu = ctx.enter_context(nc.psum_tensor(f"ex{m.uid}_pu", [P, 2, CH], F32))
        pr = ctx.enter_context(nc.psum_tensor(f"ex{m.uid}_pr", [P, CH], F32))
        pg = ctx.enter_context(nc.psum_tensor(f"ex{m.uid}_pg", [P, 2, CH], F32))
        py = ctx.enter_context(nc.psum_tensor(f"ex{m.uid}_py", [P, NE, CH], F32))
        block = ctx.enter_context(nc.Block())
        NL = NE + 4
        moving = lambda k, c: (nxT if k < KD else evT)[:, k % KD, c * CH:(c + 1) * CH]
        stationary = lambda k, t: (nxT if k < KD else evT)[:, k % KD, t * P:(t + 1) * P]

        @block.sync
        def _(sp):
            for e in range(NE):
                sp.dma_start(w1[:, e], d["L2_xcond_e_w1"][e, 0:2 * D, :].rearrange("(k p) n -> p k n", p=P)
                             ).then_inc(s_w.sem, 16)
            sp.dma_start(gw1[:, :, :], d["L2_xcond_gate_w1"][0:2 * D, :].rearrange("(k p) n -> p k n", p=P)
                         ).then_inc(s_w.sem, 16)
            sp.dma_start(gw2[:, :, :], d["L2_xcond_gate_w2"].rearrange("(k p) n -> p k n", p=P)
                         ).then_inc(s_w.sem, 16)
            sp.dma_start(gb2[:, :], d["L2_xcond_gate_b2"].partition_broadcast(P)).then_inc(s_w.sem, 16)
            sp.dma_start(rw[:, :, :], d["L2_xcond_router_W"][0:2 * D, :].rearrange("(k p) n -> p k n", p=P)
                         ).then_inc(s_w.sem, 16)

        @block.tensor
        def _(pe):
            def up(c):
                for f in range(NU):
                    i = c * NU + f
                    pe.wait_ge(s_g.sem, s_g.at(i - 1))
                    for k in range(KC):
                        if f < KD:
                            w = gw1[:, k, f * P:(f + 1) * P]
                        else:
                            e, r = divmod(f - KD, RT)
                            w = w1[:, e, k, r * P:(r + 1) * P]
                        last = pe.matmul(pu[:, i % 2, :], w, moving(k, c), start=(k == 0), stop=(k == KC - 1))
                    last.then_inc(s_u.sem, 1)

            def route(c):
                pe.wait_ge(s_rl.sem, s_rl.at(c))
                for q in range(4):
                    for k in range(KC):
                        last = pe.matmul(pr[:, q * NE:(q + 1) * NE], stationary(k, 4 * c + q), rw[:, k, :],
                                         start=(k == 0), stop=(k == KC - 1))
                last.then_inc(s_r.sem, 1)

            def open_gate(c):
                pe.wait_ge(s_g.sem, s_g.at(c * NU + KD))
                pe.wait_ge(s_gp.sem, s_gp.at(c))
                for q in range(4):
                    for k in range(KD):
                        last = pe.matmul(pg[:, q // 2, (q % 2) * D:(q % 2 + 1) * D],
                                         hid[:, c % 2, k, q * P:(q + 1) * P], gw2[:, k, :],
                                         start=(k == 0), stop=(k == KD - 1))
                last.then_inc(s_gz.sem, 1)

            def down(c):
                pe.wait_ge(s_g.sem, s_g.at((c + 1) * NU))
                for q in range(4):
                    for e in range(NE):
                        i = (4 * c + q) * NE + e
                        pe.wait_ge(s_yt.sem, s_yt.at(i - NE + 1))
                        for r in range(RT):
                            last = pe.matmul(py[:, e, 0:D], hid[:, c % 2, KD + e * RT + r, q * P:(q + 1) * P],
                                             w2o[:, e, r, :], start=(r == 0), stop=(r == RT - 1))
                        last.then_inc(s_y.sem, 1)

            pe.wait_ge(s_w.sem, s_w.at(16 * NL))
            up(0)
            for c in range(NCH):
                route(c)
                open_gate(c)
                if c + 1 < NCH:
                    up(c + 1)
                down(c)

        @block.scalar
        def _(act):
            def silus(c):
                for f in range(NU):
                    i = c * NU + f
                    act.wait_ge(s_u.sem, s_u.at(i + 1))
                    if f == 0 and c >= 2:
                        act.wait_ge(s_y.sem, s_y.at(4 * NE * (c - 1)))
                    b = m.col["gb1"] + f if f < KD else m.col["eb1"] + f - KD
                    nc.scalar.activation(hid[:, c % 2, f, :], pu[:, i % 2, :], ACT.Silu, bias=cols(m.mod, b)
                                         ).then_inc(s_g.sem, 1)

            silus(0)
            for c in range(NCH):
                act.wait_ge(s_rs.sem, s_rs.at(c + 1))
                nc.scalar.activation(rexp[:, :, :], logit[:, :, :], ACT.Exp).then_inc(s_re.sem, 1)
                act.wait_ge(s_gp.sem, s_gp.at(c + 1))
                nc.scalar.activation(gate[:, :, :], gate[:, :, :], ACT.Sigmoid).then_inc(s_gs.sem, 1)
                if c + 1 < NCH:
                    silus(c + 1)

        @block.vector
        def _(dve):
            dve.wait_ge(s_w.sem, s_w.at(16 * NL))
            for c in range(NCH):
                dve.wait_ge(s_r.sem, s_r.at(c + 1))
                nc.vector.tensor_tensor(logit[:, :, :], pr[:, 0:4 * NE].rearrange("p (q e) -> p q e", e=NE),
                                        m.router_bias[:, :].unsqueeze(1).broadcast_to([P, 4, NE]), ALU.add
                                        ).then_inc(s_rl.sem, 1)
                dve.wait_ge(s_rl.sem, s_rl.at(c + 1))
                nc.vector.reduce_max(rmax[:, :], logit[:, :, :], AX).then_inc(s_rm.sem, 1)
                dve.wait_ge(s_rm.sem, s_rm.at(c + 1))
                nc.vector.tensor_tensor(logit[:, :, :], logit[:, :, :],
                                        rmax[:, :].unsqueeze(2).broadcast_to([P, 4, NE]), ALU.subtract
                                        ).then_inc(s_rs.sem, 1)
                dve.wait_ge(s_gz.sem, s_gz.at(c + 1))
                nc.vector.tensor_tensor(gate[:, :, :], pg[:, :, :].rearrange("p a (b n) -> p (a b) n", n=D),
                                        gb2[:, :].unsqueeze(1).broadcast_to([P, 4, D]), ALU.add
                                        ).then_inc(s_gp.sem, 1)
                dve.wait_ge(s_re.sem, s_re.at(c + 1))
                nc.vector.reduce_sum(rsum[:, :], rexp[:, :, :], AX).then_inc(s_rt.sem, 1)
                dve.wait_ge(s_rt.sem, s_rt.at(c + 1))
                nc.vector.reciprocal(rmax[:, :], rsum[:, :]).then_inc(s_rr.sem, 1)
                dve.wait_ge(s_rr.sem, s_rr.at(c + 1))
                nc.vector.tensor_tensor(prob[:, :, :], rexp[:, :, :],
                                        rmax[:, :].unsqueeze(2).broadcast_to([P, 4, NE]), ALU.mult
                                        ).then_inc(s_pb.sem, 1)
                dve.wait_ge(s_pb.sem, s_pb.at(c + 1))
                dve.wait_ge(s_gs.sem, s_gs.at(c + 1))
                for q in range(4):
                    t = 4 * c + q
                    for e in range(NE):
                        i = t * NE + e
                        dve.wait_ge(s_y.sem, s_y.at(i + 1))
                        nc.vector.tensor_tensor(biased[:, e, :], py[:, e, 0:D], b2o[:, e, :], ALU.add
                                                ).then_inc(s_yt.sem, 1)
                        dve.wait_ge(s_yt.sem, s_yt.at(i + 1))
                        p = prob[:, q, e:e + 1]
                        if e == 0:
                            op = nc.vector.tensor_scalar(summed[:, :], biased[:, e, :], p, None, ALU.mult)
                        else:
                            dve.wait_ge(s_ya.sem, s_ya.at(i))
                            op = nc.vector.scalar_tensor_tensor(out=summed[:, :], in0=biased[:, e, :], scalar=p,
                                                                in1=summed[:, :], op0=ALU.mult, op1=ALU.add)
                        op.then_inc(s_ya.sem, 1)
                    dve.wait_ge(s_ya.sem, s_ya.at((t + 1) * NE))
                    nc.vector.tensor_tensor(summed[:, :], summed[:, :], gate[:, q, :], ALU.mult).then_inc(s_gy.sem, 1)
                    dve.wait_ge(s_gy.sem, s_gy.at(t + 1))
                    nc.vector.tensor_tensor(m.x[:, t, :], m.x[:, t, :], summed[:, :], ALU.add).then_inc(s_x.sem, 1)
                    row_statistics(nc, m, dve, s_x, t)
            row_statistics(nc, m, dve, s_x, NT)

    s_w.advance(16 * NL)
    for s in (s_u, s_g):
        s.advance(NCH * NU)
    for s in (s_r, s_rl, s_rm, s_rs, s_re, s_rt, s_rr, s_pb, s_gz, s_gp, s_gs):
        s.advance(NCH)
    for s in (s_y, s_yt, s_ya):
        s.advance(NT * NE)
    for s in (s_gy, s_x, m.sig["x_stats"]):
        s.advance(NT)


SIGNALS = """cond_in x_in x_stats normed_pool rows_saved mask_in mask_step const_set load weights cond_ready mod_ready mod_saved stats rstd normed turned turn_saved ones cond_bc dve
cols_ready proj_ready proj_taken rot_ready rot_taken feat_final part1 rest part2 parts_ready stored0 stored1
stored2 stored3 head0 kq0 kq1 scores_ready probs_ready av_done acc_saved max_ready max_taken maxes_ready neg_ready
m_part1 m_rest m_part2 ones_set m_parts m_out m_in v_staged v_biased rows_ready o_turned recip normalised
a_turned a_saved y_ready x_added w_folded x_biased up_ready gelu_ready r_ready r_logits r_max r_shifted r_exp
r_sum r_recip r_probs gate_ready gate_biased gate_open y_biased y_summed y_gated""".split()


def build(nc, d, out):
    m = Machine()
    m.uid = 0
    m.L = NS2 - (NC2 - 1) * P
    m.col, at = {}, 0
    for name, n in (("l0", 12), ("l1", 8), ("l3", 12), ("eb1", NE * RH // P), ("gb1", KD), ("ln2g", KD), ("ln2b", KD),
                    ("l0b1", FF // P), ("l3b1", FF // P), ("l1q", KD), ("l1k", KD), ("l3q", KD), ("l3k", KD),
                    ("l3cq", KD), ("l3ck", KD)):
        m.col[name] = at
        at += n
    m.NCOL = at
    with ExitStack() as ctx:
        sb = lambda n, s, t=F32: ctx.enter_context(nc.sbuf_tensor(n, s, t))
        m.sig = {n: Signal(ctx.enter_context(nc.semaphore(n))) for n in SIGNALS}
        m.x = sb("x_sb", [P, NT, D])
        m.v = sb("v_sb", [P, NT, D])
        m.attn = sb("attn", [P, NG * T])
        m.ctxT = sb("ctxT", [P, KD, NS2])
        m.ctxnT = sb("ctxnT", [P, KD, NS2])
        m.x_stats = sb("x_stats_sb", [P, NT, 6])
        m.x_mean_var = sb("x_mean_var", [P, NT, 2])
        m.ident = sb("ident_sb", [P, P])
        m.mod = sb("mod", [P, m.NCOL])
        m.gates = sb("gates", [P, 2, D])
        m.router_bias = sb("router_bias", [P, NE])
        m.none_left = sb("none_left", [P, 1])
        dram = lambda n, s, t: nc.dram_tensor(n, s, t, kind="Internal").ap()
        m.q_parts = dram("q_parts", (PARTS, D, T), BF16)
        m.k_parts = dram("k_parts", (PARTS, D, T), BF16)
        m.m_scratch = dram("m_scratch", (PARTS, HG * CH // P, P), BF16)
        m.mask_row = dram("mask_row", (1, NS2), BF16)
        m.const_rows = dram("const_rows", (KROWS - MASK_ROW, T), BF16)
        hT = m.attn[:, 0:KD * T].rearrange("p (k t) -> p k t", k=KD)
        evT = m.attn[:, KD * T:2 * KD * T].rearrange("p (k t) -> p k t", k=KD)
        c = m.col

        with nc.Block() as block:
            @block.sync
            def _(sp):
                for s in m.sig.values():
                    sp.sem_inc(s.sem, CREDIT)

        setup_phase(nc, m, d)

        def feature(w, wcol, src, n_src, bias, parts, keep=None):
            jobs = []
            for c0 in range(0, n_src, CH):
                n = min(CH, n_src - c0)
                for f in range(KD):
                    lhs = [w[:, k, wcol + f * P:wcol + (f + 1) * P] for k in range(KD)]
                    rhs = [src[:, k, c0:c0 + n] for k in range(KD)]
                    store = None if parts is None else parts[:, f * P:(f + 1) * P, c0:c0 + n].rearrange("a p t -> p a t")
                    kept = None if keep is None else keep[:, f, c0:c0 + n]
                    jobs.append((lhs, rhs, n, None if bias is None else bias + f, store, kept, c0))
            return jobs

        def token(w, wcol, src, n_src, bias_bc):
            jobs = []
            for t in range(-(-n_src // P)):
                r = tile_rows(n_src, t)
                jobs.append(([src[:, k, t * P:t * P + r] for k in range(KD)], r,
                             [w[:, k, wcol:wcol + D] for k in range(KD)], bias_bc, m.v[0:r, t, :]))
            return jobs

        def view(name):
            return d[name].rearrange("(k p) n -> p k n", p=P)

        def qkv(name, q, k, v, rope, k_src, nk, keep=None):
            with ExitStack() as cx:
                m.uid += 1
                tiles, loads = {}, []
                store = keep is None
                for w, _, _ in (q, k) if store else (q, k, v):
                    if w not in tiles:
                        n = d[w].shape[1]
                        tiles[w] = cx.enter_context(nc.sbuf_tensor(f"w{m.uid}_{len(tiles)}", [P, KD, n], F32))
                        loads.append((tiles[w][:, :, :], view(w)))
                if rope:
                    m.swap = cx.enter_context(nc.sbuf_tensor(f"swap{m.uid}", [P, P], F32))
                    m.cos = cx.enter_context(nc.sbuf_tensor(f"cos{m.uid}", [P, T], F32))
                    m.sin = cx.enter_context(nc.sbuf_tensor(f"sin{m.uid}", [P, T], F32))
                    for a, b in ((m.swap, "swap"), (m.cos, "cos"), (m.sin, "sin")):
                        loads.append((a[:, :], d[b]))
                bias = None
                if v[2] is not None and not store:
                    bias = cx.enter_context(nc.sbuf_tensor(f"vb{m.uid}", [P, D], F32))
                    loads.append((bias[:, :], v[2].partition_broadcast(P)))
                fj = feature(tiles[k[0]], k[1], k_src, nk, k[2], m.k_parts if store else None,
                             None if store else keep[1])
                fj += feature(tiles[q[0]], q[1], hT, T, q[2], m.q_parts if store else None,
                              None if store else keep[0])
                tj = [] if store else token(tiles[v[0]], v[1], k_src, nk, bias)
                projection_phase(nc, m, loads, fj, tj, rope)
            return k_src, view(v[0])[:, :, v[1]:v[1] + D], v[2]

        norm_phase(nc, m, hT, 1e-5, c["l0"], c["l0"] + 2)
        values = qkv("l0s", ("l0_qkv_wT", 0, None), ("l0_qkv_wT", D, None), ("l0_qkv_wT", 2 * D, None), True, hT, T)
        attention_phase(nc, m, T, False, values)
        output_phase(nc, m, d["l0_sa_wT"], None, None)
        norm_phase(nc, m, hT, 1e-5, c["l0"] + 4, c["l0"] + 6)
        values = qkv("l0c", ("l0_q_wT", 0, None), ("l0_k_wT", 0, None), ("l0_v_wT", 0, None), True, m.ctxT, NS2)
        attention_phase(nc, m, NS2, False, values)
        output_phase(nc, m, d["l0_ca_wT"], None, None)
        norm_phase(nc, m, hT, 1e-5, c["l0"] + 8, c["l0"] + 10)
        ffn_phase(nc, m, hT, d["l0_w1T"], c["l0b1"], d["l0_w2T"], d["L0_xcond_ffn_b2"], None, None)
        norm_phase(nc, m, hT, 1e-5, c["l1"], c["l1"] + 2)
        values = qkv("l1", ("L1_xcond_Wq", 0, c["l1q"]), ("L1_xcond_Wkv", 0, c["l1k"]),
            ("L1_xcond_Wkv", D, d["L1_xcond_bkv"][D:2 * D]), False, m.ctxnT, NS2)
        attention_phase(nc, m, NS2, False, values)
        output_phase(nc, m, d["L1_xcond_Wp"], d["L1_xcond_bp"], None)
        norm_phase(nc, m, hT, 1e-5, c["ln2g"], c["ln2b"])
        with ExitStack() as cx:
            q2T = cx.enter_context(nc.sbuf_tensor("q2T", [P, KD, T], F32))
            k2T = cx.enter_context(nc.sbuf_tensor("k2T", [P, KD, NS2], F32))
            qkv("l2", ("L2_xcond_Wq", 0, None), ("L2_xcond_Wk", 0, None), ("L2_xcond_Wv", 0, None), False,
                m.ctxT, NS2, keep=(q2T, k2T))
            evidence_phase(nc, m, q2T, k2T, evT)
        with ExitStack() as cx:
            w2o = cx.enter_context(nc.sbuf_tensor("w2o", [P, NE, RH // P, D], F32))
            b2o = cx.enter_context(nc.sbuf_tensor("b2o", [P, NE, D], F32))
            fold_phase(nc, m, d, w2o, b2o)
            expert_phase(nc, m, d, hT, evT, w2o, b2o)
        norm_phase(nc, m, hT, 1e-6, c["l3"] + 2, c["l3"])
        values = qkv("l3s", ("L3_xcond_qkv_w", 0, c["l3q"]), ("L3_xcond_qkv_w", D, c["l3k"]),
            ("L3_xcond_qkv_w", 2 * D, d["L3_xcond_qkv_b"][2 * D:3 * D]), False, hT, T)
        attention_phase(nc, m, T, False, values)
        output_phase(nc, m, d["L3_xcond_sa_proj_w"], d["L3_xcond_sa_proj_b"], 0)
        norm_phase(nc, m, hT, 1e-6, None, None)
        values = qkv("l3c", ("L3_xcond_q_w", 0, c["l3cq"]), ("L3_xcond_kv_w", 0, c["l3ck"]),
            ("L3_xcond_kv_w", D, d["L3_xcond_kv_b"][D:2 * D]), False, m.ctxT, NS2)
        attention_phase(nc, m, NS2, True, values)
        output_phase(nc, m, d["L3_xcond_ca_proj_w"], d["L3_xcond_ca_proj_b"], None, m.none_left)
        norm_phase(nc, m, hT, 1e-6, c["l3"] + 8, c["l3"] + 6)
        ffn_phase(nc, m, hT, d["L3_xcond_fc1_w"], c["l3b1"], d["L3_xcond_fc2_w"], d["L3_xcond_fc2_b"], 1, out)


def kernel(**inputs):
    import numpy as np
    import concourse.bacc as bacc
    from concourse.bass_utils import run_bass_kernel_spmd

    a = {n: np.ascontiguousarray(v) for n, v in inputs.items()}
    columns = lambda v: np.asarray(v).reshape(-1, P).T
    arrays = {
        "x": a["x"][0], "ctx": a["ctx_1024"][0], "cond": columns(a["cond_1024"]),
        "mask": np.pad(a["mask_BxS2_bf0"], ((0, 0), (0, -NS2 % 4))).view(np.int32),
        "ident": np.eye(P, dtype=np.float32),
        "l0_ln_wT": np.stack([a[f"L0_xcond_ln{i}_w"].T for i in (1, 2, 3)]),
        "l0_qkv_wT": a["L0_xcond_qkv_w"].T, "l0_sa_wT": a["L0_xcond_sa_out_w"].T,
        "l0_q_wT": a["L0_xcond_q_w"].T, "l0_k_wT": a["L0_xcond_k_w"].T, "l0_v_wT": a["L0_xcond_v_w"].T,
        "l0_ca_wT": a["L0_xcond_ca_out_w"].T, "l0_w1T": a["L0_xcond_ffn_w1"].T, "l0_w2T": a["L0_xcond_ffn_w2"].T,
        "e_w2T": a["L2_xcond_e_w2"].transpose(0, 2, 1),
        "e_b2_cols": columns(a["L2_xcond_e_b2"]),
        "bias_cols": np.concatenate([columns(a[n]) for n in (
            "L0_xcond_ln1_b", "L0_xcond_ln2_b", "L0_xcond_ln3_b", "L1_xcond_bss_q", "L1_xcond_bss_kv",
            "L3_xcond_ada_b", "L2_xcond_e_b1", "L2_xcond_gate_b1", "L2_xcond_ln_gamma", "L2_xcond_ln_beta",
            "L0_xcond_ffn_b1", "L3_xcond_fc1_b", "L1_xcond_bq")]
            + [columns(a["L1_xcond_bkv"][0:D])]
            + [columns(a["L3_xcond_qkv_b"][0:2 * D]), columns(a["L3_xcond_q_b"]), columns(a["L3_xcond_kv_b"][0:D])],
            axis=1),
    }
    half = DH // 2
    freq = (np.float32(1.0) / np.power(np.float32(10000.0), np.arange(half, dtype=np.float32) / np.float32(half))
            ).astype(np.float32)
    angle = np.arange(T, dtype=np.float32)[None, :] * freq[:, None]
    arrays["cos"] = np.tile(np.cos(angle), (P // half, 1)).astype(np.float32)
    arrays["sin"] = np.tile(np.concatenate([-np.sin(angle), np.sin(angle)]), (P // DH, 1)).astype(np.float32)
    swap = np.zeros((P, P), np.float32)
    swap[np.arange(P), np.arange(P) ^ half] = 1.0
    arrays["swap"] = swap
    for n in ("L1_xcond_Wss_q", "L1_xcond_Wss_kv", "L1_xcond_Wq", "L1_xcond_Wkv", "L1_xcond_bkv", "L1_xcond_Wp",
              "L1_xcond_bp", "L0_xcond_ffn_b2", "L2_xcond_Wq", "L2_xcond_Wk", "L2_xcond_Wv", "L2_xcond_router_W",
              "L2_xcond_router_b", "L2_xcond_e_w1", "L2_xcond_gate_w1", "L2_xcond_gate_w2", "L2_xcond_gate_b2",
              "L2_xcond_out_w", "L2_xcond_out_b", "L3_xcond_ada_w", "L3_xcond_ada_b", "L3_xcond_qkv_w",
              "L3_xcond_qkv_b", "L3_xcond_sa_proj_w", "L3_xcond_sa_proj_b", "L3_xcond_q_w", "L3_xcond_kv_w",
              "L3_xcond_kv_b", "L3_xcond_ca_proj_w", "L3_xcond_ca_proj_b", "L3_xcond_fc1_w", "L3_xcond_fc2_w",
              "L3_xcond_fc2_b"):
        arrays[n] = a[n]
    arrays = {"in_" + n: np.ascontiguousarray(v) for n, v in arrays.items()}
    nc = bacc.Bacc("TRN2", target_bir_lowering=False, num_devices=1)
    d = {n[3:]: nc.dram_tensor(n, v.shape, mybir.dt.from_np(v.dtype), kind="ExternalInput").ap()
         for n, v in arrays.items()}
    out = nc.dram_tensor("out_x", (T, D), F32, kind="ExternalOutput").ap()
    build(nc, d, out)
    r = run_bass_kernel_spmd(nc, [arrays], core_ids=[0])
    return r.results[0]["out_x"].reshape(1, T, D)
```

```python
from contextlib import ExitStack

import concourse.bass as bass
from concourse import mybir

F32 = mybir.dt.float32
BF16 = mybir.dt.bfloat16
F32R = mybir.dt.float32r
U8 = mybir.dt.uint8
ALU = mybir.AluOpType
ACT = mybir.ActivationFunctionType
AX = mybir.AxisListType.X

P = 128
T = 2048
D = 256
NH = 16
DH = D // NH
NT = T // P
NS2 = 1601
NC2 = -(-NS2 // P)
CH = 512
NCH = T // CH
KD = D // P
FF = 1024
NE = 3
RH = 512
HG = 4
NG = NH // HG
PARTS = 3
Q_PART = (0, 1, 2, 0, 1, 0)
K_PART = (0, 0, 0, 1, 1, 2)
PAIR_ROWS = DH * len(Q_PART)
MASK_ROW = PAIR_ROWS
MAX_ROW = MASK_ROW + 1
KROWS = MAX_ROW + PARTS
KQ = 16 * 2 * len(Q_PART)
NCONST = 16 * 3
CREDIT = 8
MASK_BIAS = -1.0e30


def tile_rows(n, i):
    return min(P, n - i * P)


class Signal:

    def __init__(self, sem):
        self.sem = sem
        self.start = CREDIT

    def at(self, n):
        return self.start + n

    def advance(self, n):
        self.start += n


class Machine:
    pass


def cols(ap, k):
    return ap[:, k:k + 1]


def setup_phase(nc, m, d):
    s_in, s_load, s_w, s_cond, s_bc, s_row, s_rowv, s_mod, s_gate, s_modv, s_cols = (m.sig[n] for n in (
        "cond_in", "load", "weights", "cond_ready", "cond_bc", "rows_ready", "rows_saved", "mod_ready",
        "gate_ready", "mod_saved", "cols_ready"))
    s_st, s_rs, s_n, s_tr, s_ev, s_ones, s_d = (m.sig[n] for n in (
        "stats", "rstd", "normed", "turned", "turn_saved", "ones", "dve"))
    s_mk, s_mkd, s_const, s_out = (m.sig[n] for n in ("mask_in", "mask_step", "const_set", "stored0"))
    with ExitStack() as ctx:
        sb = lambda n, s, t=F32: ctx.enter_context(nc.sbuf_tensor("su_" + n, s, t))
        lnw = sb("lnw", [P, 3, KD, 2 * D])
        l1w = sb("l1w", [P, 2, KD, 2 * D])
        adaw = sb("adaw", [P, KD, 6 * D])
        ew1c = sb("ew1c", [P, NE, KD, RH])
        gw1c = sb("gw1c", [P, KD, D])
        rwc = sb("rwc", [P, KD, NE])
        bias_cols = sb("bias_cols", [P, m.NCOL])
        gate_b = sb("gate_b", [P, 2, D])
        rb = sb("rb", [P, NE])
        cond = sb("cond", [P, KD])
        silu_cond = sb("silu_cond", [P, KD])
        cond_bc = sb("cond_bc", [P, 2, KD, P])
        ones = sb("ones", [P, P])
        rows = sb("rows", [P, 3, CH])
        ct = sb("ct", [P, NC2, D])
        cn = sb("cn", [P, NC2, D])
        st = sb("st", [P, NC2, 6])
        mv = sb("mv", [P, NC2, 2])
        var = sb("var", [P, NC2])
        std = sb("std", [P, NC2])
        rstd = sb("rstd", [P, NC2])
        raw = sb("raw", [P, -(-NS2 // 4)], mybir.dt.int32)
        as_f = sb("as_f", [P, NS2])
        mask_bias = sb("mask_bias", [1, NS2], BF16)
        const = sb("const", [1, 2, T], BF16)
        left = sb("left", [P, 1])
        inv = sb("inv", [P, 1])
        ps = ctx.enter_context(nc.psum_tensor("su_ps", [P, 8, CH], F32))
        L = m.L
        chunks = [(lnw[:, i], 0, CH) for i in range(3)] + [(l1w[:, i], 1, CH) for i in range(2)]
        chunks += [(adaw[:, :, i * CH:(i + 1) * CH], 1, CH) for i in range(3)]
        chunks += [(ew1c[:, e], 0, CH) for e in range(NE)] + [(gw1c, 0, D)]
        assert [m.col[n] for n in ("l0", "l1", "l3", "eb1", "gb1")] == [0, 12, 20, 32, 44]
        NCHUNK = len(chunks)
        NROW = -(-NCHUNK // 4)
        NJ = sum(w for _, _, w in chunks) // P
        plus_one = [m.col["l0"] + 4 * i for i in range(3)]
        plus_one += [m.col["l1"], m.col["l1"] + 4, m.col["l3"] + 2, m.col["l3"] + 8]
        NSTORE = 1 + KROWS - MASK_ROW
        loads = [(lnw[:, i], d["l0_ln_wT"][i].rearrange("(k p) n -> p k n", p=P)) for i in range(3)]
        loads += [(l1w[:, i], d[n].rearrange("(k p) n -> p k n", p=P))
                  for i, n in enumerate(("L1_xcond_Wss_q", "L1_xcond_Wss_kv"))]
        loads += [(adaw[:, :, :], d["L3_xcond_ada_w"].rearrange("(k p) n -> p k n", p=P))]
        loads += [(ew1c[:, e], d["L2_xcond_e_w1"][e, 2 * D:3 * D, :].rearrange("(k p) n -> p k n", p=P))
                  for e in range(NE)]
        loads += [(gw1c[:, :, :], d["L2_xcond_gate_w1"][2 * D:3 * D, :].rearrange("(k p) n -> p k n", p=P)),
                  (rwc[:, :, :], d["L2_xcond_router_W"][2 * D:3 * D, :].rearrange("(k p) n -> p k n", p=P)),
                  (bias_cols[:, :], d["bias_cols"]),
                  (rb[:, :], d["L2_xcond_router_b"].partition_broadcast(P))]
        loads += [(gate_b[:, i], d["L3_xcond_ada_b"][j * D:(j + 1) * D].partition_broadcast(P))
                  for i, j in enumerate((2, 5))]
        NLOAD = len(loads)

        block = ctx.enter_context(nc.Block())

        @block.sync
        def _(sp):
            sp.dma_start(raw[:, :], d["mask"].rearrange("a n -> (a n)").partition_broadcast(P)).then_inc(s_mk.sem, 16)
            for dst, src in loads:
                sp.dma_start(dst, src).then_inc(s_w.sem, 16)
            sp.wait_ge(s_const.sem, s_const.at(2))
            for r in range(KROWS - MASK_ROW):
                sp.dma_start(m.const_rows[r:r + 1, :], const[:, min(r, 1), :]).then_inc(s_out.sem, 16)
            sp.wait_ge(s_mkd.sem, s_mkd.at(2))
            sp.dma_start(m.mask_row[:, :], mask_bias[:, :]).then_inc(s_out.sem, 16)
            sp.wait_ge(s_out.sem, s_out.at(16 * NSTORE))

        @block.gpsimd
        def _(pool):
            nc.gpsimd.memset(ones[:, :], 1.0).then_inc(s_ones.sem, 1)
            nc.gpsimd.memset(const[:, 0, :], 0.0).then_inc(s_const.sem, 1)
            nc.gpsimd.memset(const[:, 1, :], 1.0).then_inc(s_const.sem, 1)

        @block.scalar
        def _(act):
            act.dma_start(cond[:, :], d["cond"]).then_inc(s_in.sem, 16)
            act.dma_start(m.ident[:, :], d["ident"]).then_inc(s_in.sem, 16)
            act.dma_start(ct[:, 0:NC2 - 1, :], d["ctx"][0:(NC2 - 1) * P, :].rearrange("(t p) n -> p t n", p=P)
                          ).then_inc(s_load.sem, 16)
            act.dma_start(ct[0:L, NC2 - 1, :], d["ctx"][(NC2 - 1) * P:NS2, :]).then_inc(s_load.sem, 16)
            act.dma_start(m.x[:, :, :], d["x"].rearrange("(t p) n -> p t n", p=P)).then_inc(m.sig["x_in"].sem, 16)
            act.wait_ge(s_in.sem, s_in.at(32))
            nc.scalar.activation(silu_cond[:, :], cond[:, :], ACT.Silu).then_inc(s_cond.sem, 1)
            act.wait_ge(s_st.sem, s_st.at(1))
            nc.scalar.activation(std[:, :], var[:, :], ACT.Sqrt).then_inc(s_rs.sem, 1)
            turn = 0
            for src in range(2):
                if src == 1:
                    act.wait_ge(s_row.sem, s_row.at(1))
                    nc.scalar.copy(rows[:, 0:NROW - 1, :], ps[:, 0:NROW - 1, :]).then_inc(s_rowv.sem, 1)
                    nc.scalar.copy(rows[:, NROW - 1, 0:D], ps[:, NROW - 1, 0:D]).then_inc(s_rowv.sem, 1)
                    nc.scalar.copy(rows[0:96, NROW - 1, D:CH], ps[0:96, NROW - 1, D:CH]).then_inc(s_rowv.sem, 1)
                    act.wait_ge(s_cols.sem, s_cols.at(1))
                for t4 in range(4):
                    for k in range(KD):
                        n = min(4 * P, NS2 - t4 * 4 * P)
                        act.wait_ge(s_tr.sem, s_tr.at(turn + 1))
                        dst = (m.ctxT, m.ctxnT)[src][:, k, t4 * CH:t4 * CH + n]
                        if src == 0:
                            nc.scalar.copy(dst, ps[:, 4 + turn % 4, 0:n]).then_inc(s_ev.sem, 1)
                        else:
                            c = m.col["l1"] + 4
                            nc.scalar.activation(dst, ps[:, 4 + turn % 4, 0:n], ACT.Identity,
                                                 scale=cols(m.mod, c + k), bias=cols(m.mod, c + 2 + k)
                                                 ).then_inc(s_ev.sem, 1)
                        turn += 1

        @block.vector
        def _(dve):
            dve.wait_ge(s_in.sem, s_in.at(32))
            dve.wait_ge(s_ones.sem, s_ones.at(1))
            dve.wait_ge(s_cond.sem, s_cond.at(1))
            for i, c in enumerate((cond, silu_cond)):
                for k in range(KD):
                    last = nc.vector.tensor_scalar(cond_bc[:, i, k, :], ones[:, :], cols(c, k), None, ALU.mult)
            last.then_inc(s_bc.sem, 1)
            dve.wait_ge(s_load.sem, s_load.at(32))
            for t in range(NC2):
                r = tile_rows(NS2, t)
                nc.vector.bn_stats(st[0:r, t, :], ct[0:r, t, :]).then_inc(s_d.sem, 1)
            nc.vector.memset(var[:, :], 1.0).then_inc(s_d.sem, 1)
            dve.wait_ge(s_d.sem, s_d.at(NC2 + 1))
            for t in range(NC2):
                r = tile_rows(NS2, t)
                nc.vector.bn_aggr(mv[0:r, t, :], st[0:r, t, :]).then_inc(s_d.sem, 1)
            dve.wait_ge(s_d.sem, s_d.at(2 * NC2 + 1))
            nc.vector.tensor_scalar(var[:, 0:NC2 - 1], mv[:, 0:NC2 - 1, 1], 1e-5, None, ALU.add)
            nc.vector.tensor_scalar(var[0:L, NC2 - 1:NC2], mv[0:L, NC2 - 1, 1:2], 1e-5, None, ALU.add
                                    ).then_inc(s_st.sem, 1)
            dve.wait_ge(s_rs.sem, s_rs.at(1))
            nc.vector.reciprocal(rstd[:, :], std[:, :]).then_inc(s_d.sem, 1)
            dve.wait_ge(s_d.sem, s_d.at(2 * NC2 + 2))
            for t in range(NC2):
                r = tile_rows(NS2, t)
                nc.vector.tensor_scalar(cn[0:r, t, :], ct[0:r, t, :], mv[0:r, t, 0:1], rstd[0:r, t:t + 1],
                                        ALU.subtract, ALU.mult).then_inc(s_n.sem, 1)
            dve.wait_ge(s_mk.sem, s_mk.at(16))
            nc.vector.tensor_copy(as_f[:, :], raw[:, :].bitcast(U8)[:, 0:NS2]).then_inc(s_mkd.sem, 1)
            dve.wait_ge(s_mkd.sem, s_mkd.at(1))
            nc.vector.tensor_scalar(mask_bias[:, :], as_f[0:1, :], MASK_BIAS, None, ALU.mult).then_inc(s_mkd.sem, 1)
            nc.vector.reduce_sum(left[:, :], as_f[:, :], AX).then_inc(s_mkd.sem, 1)
            dve.wait_ge(s_mkd.sem, s_mkd.at(3))
            nc.vector.tensor_scalar(left[:, :], left[:, :], -1.0, float(NS2), ALU.mult, ALU.add
                                    ).then_inc(s_mkd.sem, 1)
            dve.wait_ge(s_mkd.sem, s_mkd.at(4))
            nc.vector.reciprocal(inv[:, :], left[:, :]).then_inc(s_mkd.sem, 1)
            dve.wait_ge(s_mkd.sem, s_mkd.at(5))
            nc.vector.tensor_scalar(m.none_left[:, :], inv[:, :], 0.0, None, ALU.mult).then_inc(s_mkd.sem, 1)
            dve.wait_ge(m.sig["x_in"].sem, m.sig["x_in"].at(16))
            for t in range(NT):
                nc.vector.bn_stats(m.x_stats[:, t, :], m.x[:, t, :]).then_inc(m.sig["x_stats"].sem, 1)
            dve.wait_ge(m.sig["x_stats"].sem, m.sig["x_stats"].at(NT))
            for t in range(NT):
                nc.vector.bn_aggr(m.x_mean_var[:, t, :], m.x_stats[:, t, :])
            dve.wait_ge(s_w.sem, s_w.at(16 * NLOAD))
            dve.wait_ge(s_mod.sem, s_mod.at(1))
            for b in range(NROW):
                columns = ps[:, b, :].rearrange("p (q j r) -> p j q r", q=4, j=4)
                for j in range(4):
                    c = 16 * b + 4 * j
                    w = min(4, NJ - c)
                    last = nc.vector.tensor_tensor(m.mod[:, c:c + w], columns[:, j, 0:w, 0],
                                                   bias_cols[:, c:c + w], ALU.add)
            last.then_inc(s_d.sem, 1)
            nc.vector.tensor_copy(m.mod[:, NJ:m.NCOL], bias_cols[:, NJ:m.NCOL]).then_inc(s_d.sem, 1)
            dve.wait_ge(s_d.sem, s_d.at(2 * NC2 + 4))
            for c in plus_one:
                last = nc.vector.tensor_scalar(m.mod[:, c:c + 2], m.mod[:, c:c + 2], 1.0, None, ALU.add)
            last.then_inc(s_cols.sem, 1)
            dve.wait_ge(s_gate.sem, s_gate.at(1))
            nc.vector.tensor_tensor(m.gates[:, :, :], ps[:, 3, :].rearrange("p (a b) -> p a b", a=2),
                                    gate_b[:, :, :], ALU.add)
            dve.wait_ge(s_gate.sem, s_gate.at(2))
            nc.vector.tensor_tensor(m.router_bias[:, :], ps[:, 4, 0:NE], rb[:, :], ALU.add).then_inc(s_modv.sem, 1)

        @block.tensor
        def _(pe):
            pe.wait_ge(s_in.sem, s_in.at(32))
            pe.wait_ge(s_load.sem, s_load.at(32))
            turn = 0
            def turn_tiles(src, ready):
                nonlocal turn
                for t4 in range(4):
                    for k in range(KD):
                        if turn >= 4:
                            pe.wait_ge(s_ev.sem, s_ev.at(turn - 3))
                        tiles = range(4 * t4, min(4 * t4 + 4, NC2))
                        if ready:
                            pe.wait_ge(s_n.sem, s_n.at(tiles[-1] + 1))
                        for t in tiles:
                            r = tile_rows(NS2, t)
                            last = pe.transpose(ps[:, 4 + turn % 4, (t % 4) * P:(t % 4) * P + r],
                                                src[0:r, t, k * P:(k + 1) * P], m.ident[0:r, 0:r])
                        last.then_inc(s_tr.sem, 1)
                        turn += 1
            turn_tiles(ct, False)
            pe.wait_ge(s_bc.sem, s_bc.at(1))
            pe.wait_ge(s_w.sem, s_w.at(16 * NLOAD))
            for b in range(NROW):
                for k in range(KD):
                    for j in range(4):
                        w, which, n = chunks[4 * b + j]
                        last = pe.matmul(ps[32 * j:32 * j + 32, b, 0:n], cond_bc[:, which, k, 0:32], w[:, k, 0:n],
                                         start=(k == 0), stop=(k == KD - 1))
            last.then_inc(s_row.sem, 1)
            for i in range(2):
                j = (2, 5)[i]
                for k in range(KD):
                    last = pe.matmul(ps[:, 3, i * D:(i + 1) * D], cond_bc[:, 1, k, :],
                                     adaw[:, k, j * D:(j + 1) * D], start=(k == 0), stop=(k == KD - 1))
            last.then_inc(s_gate.sem, 1)
            pe.wait_ge(s_rowv.sem, s_rowv.at(3))
            for b in range(NROW):
                for q in range(4):
                    r = P if 16 * b + 4 * 3 + q < NJ else 96
                    last = pe.transpose(ps[:, b, q * P:q * P + r], rows[0:r, b, q * P:(q + 1) * P],
                                        m.ident[0:r, 0:r])
            last.then_inc(s_mod.sem, 1)
            turn_tiles(cn, True)
            pe.wait_ge(s_ev.sem, s_ev.at(turn - 3))
            for k in range(KD):
                last = pe.matmul(ps[:, 4, 0:NE], cond_bc[:, 0, k, :], rwc[:, k, :],
                                 start=(k == 0), stop=(k == KD - 1))
            last.then_inc(s_gate.sem, 1)

    for s, k in ((s_in, 32), (s_load, 32), (m.sig["x_in"], 16), (m.sig["x_stats"], NT), (s_w, 16 * NLOAD),
                 (s_cond, 1), (s_bc, 1), (s_row, 1),
                 (s_rowv, 3), (s_mod, 1), (s_gate, 2), (s_modv, 1), (s_cols, 1), (s_st, 1), (s_rs, 1), (s_n, NC2),
                 (s_tr, 16), (s_ev, 16), (s_ones, 1), (s_d, 2 * NC2 + 4), (s_mk, 16), (s_mkd, 6), (s_const, 2),
                 (s_out, 16 * NSTORE)):
        s.advance(k)


def row_statistics(nc, m, dve, final, t):
    s_xs = m.sig["x_stats"]
    if t < NT:
        dve.wait_ge(final.sem, final.at(t + 1))
        nc.vector.bn_stats(m.x_stats[:, t, :], m.x[:, t, :]).then_inc(s_xs.sem, 1)
    if t >= 1:
        dve.wait_ge(s_xs.sem, s_xs.at(t))
        nc.vector.bn_aggr(m.x_mean_var[:, t - 1, :], m.x_stats[:, t - 1, :])


def norm_phase(nc, m, hT, eps, scale, shift, loads):
    s_st, s_rs, s_rec, s_n, s_np, s_tr = (m.sig[n] for n in ("stats", "rstd", "recip", "normed", "normed_pool", "turned"))
    PER = CH // P
    with ExitStack() as ctx:
        m.uid += 1
        sb = lambda n, s, t=F32: ctx.enter_context(nc.sbuf_tensor(f"nm{m.uid}_" + n, s, t))
        var = sb("var", [P, NT])
        std = sb("std", [P, NT])
        rstd = sb("rstd", [P, NT])
        xn = sb("xn", [P, NT, D])
        ps = ctx.enter_context(nc.psum_tensor(f"nm{m.uid}_ps", [P, NCH * KD, CH], F32))
        block = ctx.enter_context(nc.Block())

        @block.sync
        def _(sp):
            for dst, src in loads:
                sp.dma_start(dst, src).then_inc(m.sig["weights"].sem, 16)

        @block.vector
        def _(dve):
            nc.vector.tensor_scalar(var[:, :], m.x_mean_var[:, :, 1], eps, None, ALU.add).then_inc(s_st.sem, 1)
            dve.wait_ge(s_rs.sem, s_rs.at(1))
            nc.vector.reciprocal(rstd[:, :], std[:, :]).then_inc(s_rec.sem, 1)
            dve.wait_ge(s_rec.sem, s_rec.at(1))
            for t in range(NT):
                if t % PER < PER - 1:
                    nc.vector.tensor_scalar(xn[:, t, :], m.x[:, t, :], m.x_mean_var[:, t, 0:1], rstd[:, t:t + 1],
                                            ALU.subtract, ALU.mult).then_inc(s_n.sem, 1)
            for c in range(NCH):
                dve.wait_ge(s_tr.sem, s_tr.at(c * KD + 2))
                src, dst = ps[:, c * KD + 1, :], hT[:, 1, c * CH:(c + 1) * CH]
                if scale is None:
                    nc.vector.tensor_copy(dst, src)
                else:
                    nc.vector.tensor_scalar(dst, src, cols(m.mod, scale + 1), cols(m.mod, shift + 1),
                                            ALU.mult, ALU.add)

        @block.gpsimd
        def _(pool):
            pool.wait_ge(s_rec.sem, s_rec.at(1))
            for t in range(PER - 1, NT, PER):
                nc.gpsimd.tensor_scalar(xn[:, t, :], m.x[:, t, :], m.x_mean_var[:, t, 0:1], rstd[:, t:t + 1],
                                        ALU.subtract, ALU.mult).then_inc(s_np.sem, 1)

        @block.scalar
        def _(act):
            act.wait_ge(s_st.sem, s_st.at(1))
            nc.scalar.activation(std[:, :], var[:, :], ACT.Sqrt).then_inc(s_rs.sem, 1)
            for c in range(NCH):
                act.wait_ge(s_tr.sem, s_tr.at(c * KD + 1))
                src, dst = ps[:, c * KD, :], hT[:, 0, c * CH:(c + 1) * CH]
                if scale is None:
                    nc.scalar.copy(dst, src)
                else:
                    nc.scalar.activation(dst, src, ACT.Identity, scale=cols(m.mod, scale), bias=cols(m.mod, shift))

        @block.tensor
        def _(pe):
            for c in range(NCH):
                pe.wait_ge(s_n.sem, s_n.at((PER - 1) * (c + 1)))
                pe.wait_ge(s_np.sem, s_np.at(c + 1))
                for k in range(KD):
                    for t in range(PER):
                        last = pe.transpose(ps[:, c * KD + k, t * P:(t + 1) * P],
                                            xn[:, PER * c + t, k * P:(k + 1) * P], m.ident[:, :])
                    last.then_inc(s_tr.sem, 1)

    for s, k in ((s_st, 1), (s_rs, 1), (s_rec, 1), (s_n, NCH * (PER - 1)), (s_np, NCH), (s_tr, NCH * KD)):
        s.advance(k)


def load_block(sp, stacked, source, part, c, g, n, signal):
    sp.dma_start(stacked[DH * c:DH * (c + 1), :, 0:n],
                 source[part[c], g * HG * DH:(g + 1) * HG * DH, 0:n].rearrange("(h d) t -> d h t", d=DH)
                 ).then_inc(signal.sem, 16)


def load_group(nc, m, sp, kst, qst, g, nk, signal):
    for c in range(len(Q_PART)):
        load_block(sp, kst, m.k_parts, K_PART, c, g, nk, signal)
        load_block(sp, qst, m.q_parts, Q_PART, c, g, T, signal)


def load_constant_rows(nc, m, sp, kst, qst, nk, masked, signal):
    mask = m.mask_row if masked else m.const_rows
    for dst, src in ((kst[MASK_ROW:MAX_ROW, :, 0:nk], mask[0:1, 0:nk]),
                     (qst[MASK_ROW:MAX_ROW, :, :], m.const_rows[1:2, :]),
                     (kst[MAX_ROW:KROWS, :, 0:nk], m.const_rows[1:KROWS - MASK_ROW, 0:nk])):
        rows, n = src.shape
        sp.dma_start(dst, src.unsqueeze(1).broadcast_to([rows, HG, n])).then_inc(signal.sem, 16)


def projection_phase(nc, m, nload, feature_jobs, token_jobs, rope, operands=None):
    s_w, s_pr, s_tk, s_rot, s_rv, s_f2, s_p1, s_r, s_p2, s_sp, s_d = (
        m.sig[n] for n in ("weights", "proj_ready", "proj_taken", "rot_ready", "rot_taken",
                           "feat_final", "part1", "rest", "part2", "parts_ready", "dve"))
    s_slot = [m.sig[f"stored{i}"] for i in range(4)]
    NF, NJ = len(feature_jobs), len(feature_jobs) + len(token_jobs)
    R = 4
    with ExitStack() as ctx:
        m.uid += 1
        sb = lambda n, s, t=F32: ctx.enter_context(nc.sbuf_tensor(f"pj{m.uid}_" + n, s, t))
        feat = sb("feat", [P, R, CH])
        turned = sb("turned", [P, R, CH])
        final = sb("final", [P, R, CH]) if rope else feat
        rest = sb("rest", [P, R, CH])
        parts = sb("parts", [P, R, PARTS, CH], BF16)
        ps = ctx.enter_context(nc.psum_tensor(f"pj{m.uid}_ps", [P, 4, CH], F32))
        pr = ctx.enter_context(nc.psum_tensor(f"pj{m.uid}_pr", [P, 2, CH], F32))
        block = ctx.enter_context(nc.Block())
        split = [f for f in range(NF) if feature_jobs[f][4] is not None]
        assert not split or split == list(range(NF))
        stored = len(split) > 0

        @block.sync
        def _(sp):
            if stored:
                nk, masked = operands[2:]
                load_constant_rows(nc, m, sp, operands[0], operands[1], nk, masked, m.sig["constants0"])
                reloads = [(operands[0], m.k_parts, K_PART, NF // 4 + 1, NF // 4),
                           (operands[1], m.q_parts, Q_PART, NF // 2 + 1, NF // 2)]
                assert NF // 2 + 1 + len(Q_PART) <= NF
            for f in split:
                n = feature_jobs[f][2]
                sp.wait_ge(s_sp.sem, s_sp.at(f + 1))
                sp.dma_start(feature_jobs[f][4], parts[:, f % R, :, 0:n]).then_inc(s_slot[f % R].sem, 16)
                for stacked, source, part, first, end in reloads:
                    if f == first:
                        for r in range(R):
                            sp.wait_ge(s_slot[r].sem, s_slot[r].at(16 * len(range(r, end, R))))
                    if 0 <= f - first < len(part):
                        load_block(sp, stacked, source, part, f - first, 0, nk if stacked is operands[0] else T,
                                   m.sig["kq0"])
            for r in range(min(R, len(split))):
                sp.wait_ge(s_slot[r].sem, s_slot[r].at(16 * len(range(r, len(split), R))))

        @block.tensor
        def _(pe):
            pe.wait_ge(s_w.sem, s_w.at(16 * nload))

            def rotate(f):
                n = feature_jobs[f][2]
                pe.wait_ge(s_tk.sem, s_tk.at(f + 1))
                pe.wait_ge(s_rv.sem, s_rv.at(f - 1))
                pe.matmul(pr[:, f % 2, 0:n], m.swap[:, :], feat[:, f % R, 0:n], start=True, stop=True
                          ).then_inc(s_rot.sem, 1)

            for i in range(NJ):
                pe.wait_ge(s_tk.sem, s_tk.at(i - 3))
                if i < NF:
                    w, x, n = feature_jobs[i][:3]
                    for k in range(KD):
                        last = pe.matmul(ps[:, i % 4, 0:n], w[k], x[k], start=(k == 0), stop=(k == KD - 1))
                else:
                    x, r, w = token_jobs[i - NF][:3]
                    for k in range(KD):
                        last = pe.matmul(ps[0:r, i % 4, 0:D], x[k], w[k], start=(k == 0), stop=(k == KD - 1))
                last.then_inc(s_pr.sem, 1)
                if rope and 1 <= i:
                    rotate(i - 1)
            if rope:
                rotate(NF - 1)

        whole = s_f2 if rope else s_tk

        def take_feature(engine, f):
            n, bias, _, kept = feature_jobs[f][2:6]
            dst = feat[:, f % R, 0:n] if kept is None else kept
            engine.wait_ge(s_pr.sem, s_pr.at(f + 1))
            if f >= R:
                if rope:
                    engine.wait_ge(s_rot.sem, s_rot.at(f - R + 1))
                    engine.wait_ge(s_d.sem, s_d.at(f - R + 1))
                elif stored:
                    engine.wait_ge(s_p1.sem, s_p1.at(f - R + 1))
                    engine.wait_ge(s_r.sem, s_r.at(f - R + 1))
            if rope:
                op = nc.scalar.copy(dst, ps[:, f % 4, 0:n])
            elif bias is None:
                op = nc.vector.tensor_copy(dst, ps[:, f % 4, 0:n])
            else:
                op = nc.vector.tensor_scalar(dst, ps[:, f % 4, 0:n], cols(m.mod, bias), None, ALU.add)
            op.then_inc(s_tk.sem, 1)

        @block.vector
        def _(dve):
            dve.wait_ge(s_w.sem, s_w.at(16 * nload))

            def times_cos(f):
                n, c0 = feature_jobs[f][2], feature_jobs[f][6]
                dve.wait_ge(s_tk.sem, s_tk.at(f + 1))
                if f >= R:
                    dve.wait_ge(s_p1.sem, s_p1.at(f - R + 1))
                    dve.wait_ge(s_r.sem, s_r.at(f - R + 1))
                nc.vector.tensor_tensor(final[:, f % R, 0:n], feat[:, f % R, 0:n], m.cos[:, c0:c0 + n], ALU.mult
                                        ).then_inc(s_d.sem, 1)

            def rotated(f):
                n, c0 = feature_jobs[f][2], feature_jobs[f][6]
                dve.wait_ge(s_rot.sem, s_rot.at(f + 1))
                nc.vector.tensor_tensor(turned[:, f % R, 0:n], pr[:, f % 2, 0:n], m.sin[:, c0:c0 + n], ALU.mult
                                        ).then_inc(s_rv.sem, 1)
                dve.wait_ge(s_rv.sem, s_rv.at(f + 1))
                dve.wait_ge(s_d.sem, s_d.at(f + 1))
                nc.vector.tensor_tensor(final[:, f % R, 0:n], final[:, f % R, 0:n], turned[:, f % R, 0:n], ALU.add
                                        ).then_inc(s_f2.sem, 1)

            def leave_rest(f):
                n = feature_jobs[f][2]
                dve.wait_ge(s_p1.sem, s_p1.at(f + 1))
                if f >= R:
                    dve.wait_ge(s_sp.sem, s_sp.at(f - R + 1))
                nc.vector.tensor_tensor(rest[:, f % R, 0:n], final[:, f % R, 0:n], parts[:, f % R, 0, 0:n],
                                        ALU.subtract).then_inc(s_r.sem, 1)

            lag = 3 if rope else 1
            for i in range(NF + lag):
                if i < NF:
                    if rope:
                        times_cos(i)
                    else:
                        take_feature(dve, i)
                if rope and 1 <= i <= NF:
                    rotated(i - 1)
                if stored and i >= lag:
                    leave_rest(i - lag)
            for i in range(NF, NJ):
                _, r, _, bias, dst = token_jobs[i - NF]
                dve.wait_ge(s_pr.sem, s_pr.at(i + 1))
                if bias is None:
                    op = nc.vector.tensor_copy(dst, ps[0:r, i % 4, 0:D])
                else:
                    op = nc.vector.tensor_tensor(dst, ps[0:r, i % 4, 0:D], bias[0:r, :], ALU.add)
                op.then_inc(s_tk.sem, 1)

        @block.scalar
        def _(act):
            def first_part(f):
                n = feature_jobs[f][2]
                act.wait_ge(whole.sem, whole.at(f + 1))
                if f >= R:
                    act.wait_ge(s_slot[f % R].sem, s_slot[f % R].at(16 * (f // R)))
                nc.scalar.copy(parts[:, f % R, 0, 0:n], final[:, f % R, 0:n]).then_inc(s_p1.sem, 1)

            def second_part(f):
                n = feature_jobs[f][2]
                act.wait_ge(s_r.sem, s_r.at(f + 1))
                nc.scalar.copy(parts[:, f % R, 1, 0:n], rest[:, f % R, 0:n]).then_inc(s_p2.sem, 1)

            lag = (2, 4) if rope else (0, 1)
            for i in range(NF + lag[1]):
                if rope and i < NF:
                    take_feature(act, i)
                if stored and 0 <= i - lag[0] < NF:
                    first_part(i - lag[0])
                if stored and 0 <= i - lag[1]:
                    second_part(i - lag[1])

        @block.gpsimd
        def _(pool):
            for f in split:
                n = feature_jobs[f][2]
                pool.wait_ge(s_p2.sem, s_p2.at(f + 1))
                nc.gpsimd.tensor_tensor(parts[:, f % R, 2, 0:n], rest[:, f % R, 0:n], parts[:, f % R, 1, 0:n],
                                        ALU.subtract).then_inc(s_sp.sem, 1)

    s_w.advance(16 * nload)
    for s in (s_pr, s_tk):
        s.advance(NJ)
    if rope:
        for s in (s_rot, s_rv, s_f2, s_d):
            s.advance(NF)
    if stored:
        for s in (s_p1, s_r, s_p2, s_sp):
            s.advance(NF)
        for r in range(R):
            s_slot[r].advance(16 * len(range(r, NF, R)))


def piece_width(nk):
    return -(-nk // -(-nk // CH))


def max_pieces(nk, items, bank, turn_after):
    out = []
    width = piece_width(nk)
    for it in items:
        for key in range(0, nk, width):
            out.append(((it, key, min(width, nk - key)), bank))
            bank = (bank + 1) % 3
            if len(out) == turn_after:
                out.append(("turn", bank))
                bank = (bank + 1) % 3
    return out, bank


def attention_phase(nc, m, nk, masked, values, first_operands):
    v_src, vw, vb = values
    s_kq = [m.sig["kq0"], m.sig["kq1"]]
    s_st, s_p, s_av, s_acc, s_mx, s_mt, s_nm, s_m1, s_mr, s_m2, s_ones, s_ms, s_mo, s_mi, s_v = (
        m.sig[n] for n in ("scores_ready", "probs_ready", "av_done", "acc_saved", "max_ready", "max_taken",
                           "maxes_ready", "m_part1", "m_rest", "m_part2", "ones_set", "m_parts",
                           "m_out", "m_in", "v_staged"))
    s_init = [m.sig["constants0"], m.sig["constants1"]]
    s_pr, s_tk, s_vb = (m.sig[n] for n in ("proj_ready", "proj_taken", "v_biased"))
    KT = -(-nk // P)
    items = HG * (CH // P)
    NP = -(-nk // CH)
    LEAD = 4
    this = [(0, q) for q in range(LEAD, items)]
    ahead = [(1, q) for q in range(LEAD)]
    TURN_AT = len(this) * NP + 3
    full, end = max_pieces(nk, this + ahead, 0, TURN_AT)
    skip = -end % 3
    first_items = [(0, q) for q in range(items)] + ahead
    first, end = max_pieces(nk, first_items, -(len(first_items) * NP + 1 + skip) % 3, items * NP + 3)
    assert (end + skip) % 3 == 0 and [x[1:] for x in first[-6:]] == [x[1:] for x in full[-6:]]
    short, _ = max_pieces(nk, this, 0, len(this) * NP)

    def with_needs(stream):
        last = {b: q + 1 - len(full) for q, (_, b) in enumerate(full)}
        out = []
        for q, (piece, b) in enumerate(stream):
            out.append((piece, b, last[b]))
            last[b] = q + 1
        return out

    NFIRST, NFULL, NSHORT = len(first), len(full), len(short)
    streams = {"first": [x[:2] + (max(x[2], 0),) for x in with_needs(first)], "full": with_needs(full),
               "short": with_needs(short), "none": []}
    UB = 2 * NCH
    NU = NG * NCH
    NB = NU // UB
    assert NB == 2
    HELD = 2

    with ExitStack() as ctx:
        m.uid += 1
        sb = lambda n, s, t=F32: ctx.enter_context(nc.sbuf_tensor(f"at{m.uid}_" + n, s, t))
        kst = [first_operands[0], sb("kst", [P, HG, T], BF16)]
        qst = [first_operands[1], sb("qst", [P, HG, T], BF16)]
        probs = sb("probs", [P, 2, HG, CH])
        vst = sb("vst", [P, 2, NT, HG, 2 * DH])
        mpart = sb("mpart", [P, 2, items, NP])
        mmax = sb("mmax", [P, 2, items])
        neg = sb("neg", [items, P])
        mrest = sb("mrest", [items, P])
        zero = sb("zero", [items, P])
        mparts = sb("mparts", [items, PARTS, P], BF16)
        scores = ctx.enter_context(nc.psum_tensor(f"at{m.uid}_scores", [P, 4, CH], F32))
        acc = ctx.enter_context(nc.psum_tensor(f"at{m.uid}_acc", [P, CH], F32))
        mxp = ctx.enter_context(nc.psum_tensor(f"at{m.uid}_mxp", [P, 3, CH], F32))
        block = ctx.enter_context(nc.Block())

        def taken_before(U):
            return NFIRST + U * NFULL

        @block.sync
        def _(sp):
            def spread_max(par, c, n):
                sp.wait_ge(s_ms.sem, s_ms.at(n + 1))
                sp.dma_start(m.m_scratch.rearrange("a i q -> i a q"), mparts[:, :, :]).then_inc(s_mo.sem, 16)
                sp.wait_ge(s_mo.sem, s_mo.at(16 * (n + 1)))
                sp.dma_start(qst[par][MAX_ROW:MAX_ROW + PARTS, :, c * CH:(c + 1) * CH],
                             m.m_scratch.rearrange("a (h i) q -> a h (i q)", h=HG)).then_inc(s_mi.sem, 16)

            load_constant_rows(nc, m, sp, kst[1], qst[1], nk, masked, s_init[1])
            spread_max(0, 0, 0)
            with sp.Fori(0, NB) as i:
                for u in range(UB):
                    U = i * UB + u
                    if u == 0:
                        with sp.If(i < NB - 1):
                            load_group(nc, m, sp, kst[1], qst[1], 1, nk, s_kq[1])
                        with sp.Else():
                            sp.wait_ge(s_st.sem, s_st.at(U * 2 * KT))
                            load_group(nc, m, sp, kst[1], qst[1], 3, nk, s_kq[1])
                    if u == NCH:
                        with sp.If(i < NB - 1):
                            sp.wait_ge(s_st.sem, s_st.at(U * 2 * KT))
                            load_group(nc, m, sp, kst[0], qst[0], 2, nk, s_kq[0])
                    nxt = (u + 1) % UB
                    if u < UB - 1:
                        spread_max(nxt // NCH, nxt % NCH, U + 1)
                    else:
                        with sp.If(i < NB - 1):
                            spread_max(0, 0, U + 1)
            sp.wait_ge(s_mi.sem, s_mi.at(16 * NU))

        @block.tensor
        def _(pe):
            def take_pieces(stream, lo, hi, before, unit_of, turned):
                for piece, b, need in streams[stream][lo:hi]:
                    pe.wait_ge(s_mt.sem, s_mt.at(before + need))
                    if piece == "turn":
                        pe.wait_ge(s_nm.sem, s_nm.at(turned[1]))
                        last = pe.transpose(mxp[0:items, b, 0:P], mmax[:, turned[0], :], m.ident[:, :])
                    else:
                        (which, q), key, n = piece
                        par, c = unit_of[which]
                        h, qt = divmod(q, CH // P)
                        last = pe.matmul(mxp[:, b, 0:n],
                                         qst[par][0:MAX_ROW, h, c * CH + qt * P:c * CH + (qt + 1) * P],
                                         kst[par][0:MAX_ROW, h, key:key + n], start=True, stop=True)
                    last.then_inc(s_mx.sem, 1)

            def unit(i, u, stream):
                U = i * UB + u
                par, c = divmod(u, NCH)
                total = len(streams[stream])
                unit_of = [divmod((u + x) % UB, NCH) for x in (1, 2)]
                done = [0]

                def some(upto):
                    if done[0] <= AHEAD_AT < upto and (u + 2) % NCH == 0 and stream == "full":
                        tpar = unit_of[1][0]
                        take_pieces(stream, done[0], AHEAD_AT, taken_before(U), unit_of, ((u + 1) % 2, U + 2))
                        done[0] = AHEAD_AT
                        pe.wait_ge(s_kq[tpar].sem, s_kq[tpar].at(KQ * (i + 1) + (KQ if tpar == 0 else 0)))
                    take_pieces(stream, done[0], upto, taken_before(U), unit_of, ((u + 1) % 2, U + 2))
                    done[0] = upto

                def weigh(s):
                    pe.wait_ge(s_p.sem, s_p.at((U * KT + s) * 2 + 2))
                    if s == 0:
                        pe.wait_ge(s_acc.sem, s_acc.at(U))
                    r = tile_rows(nk, s)
                    for j in range(HG):
                        last = pe.matmul(acc[32 * j:32 * j + 2 * DH, :], vst[0:r, par, s, j, :],
                                         probs[0:r, s % 2, j, :], start=(s == 0), stop=(s == KT - 1))
                    last.then_inc(s_av.sem, 1)

                pe.wait_ge(s_mi.sem, s_mi.at(16 * (U + 1)))
                if u % NCH == 0:
                    pe.wait_ge(s_v.sem, s_v.at(1 + i * 2 + u // NCH))
                held = HELD if total > HELD else 0
                slots, at = (HG + 1) * KT, 0
                for s in range(KT):
                    r = tile_rows(nk, s)
                    for j in range(HG):
                        at += 1
                        some((total - held) * at // slots)
                        if j % 2 == 0:
                            pe.wait_ge(s_p.sem, s_p.at((U * KT + s) * 2 + j // 2 - 1))
                        last = pe.matmul(scores[0:r, j, :], kst[par][0:KROWS, j, s * P:s * P + r],
                                         qst[par][0:KROWS, j, c * CH:(c + 1) * CH], start=True, stop=True)
                        if j % 2:
                            last.then_inc(s_st.sem, 1)
                    at += 1
                    some((total - held) * at // slots)
                    if s:
                        weigh(s - 1)
                some(total)
                weigh(KT - 1)

            AHEAD_AT = [n for n, (pc, _) in enumerate(full) if pc != "turn" and pc[0][0] == 1][0]
            def project_v(t):
                pe.wait_ge(s_tk.sem, s_tk.at(t - 3))
                r = tile_rows(nk, t)
                for k in range(KD):
                    last = pe.matmul(scores[0:r, t % 4, 0:D], v_src[:, k, t * P:t * P + r], vw[:, k, :],
                                     start=(k == 0), stop=(k == KD - 1))
                last.then_inc(s_pr.sem, 1)

            pe.wait_ge(s_init[0].sem, s_init[0].at(NCONST))
            pe.wait_ge(s_kq[0].sem, s_kq[0].at(KQ))
            t = 0
            for q in range(NFIRST):
                take_pieces("first", q, q + 1, 0, [(0, 0), (0, 1)], (0, 1))
                if q % 3 == 2 and t < KT:
                    project_v(t)
                    t += 1
            assert t == KT
            pe.wait_ge(s_tk.sem, s_tk.at(KT))
            pe.wait_ge(s_init[1].sem, s_init[1].at(NCONST))
            with pe.Fori(0, NB) as i:
                for u in range(UB - 2):
                    unit(i, u, "full")
                with pe.If(i < NB - 1):
                    unit(i, UB - 2, "full")
                    unit(i, UB - 1, "full")
                with pe.Else():
                    unit(i, UB - 2, "short")
                    unit(i, UB - 1, "none")

        @block.scalar
        def _(act):
            for t in range(KT):
                r = tile_rows(nk, t)
                act.wait_ge(s_pr.sem, s_pr.at(t + 1))
                nc.scalar.copy(m.v[0:r, t, :], scores[0:r, t % 4, 0:D]).then_inc(s_tk.sem, 1)
            with act.Fori(0, NB) as i:
                for u in range(UB):
                    U = i * UB + u
                    g, c = divmod(u, NCH)
                    for s in range(KT):
                        r = tile_rows(nk, s)
                        act.wait_ge(s_av.sem, s_av.at(U * KT + s - 1))
                        for half in range(2):
                            act.wait_ge(s_st.sem, s_st.at((U * KT + s) * 2 + half + 1))
                            nc.scalar.activation(probs[0:r, s % 2, 2 * half:2 * half + 2, :],
                                                 scores[0:r, 2 * half:2 * half + 2, :], ACT.Exp,
                                                 scale=1.0 / DH ** 0.5).then_inc(s_p.sem, 1)
                    act.wait_ge(s_av.sem, s_av.at((U + 1) * KT))
                    nc.scalar.copy(m.attn[:, bass.ds((i * 2 + g) * T + c * CH, CH)], acc[:, :]
                                   ).then_inc(s_acc.sem, 1)

        @block.vector
        def _(dve):
            def take(stream, before, next_unit, slot):
                for q, (piece, b, _) in enumerate(streams[stream]):
                    if piece == "turn":
                        dve.wait_ge(s_m1.sem, s_m1.at(next_unit))
                        dve.wait_ge(s_mr.sem, s_mr.at(next_unit))
                        dve.wait_ge(s_mx.sem, s_mx.at(before + q + 1))
                        nc.vector.tensor_scalar(neg[:, :], mxp[0:items, b, 0:P], -1.0, None, ALU.mult
                                                ).then_inc(s_mt.sem, 1)
                        continue
                    (which, item), key, n = piece
                    if item == 0 and key == 0 and which == 1:
                        dve.wait_ge(s_nm.sem, s_nm.at(next_unit))
                    dve.wait_ge(s_mx.sem, s_mx.at(before + q + 1))
                    part = key // piece_width(nk)
                    nc.vector.reduce_max(mpart[:, (slot + which) % 2, item, part:part + 1], mxp[:, b, 0:n], AX
                                         ).then_inc(s_mt.sem, 1)
                    if which == 0 and item == items - 1 and key + n == nk:
                        dve.wait_ge(s_mt.sem, s_mt.at(before + q + 1))
                        nc.vector.reduce_max(mmax[:, slot, :], mpart[:, slot, :, :], AX).then_inc(s_nm.sem, 1)

            take("first", 0, 0, 0)
            with dve.Fori(0, NB) as i:
                for u in range(UB - 2):
                    take("full", taken_before(i * UB + u), i * UB + u + 1, (u + 1) % 2)
                with dve.If(i < NB - 1):
                    for u in (UB - 2, UB - 1):
                        take("full", taken_before(i * UB + u), i * UB + u + 1, (u + 1) % 2)
                with dve.Else():
                    take("short", taken_before(i * UB + UB - 2), i * UB + UB - 1, 1)

        @block.gpsimd
        def _(pool):
            def stage_v(par, g):
                whole = nk // P
                for kt in range(0, whole, 4):
                    e = min(kt + 4, whole)
                    last = nc.gpsimd.tensor_copy(vst[:, par, kt:e, :, 0:DH],
                                                 m.v[:, kt:e, bass.ds(g * HG * DH, HG * DH)].rearrange(
                                                     "p t (h e) -> p t h e", e=DH))
                if nk % P:
                    r = nk % P
                    last = nc.gpsimd.tensor_copy(vst[0:r, par, whole, :, 0:DH],
                                                 m.v[0:r, whole, bass.ds(g * HG * DH, HG * DH)].rearrange(
                                                     "p (h e) -> p h e", e=DH))
                last.then_inc(s_v.sem, 1)

            def cut_max(turn_at, n):
                pool.wait_ge(s_mt.sem, s_mt.at(turn_at))
                pool.wait_ge(s_mo.sem, s_mo.at(16 * n))
                pool.wait_ge(s_mi.sem, s_mi.at(16 * n))
                nc.gpsimd.tensor_tensor(mparts[:, 0, :], neg[:, :], zero[:, :], ALU.add).then_inc(s_m1.sem, 1)
                pool.wait_ge(s_m1.sem, s_m1.at(n + 1))
                nc.gpsimd.tensor_tensor(mrest[:, :], neg[:, :], mparts[:, 0, :], ALU.subtract).then_inc(s_mr.sem, 1)
                pool.wait_ge(s_mr.sem, s_mr.at(n + 1))
                nc.gpsimd.tensor_tensor(mparts[:, 1, :], mrest[:, :], zero[:, :], ALU.add).then_inc(s_m2.sem, 1)
                pool.wait_ge(s_m2.sem, s_m2.at(n + 1))
                nc.gpsimd.tensor_tensor(mparts[:, 2, :], mrest[:, :], mparts[:, 1, :], ALU.subtract
                                        ).then_inc(s_ms.sem, 1)

            nc.gpsimd.memset(zero[:, :], 0.0)
            nc.gpsimd.memset(vst[:, :, :, :, :], 1.0).then_inc(s_ones.sem, 1)
            pool.wait_ge(s_ones.sem, s_ones.at(1))
            if vb is None:
                pool.wait_ge(s_tk.sem, s_tk.at(KT))
            else:
                for t in range(KT):
                    r = tile_rows(nk, t)
                    pool.wait_ge(s_tk.sem, s_tk.at(t + 1))
                    nc.gpsimd.tensor_tensor(m.v[0:r, t, :], m.v[0:r, t, :], vb[0:r, :], ALU.add
                                            ).then_inc(s_vb.sem, 1)
                pool.wait_ge(s_vb.sem, s_vb.at(KT))
            stage_v(0, 0)
            cut_max(items * NP + 3 + 1, 0)
            with pool.Fori(0, NB) as i:
                for u in range(UB):
                    U = i * UB + u
                    if u == 0:
                        pool.wait_ge(s_av.sem, s_av.at(U * KT))
                        stage_v(1, i * 2 + 1)
                    if u == NCH:
                        with pool.If(i < NB - 1):
                            pool.wait_ge(s_av.sem, s_av.at(U * KT))
                            stage_v(0, i + 2)   
                    if u < UB - 2:
                        cut_max(taken_before(U) + TURN_AT + 1, U + 1)
                with pool.If(i < NB - 1):
                    for u in (UB - 2, UB - 1):
                        U = i * UB + u
                        cut_max(taken_before(U) + TURN_AT + 1, U + 1)
                with pool.Else():
                    cut_max(taken_before(i * UB + UB - 2) + NSHORT, i * UB + UB - 1)

    s_kq[0].advance(2 * KQ)
    s_kq[1].advance(2 * KQ)
    s_st.advance(NU * 2 * KT)
    s_p.advance(NU * 2 * KT)
    s_av.advance(NU * KT)
    s_acc.advance(NU)
    for s in (s_mx, s_mt):
        s.advance(taken_before(NU - 2) + NSHORT)
    for s in (s_nm, s_m1, s_mr, s_m2, s_ms):
        s.advance(NU)
    for s in s_init:
        s.advance(NCONST)
    s_ones.advance(1)
    s_mo.advance(16 * NU)
    s_mi.advance(16 * NU)
    s_v.advance(NG)
    s_pr.advance(KT)
    s_tk.advance(KT)
    if vb is not None:
        s_vb.advance(KT)


def output_phase(nc, m, weight, bias, gate, extra=None):
    s_w, s_o, s_rd, s_a, s_at, s_as, s_y, s_x, s_wf, s_xb = (
        m.sig[n] for n in ("weights", "o_turned", "recip", "normalised", "a_turned", "a_saved", "y_ready",
                           "x_added", "w_folded", "x_biased"))
    nload = 1 + (bias is not None)
    with ExitStack() as ctx:
        m.uid += 1
        sb = lambda n, s, t=F32: ctx.enter_context(nc.sbuf_tensor(f"op{m.uid}_" + n, s, t))
        w = sb("w", [P, KD, D])
        bb = sb("bb", [P, D])
        rd = sb("rd", [P, 2, NH])
        a = sb("a", [P, 2, NH, DH])
        aT = sb("aT", [P, 2, KD, P])
        po = ctx.enter_context(nc.psum_tensor(f"op{m.uid}_po", [P, 2, CH], F32))
        pt = ctx.enter_context(nc.psum_tensor(f"op{m.uid}_pt", [P, 2, CH], F32))
        py = ctx.enter_context(nc.psum_tensor(f"op{m.uid}_py", [P, 2, CH], F32))
        block = ctx.enter_context(nc.Block())

        @block.sync
        def _(sp):
            sp.dma_start(w[:, :, :], weight.rearrange("(k p) n -> p k n", p=P)).then_inc(s_w.sem, 16)
            if bias is not None:
                sp.dma_start(bb[:, :], bias.partition_broadcast(P)).then_inc(s_w.sem, 16)

        @block.gpsimd
        def _(pool):
            pool.wait_ge(s_w.sem, s_w.at(16 * nload))
            if gate is not None:
                for k in range(KD):
                    last = nc.gpsimd.tensor_tensor(w[:, k, :], w[:, k, :], m.gates[:, gate, :], ALU.mult)
                last.then_inc(s_wf.sem, 1)
                nc.gpsimd.tensor_tensor(bb[:, :], bb[:, :], m.gates[:, gate, :], ALU.mult).then_inc(s_wf.sem, 1)
                pool.wait_ge(s_wf.sem, s_wf.at(2))
            if extra is not None:
                nc.gpsimd.tensor_scalar(bb[:, :], bb[:, :], extra[:, :], None, ALU.add).then_inc(s_wf.sem, 1)
                pool.wait_ge(s_wf.sem, s_wf.at(1))
            if bias is not None:
                for t in range(NT):
                    nc.gpsimd.tensor_tensor(m.x[:, t, :], m.x[:, t, :], bb[:, :], ALU.add).then_inc(s_xb.sem, 1)

        @block.tensor
        def _(pe):
            def open_heads(t):
                pe.wait_ge(s_a.sem, s_a.at(t - 1))
                for g in range(NG):
                    last = pe.transpose(po[:, t % 2, g * P:(g + 1) * P],
                                        m.attn[:, g * T + t * P:g * T + (t + 1) * P], m.ident[:, :])
                last.then_inc(s_o.sem, 1)

            def turn_back(t):
                pe.wait_ge(s_a.sem, s_a.at(t + 1))
                pe.wait_ge(s_as.sem, s_as.at(t - 1))
                for k in range(KD):
                    last = pe.transpose(pt[:, t % 2, k * P:(k + 1) * P],
                                        a[:, t % 2, k * (NH // KD):(k + 1) * (NH // KD), :].rearrange(
                                            "p h e -> p (h e)"), m.ident[:, :])
                last.then_inc(s_at.sem, 1)

            def project(t):
                pe.wait_ge(s_as.sem, s_as.at(t + 1))
                pe.wait_ge(s_x.sem, s_x.at(t - 1))
                for k in range(KD):
                    last = pe.matmul(py[:, t % 2, 0:D], aT[:, t % 2, k, :], w[:, k, :],
                                     start=(k == 0), stop=(k == KD - 1))
                last.then_inc(s_y.sem, 1)

            for t in range(NT + 2):
                if t < NT:
                    open_heads(t)
                if 1 <= t <= NT:
                    turn_back(t - 1)
                if t == 2:
                    pe.wait_ge(s_w.sem, s_w.at(16 * nload))
                    if gate is not None:
                        pe.wait_ge(s_wf.sem, s_wf.at(2))
                if t >= 2:
                    project(t - 2)

        @block.scalar
        def _(act):
            for t in range(NT):
                act.wait_ge(s_at.sem, s_at.at(t + 1))
                act.wait_ge(s_y.sem, s_y.at(t - 1))
                nc.scalar.copy(aT[:, t % 2, :, :].rearrange("p k n -> p (k n)"), pt[:, t % 2, 0:D]
                               ).then_inc(s_as.sem, 1)

        @block.vector
        def _(dve):
            for t in range(NT + 2):
                if t < NT:
                    heads = po[:, t % 2, :].rearrange("p (h e) -> p h e", e=2 * DH)
                    dve.wait_ge(s_o.sem, s_o.at(t + 1))
                    nc.vector.reciprocal(rd[:, t % 2, :], heads[:, :, DH]).then_inc(s_rd.sem, 1)
                    dve.wait_ge(s_rd.sem, s_rd.at(t + 1))
                    dve.wait_ge(s_at.sem, s_at.at(t - 1))
                    nc.vector.tensor_tensor(a[:, t % 2, :, :], heads[:, :, 0:DH],
                                            rd[:, t % 2, :].unsqueeze(2).broadcast_to([P, NH, DH]), ALU.mult
                                            ).then_inc(s_a.sem, 1)
                if t >= 2:
                    y = t - 2
                    dve.wait_ge(s_y.sem, s_y.at(y + 1))
                    if bias is not None:
                        dve.wait_ge(s_xb.sem, s_xb.at(y + 1))
                    nc.vector.tensor_tensor(m.x[:, y, :], py[:, y % 2, 0:D], m.x[:, y, :], ALU.add
                                            ).then_inc(s_x.sem, 1)
                if t >= 3:
                    row_statistics(nc, m, dve, s_x, t - 3)
            for t in (NT - 1, NT):
                row_statistics(nc, m, dve, s_x, t)

    s_w.advance(16 * nload)
    for s in (s_o, s_rd, s_a, s_at, s_as, s_y, s_x, m.sig["x_stats"]):
        s.advance(NT)
    if gate is not None:
        s_wf.advance(2)
    if extra is not None:
        s_wf.advance(1)
    if bias is not None:
        s_xb.advance(NT)


def ffn_phase(nc, m, hT, norm, w1, b1_col, w2, b2, gate, out):
    s_w, s_u, s_g, s_hh, s_hl, s_ud, s_x, s_wf, s_xb, s_out = (m.sig[n] for n in (
        "weights", "up_ready", "gelu_ready", "hid_high", "hid_low", "down_done", "x_added", "w_folded",
        "x_biased", "stored0"))
    s_h1, s_h2, s_w1h, s_w1l, s_w2h, s_w2l = (m.sig[n] for n in (
        "h_high", "h_low", "w1_high", "w1_low", "w2_high", "w2_low"))
    NF = FF // P
    NI = NCH * NF
    RU, RG, LAG = 4, 4, 3
    PER = CH // P
    WB = FF // CH
    PASSES = ((0, 0), (1, 0), (0, 1))
    with ExitStack() as ctx:
        m.uid += 1
        sb = lambda n, s, t=F32: ctx.enter_context(nc.sbuf_tensor(f"ff{m.uid}_" + n, s, t))
        w1s = sb("w1", [P, KD, FF])
        w2s = sb("w2", [P, NF, D])
        bb = sb("bb", [P, D])
        norm_phase(nc, m, hT, *norm, [(w1s[:, :, :], w1.rearrange("(k p) n -> p k n", p=P)),
                                      (w2s[:, :, :], w2.rearrange("(k p) n -> p k n", p=P)),
                                      (bb[:, :], b2.partition_broadcast(P))])
        m.uid += 1
        h2 = [sb(n, [P, KD, T], F32R) for n in ("h_high", "h_low")]
        w1r = [sb(n, [P, KD, FF], F32R) for n in ("w1_high", "w1_low")]
        w2r = [sb(n, [P, NF, D], F32R) for n in ("w2_high", "w2_low")]
        hid = sb("hid", [P, RG, CH])
        hr = [sb(n, [P, RG, CH], F32R) for n in ("hid_high", "hid_low")]
        pu = ctx.enter_context(nc.psum_tensor(f"ff{m.uid}_pu", [P, RU, CH], F32))
        py = ctx.enter_context(nc.psum_tensor(f"ff{m.uid}_py", [P, 2, PER, D], F32))
        block = ctx.enter_context(nc.Block())
        w1_block = lambda t, b: t[:, :, b * CH:(b + 1) * CH]
        w2_block = lambda t, b: t[:, 4 * b:4 * b + 4, :]

        @block.sync
        def _(sp):
            if out is not None:
                for c in range(NCH):
                    sp.wait_ge(s_x.sem, s_x.at(4 * c + 4))
                    sp.dma_start(out[c * CH:(c + 1) * CH, :].rearrange("(t p) n -> p t n", p=P),
                                 m.x[:, 4 * c:4 * c + 4, :]).then_inc(s_out.sem, 16)
                sp.wait_ge(s_out.sem, s_out.at(16 * NCH))

        @block.gpsimd
        def _(pool):
            pool.wait_ge(s_w.sem, s_w.at(48))
            if gate is not None:
                for k in range(NF):
                    last = nc.gpsimd.tensor_tensor(w2s[:, k, :], w2s[:, k, :], m.gates[:, gate, :], ALU.mult)
                last.then_inc(s_wf.sem, 1)
                nc.gpsimd.tensor_tensor(bb[:, :], bb[:, :], m.gates[:, gate, :], ALU.mult).then_inc(s_wf.sem, 1)
                pool.wait_ge(s_wf.sem, s_wf.at(2))
            for t in range(NT):
                nc.gpsimd.tensor_tensor(m.x[:, t, :], m.x[:, t, :], bb[:, :], ALU.add).then_inc(s_xb.sem, 1)

        @block.tensor
        def _(pe):
            def up(i):
                c, f = divmod(i, NF)
                pe.wait_ge(s_g.sem, s_g.at(i - RU + 1))
                if f == 0:
                    pe.wait_ge(s_h2.sem, s_h2.at(c + 1))
                if c == 0:
                    pe.wait_ge(s_w1l.sem, s_w1l.at(f * P // CH + 1))
                n = 0
                for k in range(KD):
                    for a, b in PASSES:
                        last = pe.matmul(pu[:, i % RU, :], w1r[a][:, k, f * P:(f + 1) * P],
                                         h2[b][:, k, c * CH:(c + 1) * CH], start=(n == 0), stop=(n == 3 * KD - 1))
                        n += 1
                last.then_inc(s_u.sem, 1)

            def down(i):
                c, f = divmod(i, NF)
                pe.wait_ge(s_hl.sem, s_hl.at(i + 1))
                if c == 0:
                    pe.wait_ge(s_w2l.sem, s_w2l.at(f // 4 + 1))
                if f == 0 and c >= 2:
                    pe.wait_ge(s_x.sem, s_x.at(PER * (c - 1)))
                for q in range(PER):
                    for n, (a, b) in enumerate(PASSES):
                        last = pe.matmul(py[:, c % 2, q, :], hr[a][:, i % RG, q * P:(q + 1) * P], w2r[b][:, f, :],
                                         start=(f == 0 and n == 0 and q % 2 == 0),
                                         stop=(f == NF - 1 and n == 2 and q % 2 == 1))
                last.then_inc(s_ud.sem, 1)

            for i in range(NI + LAG):
                if i < NI:
                    up(i)
                if i >= LAG:
                    down(i - LAG)

        @block.scalar
        def _(act):
            def cut_w2(b):
                if gate is not None:
                    act.wait_ge(s_wf.sem, s_wf.at(1))
                nc.scalar.copy(w2_block(w2r[0], b), w2_block(w2s, b)).then_inc(s_w2h.sem, 1)

            act.wait_ge(s_w.sem, s_w.at(48))
            for b in range(WB):
                nc.scalar.copy(w1_block(w1r[0], b), w1_block(w1s, b)).then_inc(s_w1h.sem, 1)
            for i in range(NI + 1):
                if i < NI:
                    c, f = divmod(i, NF)
                    act.wait_ge(s_u.sem, s_u.at(i + 1))
                    act.wait_ge(s_hl.sem, s_hl.at(i - RG + 1))
                    nc.scalar.activation(hid[:, i % RG, :], pu[:, i % RU, :], ACT.Gelu, bias=cols(m.mod, b1_col + f)
                                         ).then_inc(s_g.sem, 1)
                if i in (0, 3):
                    cut_w2(i // 3)
                if i >= 1:
                    act.wait_ge(s_g.sem, s_g.at(i))
                    act.wait_ge(s_ud.sem, s_ud.at(i - RG))
                    nc.scalar.copy(hr[0][:, (i - 1) % RG, :], hid[:, (i - 1) % RG, :]).then_inc(s_hh.sem, 1)

        @block.vector
        def _(dve):
            def cut_h(c):
                x = slice(c * CH, (c + 1) * CH)
                nc.vector.tensor_copy(h2[0][:, :, x], hT[:, :, x]).then_inc(s_h1.sem, 1)
                dve.wait_ge(s_h1.sem, s_h1.at(c + 1))
                nc.vector.tensor_tensor(h2[1][:, :, x], hT[:, :, x], h2[0][:, :, x].bitcast(F32), ALU.subtract
                                        ).then_inc(s_h2.sem, 1)

            def cut_hid(i):
                dve.wait_ge(s_hh.sem, s_hh.at(i + 1))
                nc.vector.tensor_tensor(hr[1][:, i % RG, :], hid[:, i % RG, :], hr[0][:, i % RG, :].bitcast(F32),
                                        ALU.subtract).then_inc(s_hl.sem, 1)

            def add(t):
                c, q = divmod(t, PER)
                dve.wait_ge(s_ud.sem, s_ud.at((c + 1) * NF))
                dve.wait_ge(s_xb.sem, s_xb.at(t + 1))
                nc.vector.tensor_tensor(m.x[:, t, :], py[:, c % 2, q, :], m.x[:, t, :], ALU.add).then_inc(s_x.sem, 1)
                if out is None:
                    row_statistics(nc, m, dve, s_x, t)

            cut_h(0)
            for b in range(WB):
                dve.wait_ge(s_w1h.sem, s_w1h.at(b + 1))
                nc.vector.tensor_tensor(w1_block(w1r[1], b), w1_block(w1s, b), w1_block(w1r[0], b).bitcast(F32),
                                        ALU.subtract).then_inc(s_w1l.sem, 1)
            for i in range(NI):
                if i in (1, 4):
                    dve.wait_ge(s_w2h.sem, s_w2h.at(i // 3 + 1))
                    nc.vector.tensor_tensor(w2_block(w2r[1], i // 3), w2_block(w2s, i // 3),
                                            w2_block(w2r[0], i // 3).bitcast(F32), ALU.subtract
                                            ).then_inc(s_w2l.sem, 1)
                cut_hid(i)
                c, f = divmod(i, NF)
                if f == 5 and c + 1 < NCH:
                    cut_h(c + 1)
                if c and f >= LAG and f - LAG < PER:
                    add(PER * (c - 1) + f - LAG)
            for t in range(NT - PER, NT):
                add(t)
            if out is None:
                row_statistics(nc, m, dve, s_x, NT)

    s_w.advance(48)
    for s in (s_u, s_g, s_hh, s_hl, s_ud):
        s.advance(NI)
    for s in (s_h1, s_h2):
        s.advance(NCH)
    for s in (s_w1h, s_w1l, s_w2h, s_w2l):
        s.advance(WB)
    for s in (s_x, s_xb):
        s.advance(NT)
    if gate is not None:
        s_wf.advance(2)
    if out is not None:
        s_out.advance(16 * NCH)
    else:
        m.sig["x_stats"].advance(NT)


def evidence_phase(nc, m, qT, kT, evT):
    s_sc, s_mx, s_nb, s_e, s_rd, s_pn, s_tr, s_ts, s_ev, s_es = (m.sig[n] for n in (
        "scores_ready", "max_ready", "neg_ready", "probs_ready", "recip", "normalised", "turned", "turn_saved",
        "av_done", "acc_saved"))
    GROUPS = [(g, min(g + 4, NC2)) for g in range(0, NC2, 4)]
    NGR = len(GROUPS)
    SC = 1.0 / D ** 0.5
    with ExitStack() as ctx:
        m.uid += 1
        sb = lambda n, s, t=F32: ctx.enter_context(nc.sbuf_tensor(f"ev{m.uid}_" + n, s, t))
        probs = sb("probs", [P, 2, NS2])
        probsT = sb("probsT", [P, 2, NC2, CH])
        mx = sb("mx", [P, NT])
        nb = sb("nb", [P, NT])
        den = sb("den", [P, NT])
        rden = sb("rden", [P, NT])
        ps = ctx.enter_context(nc.psum_tensor(f"ev{m.uid}_ps", [P, 4, CH], F32))
        pt = ctx.enter_context(nc.psum_tensor(f"ev{m.uid}_pt", [P, 2, CH], F32))
        po = ctx.enter_context(nc.psum_tensor(f"ev{m.uid}_po", [P, 2, CH], F32))
        allkeys = ps[:, :, :].rearrange("p a b -> p (a b)")[:, 0:NS2]
        block = ctx.enter_context(nc.Block())

        @block.tensor
        def _(pe):
            def score(t):
                pe.wait_ge(s_e.sem, s_e.at(t))
                for b in range(4):
                    n = min(CH, NS2 - b * CH)
                    for k in range(KD):
                        last = pe.matmul(ps[:, b, 0:n], qT[:, k, t * P:(t + 1) * P], kT[:, k, b * CH:b * CH + n],
                                         start=(k == 0), stop=(k == KD - 1))
                last.then_inc(s_sc.sem, 1)

            def turn(t):
                pe.wait_ge(s_pn.sem, s_pn.at(t + 1))
                for g, (a, b) in enumerate(GROUPS):
                    i = t * NGR + g
                    pe.wait_ge(s_ts.sem, s_ts.at(i - 1))
                    for kt in range(a, b):
                        r = tile_rows(NS2, kt)
                        last = pe.transpose(pt[0:r, i % 2, (kt - a) * P:(kt - a + 1) * P],
                                            probs[:, t % 2, kt * P:kt * P + r], m.ident[:, :])
                    last.then_inc(s_tr.sem, 1)

            steps = [(k, kt) for k in range(KD) for kt in range(NC2)]

            def weigh(c, quarter):
                pe.wait_ge(s_ts.sem, s_ts.at(NGR * 4 * (c + 1)))
                for k, kt in steps[len(steps) * quarter // 4:len(steps) * (quarter + 1) // 4]:
                    if kt == 0:
                        pe.wait_ge(s_es.sem, s_es.at(KD * (c - 1) + k + 1))
                    r = tile_rows(NS2, kt)
                    last = pe.matmul(po[:, k, :], m.v[0:r, kt, k * P:(k + 1) * P], probsT[0:r, c % 2, kt, :],
                                     start=(kt == 0), stop=(kt == NC2 - 1))
                    if kt == NC2 - 1:
                        last.then_inc(s_ev.sem, 1)

            for t in range(NT + 5):
                if t < NT:
                    score(t)
                if t >= 5:
                    weigh(*divmod(t - 5, 4))
                if 1 <= t <= NT:
                    turn(t - 1)

        @block.vector
        def _(dve):
            def save(c, k):
                dve.wait_ge(s_ev.sem, s_ev.at(KD * c + k + 1))
                nc.vector.tensor_copy(evT[:, k, c * CH:(c + 1) * CH], po[:, k, :]).then_inc(s_es.sem, 1)

            for t in range(NT + 6):
                if t >= 8 and t % 4 < KD:
                    save(t // 4 - 2, t % 4)
                if t < NT:
                    dve.wait_ge(s_sc.sem, s_sc.at(t + 1))
                    nc.vector.reduce_max(cols(mx, t), allkeys, AX).then_inc(s_mx.sem, 1)
                    dve.wait_ge(s_mx.sem, s_mx.at(t + 1))
                    nc.vector.tensor_scalar(cols(nb, t), cols(mx, t), -SC, None, ALU.mult).then_inc(s_nb.sem, 1)
                    dve.wait_ge(s_e.sem, s_e.at(t + 1))
                    nc.vector.reciprocal(cols(rden, t), cols(den, t)).then_inc(s_rd.sem, 1)
                    dve.wait_ge(s_rd.sem, s_rd.at(t + 1))
                    nc.vector.tensor_scalar(probs[:, t % 2, :], probs[:, t % 2, :], cols(rden, t), None, ALU.mult
                                            ).then_inc(s_pn.sem, 1)

        @block.scalar
        def _(act):
            def save_turned(t):
                for g, (a, b) in enumerate(GROUPS):
                    i = t * NGR + g
                    r = tile_rows(NS2, a)
                    act.wait_ge(s_tr.sem, s_tr.at(i + 1))
                    if t % 4 == 0 and g == 0 and t >= 8:
                        act.wait_ge(s_ev.sem, s_ev.at(KD * (t // 4 - 1)))
                    nc.scalar.copy(probsT[0:r, (t // 4) % 2, a:b, (t % 4) * P:(t % 4 + 1) * P],
                                   pt[0:r, i % 2, 0:(b - a) * P].rearrange("p (a b) -> p a b", b=P)
                                   ).then_inc(s_ts.sem, 1)

            for t in range(NT + 1):
                if t < NT:
                    act.wait_ge(s_nb.sem, s_nb.at(t + 1))
                    act.wait_ge(s_tr.sem, s_tr.at(NGR * (t - 1)) if t else s_tr.at(0))
                    nc.scalar.activation(probs[:, t % 2, :], allkeys, ACT.Exp, bias=cols(nb, t), scale=SC,
                                         accum_out=cols(den, t)).then_inc(s_e.sem, 1)
                if t >= 1:
                    save_turned(t - 1)

    for s in (s_sc, s_mx, s_nb, s_e, s_rd, s_pn):
        s.advance(NT)
    for s in (s_tr, s_ts):
        s.advance(NT * NGR)
    for s in (s_ev, s_es):
        s.advance(NCH * KD)


def fold_phase(nc, m, d, w2o, b2o, loads):
    s_w, s_pr, s_tk, s_o, s_bc = (m.sig[n] for n in ("weights", "proj_ready", "proj_taken", "ones", "cond_bc"))
    RT = RH // P
    with ExitStack() as ctx:
        m.uid += 1
        sb = lambda n, s, t=F32: ctx.enter_context(nc.sbuf_tensor(f"fo{m.uid}_" + n, s, t))
        w2T = sb("w2T", [P, NE, KD, RH])
        ow = sb("ow", [P, KD, D])
        ob = sb("ob", [P, D])
        b2 = sb("b2", [P, NE, KD])
        b2bc = sb("b2bc", [P, NE, KD, P])
        ones = sb("ones", [P, P])
        ps = ctx.enter_context(nc.psum_tensor(f"fo{m.uid}_ps", [P, 4, CH], F32))
        block = ctx.enter_context(nc.Block())

        @block.sync
        def _(sp):
            for e in range(NE):
                sp.dma_start(w2T[:, e], d["e_w2T"][e].rearrange("(k p) r -> p k r", p=P)).then_inc(s_w.sem, 16)
            sp.dma_start(ow[:, :, :], d["L2_xcond_out_w"].rearrange("(k p) n -> p k n", p=P)).then_inc(s_w.sem, 16)
            sp.dma_start(ob[:, :], d["L2_xcond_out_b"].partition_broadcast(P)).then_inc(s_w.sem, 16)
            sp.dma_start(b2[:, :, :], d["e_b2_cols"].rearrange("p (e k) -> p e k", e=NE)).then_inc(s_w.sem, 16)
            for dst, src in loads:
                sp.dma_start(dst, src).then_inc(m.sig["load"].sem, 16)

        @block.gpsimd
        def _(pool):
            nc.gpsimd.memset(ones[:, :], 1.0).then_inc(s_o.sem, 1)

        @block.tensor
        def _(pe):
            pe.wait_ge(s_w.sem, s_w.at(96))
            pe.wait_ge(s_bc.sem, s_bc.at(1))
            for i in range(NE * (RT + 1)):
                e, r = divmod(i, RT + 1)
                pe.wait_ge(s_tk.sem, s_tk.at(i - 3))
                for k in range(KD):
                    lhs = w2T[:, e, k, r * P:(r + 1) * P] if r < RT else b2bc[:, e, k, :]
                    last = pe.matmul(ps[:, i % 4, 0:D], lhs, ow[:, k, :], start=(k == 0), stop=(k == KD - 1))
                last.then_inc(s_pr.sem, 1)

        @block.vector
        def _(dve):
            dve.wait_ge(s_w.sem, s_w.at(96))
            dve.wait_ge(s_o.sem, s_o.at(1))
            for e in range(NE):
                for k in range(KD):
                    last = nc.vector.tensor_scalar(b2bc[:, e, k, :], ones[:, :], b2[:, e, k:k + 1], None, ALU.mult)
            last.then_inc(s_bc.sem, 1)
            for i in range(NE * (RT + 1)):
                e, r = divmod(i, RT + 1)
                dve.wait_ge(s_pr.sem, s_pr.at(i + 1))
                if r < RT:
                    nc.vector.tensor_copy(w2o[:, e, r, :], ps[:, i % 4, 0:D]).then_inc(s_tk.sem, 1)
                else:
                    nc.vector.tensor_tensor(b2o[:, e, :], ps[:, i % 4, 0:D], ob[:, :], ALU.add).then_inc(s_tk.sem, 1)

    s_w.advance(96)
    s_o.advance(1)
    s_bc.advance(1)
    for s in (s_pr, s_tk):
        s.advance(NE * (RT + 1))


def expert_weights(nc, ctx, d):
    sb = lambda n, s: ctx.enter_context(nc.sbuf_tensor("ew_" + n, s, F32))
    KC = 2 * KD
    w1, gw1, gw2 = sb("w1", [P, NE, KC, RH]), sb("gw1", [P, KC, D]), sb("gw2", [P, KD, D])
    gb2, rw = sb("gb2", [P, D]), sb("rw", [P, KC, NE])
    loads = [(w1[:, e], d["L2_xcond_e_w1"][e, 0:2 * D, :].rearrange("(k p) n -> p k n", p=P)) for e in range(NE)]
    loads += [(gw1[:, :, :], d["L2_xcond_gate_w1"][0:2 * D, :].rearrange("(k p) n -> p k n", p=P)),
              (gw2[:, :, :], d["L2_xcond_gate_w2"].rearrange("(k p) n -> p k n", p=P)),
              (gb2[:, :], d["L2_xcond_gate_b2"].partition_broadcast(P)),
              (rw[:, :, :], d["L2_xcond_router_W"][0:2 * D, :].rearrange("(k p) n -> p k n", p=P))]
    return (w1, gw1, gw2, gb2, rw), loads


def expert_phase(nc, m, nxT, evT, weights, nload, w2o, b2o):
    (s_w, s_u, s_g, s_r, s_rl, s_rm, s_rs, s_re, s_rt, s_rr, s_pb, s_gz, s_gp, s_gs, s_y, s_yt, s_ya, s_gy, s_x) = (
        m.sig[n] for n in ("load", "up_ready", "gelu_ready", "r_ready", "r_logits", "r_max", "r_shifted",
                           "r_exp", "r_sum", "r_recip", "r_probs", "gate_ready", "gate_biased", "gate_open",
                           "y_ready", "y_biased", "y_summed", "y_gated", "x_added"))
    RT = RH // P
    KC = 2 * KD
    NU = KD + NE * RT
    with ExitStack() as ctx:
        m.uid += 1
        sb = lambda n, s, t=F32: ctx.enter_context(nc.sbuf_tensor(f"ex{m.uid}_" + n, s, t))
        w1, gw1, gw2, gb2, rw = weights
        hid = sb("hid", [P, 2, NU, CH])
        logit = sb("logit", [P, 4, NE])
        rmax = sb("rmax", [P, 4])
        rexp = sb("rexp", [P, 4, NE])
        rsum = sb("rsum", [P, 4])
        prob = sb("prob", [P, 4, NE])
        gate = sb("gate", [P, 4, D])
        biased = sb("biased", [P, NE, D])
        summed = sb("summed", [P, D])
        pu = ctx.enter_context(nc.psum_tensor(f"ex{m.uid}_pu", [P, 2, CH], F32))
        pr = ctx.enter_context(nc.psum_tensor(f"ex{m.uid}_pr", [P, CH], F32))
        pg = ctx.enter_context(nc.psum_tensor(f"ex{m.uid}_pg", [P, 2, CH], F32))
        py = ctx.enter_context(nc.psum_tensor(f"ex{m.uid}_py", [P, NE, CH], F32))
        block = ctx.enter_context(nc.Block())
        moving = lambda k, c: (nxT if k < KD else evT)[:, k % KD, c * CH:(c + 1) * CH]
        stationary = lambda k, t: (nxT if k < KD else evT)[:, k % KD, t * P:(t + 1) * P]

        @block.tensor
        def _(pe):
            def up(c):
                for f in range(NU):
                    i = c * NU + f
                    pe.wait_ge(s_g.sem, s_g.at(i - 1))
                    for k in range(KC):
                        if f < KD:
                            w = gw1[:, k, f * P:(f + 1) * P]
                        else:
                            e, r = divmod(f - KD, RT)
                            w = w1[:, e, k, r * P:(r + 1) * P]
                        last = pe.matmul(pu[:, i % 2, :], w, moving(k, c), start=(k == 0), stop=(k == KC - 1))
                    last.then_inc(s_u.sem, 1)

            def route(c):
                pe.wait_ge(s_rl.sem, s_rl.at(c))
                for q in range(4):
                    for k in range(KC):
                        last = pe.matmul(pr[:, q * NE:(q + 1) * NE], stationary(k, 4 * c + q), rw[:, k, :],
                                         start=(k == 0), stop=(k == KC - 1))
                last.then_inc(s_r.sem, 1)

            def open_gate(c):
                pe.wait_ge(s_g.sem, s_g.at(c * NU + KD))
                pe.wait_ge(s_gp.sem, s_gp.at(c))
                for q in range(4):
                    for k in range(KD):
                        last = pe.matmul(pg[:, q // 2, (q % 2) * D:(q % 2 + 1) * D],
                                         hid[:, c % 2, k, q * P:(q + 1) * P], gw2[:, k, :],
                                         start=(k == 0), stop=(k == KD - 1))
                last.then_inc(s_gz.sem, 1)

            def down(c):
                pe.wait_ge(s_g.sem, s_g.at((c + 1) * NU))
                for q in range(4):
                    for e in range(NE):
                        i = (4 * c + q) * NE + e
                        pe.wait_ge(s_yt.sem, s_yt.at(i - NE + 1))
                        for r in range(RT):
                            last = pe.matmul(py[:, e, 0:D], hid[:, c % 2, KD + e * RT + r, q * P:(q + 1) * P],
                                             w2o[:, e, r, :], start=(r == 0), stop=(r == RT - 1))
                        last.then_inc(s_y.sem, 1)

            pe.wait_ge(s_w.sem, s_w.at(16 * nload))
            up(0)
            for c in range(NCH):
                route(c)
                open_gate(c)
                if c + 1 < NCH:
                    up(c + 1)
                down(c)

        @block.scalar
        def _(act):
            def silus(c):
                for f in range(NU):
                    i = c * NU + f
                    act.wait_ge(s_u.sem, s_u.at(i + 1))
                    if f == 0 and c >= 2:
                        act.wait_ge(s_y.sem, s_y.at(4 * NE * (c - 1)))
                    b = m.col["gb1"] + f if f < KD else m.col["eb1"] + f - KD
                    nc.scalar.activation(hid[:, c % 2, f, :], pu[:, i % 2, :], ACT.Silu, bias=cols(m.mod, b)
                                         ).then_inc(s_g.sem, 1)

            silus(0)
            for c in range(NCH):
                act.wait_ge(s_rs.sem, s_rs.at(c + 1))
                nc.scalar.activation(rexp[:, :, :], logit[:, :, :], ACT.Exp).then_inc(s_re.sem, 1)
                act.wait_ge(s_gp.sem, s_gp.at(c + 1))
                nc.scalar.activation(gate[:, :, :], gate[:, :, :], ACT.Sigmoid).then_inc(s_gs.sem, 1)
                if c + 1 < NCH:
                    silus(c + 1)

        @block.vector
        def _(dve):
            dve.wait_ge(s_w.sem, s_w.at(16 * nload))
            for c in range(NCH):
                dve.wait_ge(s_r.sem, s_r.at(c + 1))
                nc.vector.tensor_tensor(logit[:, :, :], pr[:, 0:4 * NE].rearrange("p (q e) -> p q e", e=NE),
                                        m.router_bias[:, :].unsqueeze(1).broadcast_to([P, 4, NE]), ALU.add
                                        ).then_inc(s_rl.sem, 1)
                dve.wait_ge(s_rl.sem, s_rl.at(c + 1))
                nc.vector.reduce_max(rmax[:, :], logit[:, :, :], AX).then_inc(s_rm.sem, 1)
                dve.wait_ge(s_rm.sem, s_rm.at(c + 1))
                nc.vector.tensor_tensor(logit[:, :, :], logit[:, :, :],
                                        rmax[:, :].unsqueeze(2).broadcast_to([P, 4, NE]), ALU.subtract
                                        ).then_inc(s_rs.sem, 1)
                dve.wait_ge(s_gz.sem, s_gz.at(c + 1))
                nc.vector.tensor_tensor(gate[:, :, :], pg[:, :, :].rearrange("p a (b n) -> p (a b) n", n=D),
                                        gb2[:, :].unsqueeze(1).broadcast_to([P, 4, D]), ALU.add
                                        ).then_inc(s_gp.sem, 1)
                dve.wait_ge(s_re.sem, s_re.at(c + 1))
                nc.vector.reduce_sum(rsum[:, :], rexp[:, :, :], AX).then_inc(s_rt.sem, 1)
                dve.wait_ge(s_rt.sem, s_rt.at(c + 1))
                nc.vector.reciprocal(rmax[:, :], rsum[:, :]).then_inc(s_rr.sem, 1)
                dve.wait_ge(s_rr.sem, s_rr.at(c + 1))
                nc.vector.tensor_tensor(prob[:, :, :], rexp[:, :, :],
                                        rmax[:, :].unsqueeze(2).broadcast_to([P, 4, NE]), ALU.mult
                                        ).then_inc(s_pb.sem, 1)
                dve.wait_ge(s_pb.sem, s_pb.at(c + 1))
                dve.wait_ge(s_gs.sem, s_gs.at(c + 1))
                for q in range(4):
                    t = 4 * c + q
                    for e in range(NE):
                        i = t * NE + e
                        dve.wait_ge(s_y.sem, s_y.at(i + 1))
                        nc.vector.tensor_tensor(biased[:, e, :], py[:, e, 0:D], b2o[:, e, :], ALU.add
                                                ).then_inc(s_yt.sem, 1)
                        dve.wait_ge(s_yt.sem, s_yt.at(i + 1))
                        p = prob[:, q, e:e + 1]
                        if e == 0:
                            op = nc.vector.tensor_scalar(summed[:, :], biased[:, e, :], p, None, ALU.mult)
                        else:
                            dve.wait_ge(s_ya.sem, s_ya.at(i))
                            op = nc.vector.scalar_tensor_tensor(out=summed[:, :], in0=biased[:, e, :], scalar=p,
                                                                in1=summed[:, :], op0=ALU.mult, op1=ALU.add)
                        op.then_inc(s_ya.sem, 1)
                    dve.wait_ge(s_ya.sem, s_ya.at((t + 1) * NE))
                    nc.vector.tensor_tensor(summed[:, :], summed[:, :], gate[:, q, :], ALU.mult).then_inc(s_gy.sem, 1)
                    dve.wait_ge(s_gy.sem, s_gy.at(t + 1))
                    nc.vector.tensor_tensor(m.x[:, t, :], m.x[:, t, :], summed[:, :], ALU.add).then_inc(s_x.sem, 1)
                    row_statistics(nc, m, dve, s_x, t)
            row_statistics(nc, m, dve, s_x, NT)

    s_w.advance(16 * nload)
    for s in (s_u, s_g):
        s.advance(NCH * NU)
    for s in (s_r, s_rl, s_rm, s_rs, s_re, s_rt, s_rr, s_pb, s_gz, s_gp, s_gs):
        s.advance(NCH)
    for s in (s_y, s_yt, s_ya):
        s.advance(NT * NE)
    for s in (s_gy, s_x, m.sig["x_stats"]):
        s.advance(NT)


SIGNALS = """cond_in x_in x_stats normed_pool rows_saved mask_in mask_step const_set load weights cond_ready
mod_ready mod_saved stats rstd normed turned turn_saved ones cond_bc dve cols_ready proj_ready
proj_taken rot_ready rot_taken feat_final part1 rest part2 parts_ready stored0 stored1 stored2 stored3
constants0 constants1 kq0 kq1 scores_ready probs_ready av_done acc_saved max_ready max_taken maxes_ready
neg_ready m_part1 m_rest m_part2 ones_set m_parts m_out m_in v_staged v_biased rows_ready o_turned recip
normalised a_turned a_saved y_ready x_added w_folded x_biased up_ready gelu_ready r_ready r_logits r_max
r_shifted r_exp r_sum r_recip r_probs gate_ready gate_biased gate_open y_biased y_summed y_gated
hid_high hid_low down_done h_high h_low w1_high w1_low w2_high w2_low""".split()


def build(nc, d, out):
    m = Machine()
    m.uid = 0
    m.L = NS2 - (NC2 - 1) * P
    m.col, at = {}, 0
    for name, n in (("l0", 12), ("l1", 8), ("l3", 12), ("eb1", NE * RH // P), ("gb1", KD), ("ln2g", KD), ("ln2b", KD),
                    ("l0b1", FF // P), ("l3b1", FF // P), ("l1q", KD), ("l1k", KD), ("l3q", KD), ("l3k", KD),
                    ("l3cq", KD), ("l3ck", KD)):
        m.col[name] = at
        at += n
    m.NCOL = at
    with ExitStack() as ctx:
        sb = lambda n, s, t=F32: ctx.enter_context(nc.sbuf_tensor(n, s, t))
        m.sig = {n: Signal(ctx.enter_context(nc.semaphore(n))) for n in SIGNALS}
        m.x = sb("x_sb", [P, NT, D])
        m.v = sb("v_sb", [P, NT, D])
        m.attn = sb("attn", [P, NG * T])
        m.ctxT = sb("ctxT", [P, KD, NS2])
        m.ctxnT = sb("ctxnT", [P, KD, NS2])
        m.x_stats = sb("x_stats_sb", [P, NT, 6])
        m.x_mean_var = sb("x_mean_var", [P, NT, 2])
        m.ident = sb("ident_sb", [P, P])
        m.mod = sb("mod", [P, m.NCOL])
        m.gates = sb("gates", [P, 2, D])
        m.router_bias = sb("router_bias", [P, NE])
        m.none_left = sb("none_left", [P, 1])
        dram = lambda n, s, t: nc.dram_tensor(n, s, t, kind="Internal").ap()
        m.q_parts = dram("q_parts", (PARTS, D, T), BF16)
        m.k_parts = dram("k_parts", (PARTS, D, T), BF16)
        m.m_scratch = dram("m_scratch", (PARTS, HG * CH // P, P), BF16)
        m.mask_row = dram("mask_row", (1, NS2), BF16)
        m.const_rows = dram("const_rows", (KROWS - MASK_ROW, T), BF16)
        hT = m.attn[:, 0:KD * T].rearrange("p (k t) -> p k t", k=KD)
        evT = m.attn[:, KD * T:2 * KD * T].rearrange("p (k t) -> p k t", k=KD)
        c = m.col

        with nc.Block() as block:
            @block.sync
            def _(sp):
                for s in m.sig.values():
                    sp.sem_inc(s.sem, CREDIT)

        setup_phase(nc, m, d)

        def feature(w, wcol, src, n_src, bias, parts, keep=None):
            jobs = []
            for c0 in range(0, n_src, CH):
                n = min(CH, n_src - c0)
                for f in range(KD):
                    lhs = [w[:, k, wcol + f * P:wcol + (f + 1) * P] for k in range(KD)]
                    rhs = [src[:, k, c0:c0 + n] for k in range(KD)]
                    store = None if parts is None else parts[:, f * P:(f + 1) * P, c0:c0 + n].rearrange("a p t -> p a t")
                    kept = None if keep is None else keep[:, f, c0:c0 + n]
                    jobs.append((lhs, rhs, n, None if bias is None else bias + f, store, kept, c0))
            return jobs

        def token(w, wcol, src, n_src, bias_bc):
            jobs = []
            for t in range(-(-n_src // P)):
                r = tile_rows(n_src, t)
                jobs.append(([src[:, k, t * P:t * P + r] for k in range(KD)], r,
                             [w[:, k, wcol:wcol + D] for k in range(KD)], bias_bc, m.v[0:r, t, :]))
            return jobs

        def view(name):
            return d[name].rearrange("(k p) n -> p k n", p=P)

        def attend(masked, norm, q, k, v, rope, k_src, nk):
            with ExitStack() as cx:
                m.uid += 1
                tile = lambda n, s, t=F32: cx.enter_context(nc.sbuf_tensor(f"{n}{m.uid}", s, t))
                first = tile("k_first", [P, HG, T], BF16), tile("q_first", [P, HG, T], BF16)
                vw = tile("v_weights", [P, KD, D])
                vb = tile("v_bias", [P, D]) if v[2] is not None else None
                loads = [(vw[:, :, :], view(v[0])[:, :, v[1]:v[1] + D])]
                if vb is not None:
                    loads.append((vb[:, :], v[2].partition_broadcast(P)))
                qkv(norm, q, k, None, rope, k_src, nk, first + (nk, masked), loads)
                attention_phase(nc, m, nk, masked, (k_src, vw, vb), first)

        def qkv(norm, q, k, v, rope, k_src, nk, operands, more_loads=(), keep=None):
            with ExitStack() as cx:
                m.uid += 1
                tiles, loads = {}, list(more_loads)
                store = keep is None
                for w, _, _ in (q, k) if store else (q, k, v):
                    if w not in tiles:
                        n = d[w].shape[1]
                        tiles[w] = cx.enter_context(nc.sbuf_tensor(f"w{m.uid}_{len(tiles)}", [P, KD, n], F32))
                        loads.append((tiles[w][:, :, :], view(w)))
                if rope:
                    m.swap = cx.enter_context(nc.sbuf_tensor(f"swap{m.uid}", [P, P], F32))
                    m.cos = cx.enter_context(nc.sbuf_tensor(f"cos{m.uid}", [P, T], F32))
                    m.sin = cx.enter_context(nc.sbuf_tensor(f"sin{m.uid}", [P, T], F32))
                    for a, b in ((m.swap, "swap"), (m.cos, "cos"), (m.sin, "sin")):
                        loads.append((a[:, :], d[b]))
                bias = None
                if not store and v[2] is not None:
                    bias = cx.enter_context(nc.sbuf_tensor(f"vb{m.uid}", [P, D], F32))
                    loads.append((bias[:, :], v[2].partition_broadcast(P)))
                fk = feature(tiles[k[0]], k[1], k_src, nk, k[2], m.k_parts if store else None,
                             None if store else keep[1])
                fq = feature(tiles[q[0]], q[1], hT, T, q[2], m.q_parts if store else None,
                             None if store else keep[0])
                fj = [j for f in range(KD) for j in fk[f::KD] + fq[f::KD]]
                tj = [] if store else token(tiles[v[0]], v[1], k_src, nk, bias)
                norm_phase(nc, m, hT, *norm, loads)
                projection_phase(nc, m, len(loads), fj, tj, rope, operands)

        attend(False, (1e-5, c["l0"], c["l0"] + 2), ("l0_qkv_wT", 0, None), ("l0_qkv_wT", D, None),
               ("l0_qkv_wT", 2 * D, None), True, hT, T)
        output_phase(nc, m, d["l0_sa_wT"], None, None)
        attend(False, (1e-5, c["l0"] + 4, c["l0"] + 6), ("l0_q_wT", 0, None), ("l0_k_wT", 0, None),
               ("l0_v_wT", 0, None), True, m.ctxT, NS2)
        output_phase(nc, m, d["l0_ca_wT"], None, None)
        ffn_phase(nc, m, hT, (1e-5, c["l0"] + 8, c["l0"] + 10), d["l0_w1T"], c["l0b1"], d["l0_w2T"],
                  d["L0_xcond_ffn_b2"], None, None)
        attend(False, (1e-5, c["l1"], c["l1"] + 2), ("L1_xcond_Wq", 0, c["l1q"]), ("L1_xcond_Wkv", 0, c["l1k"]),
               ("L1_xcond_Wkv", D, d["L1_xcond_bkv"][D:2 * D]), False, m.ctxnT, NS2)
        output_phase(nc, m, d["L1_xcond_Wp"], d["L1_xcond_bp"], None)
        with ExitStack() as cx:
            q2T = cx.enter_context(nc.sbuf_tensor("q2T", [P, KD, T], F32))
            k2T = cx.enter_context(nc.sbuf_tensor("k2T", [P, KD, NS2], F32))
            qkv((1e-5, c["ln2g"], c["ln2b"]), ("L2_xcond_Wq", 0, None), ("L2_xcond_Wk", 0, None), ("L2_xcond_Wv", 0, None),
                False, m.ctxT, NS2, None, keep=(q2T, k2T))
            evidence_phase(nc, m, q2T, k2T, evT)
        with ExitStack() as cx:
            w2o = cx.enter_context(nc.sbuf_tensor("w2o", [P, NE, RH // P, D], F32))
            b2o = cx.enter_context(nc.sbuf_tensor("b2o", [P, NE, D], F32))
            weights, loads = expert_weights(nc, cx, d)
            fold_phase(nc, m, d, w2o, b2o, loads)
            expert_phase(nc, m, hT, evT, weights, len(loads), w2o, b2o)
        attend(False, (1e-6, c["l3"] + 2, c["l3"]), ("L3_xcond_qkv_w", 0, c["l3q"]), ("L3_xcond_qkv_w", D, c["l3k"]),
               ("L3_xcond_qkv_w", 2 * D, d["L3_xcond_qkv_b"][2 * D:3 * D]), False, hT, T)
        output_phase(nc, m, d["L3_xcond_sa_proj_w"], d["L3_xcond_sa_proj_b"], 0)
        attend(True, (1e-6, None, None), ("L3_xcond_q_w", 0, c["l3cq"]), ("L3_xcond_kv_w", 0, c["l3ck"]),
               ("L3_xcond_kv_w", D, d["L3_xcond_kv_b"][D:2 * D]), False, m.ctxT, NS2)
        output_phase(nc, m, d["L3_xcond_ca_proj_w"], d["L3_xcond_ca_proj_b"], None, m.none_left)
        ffn_phase(nc, m, hT, (1e-6, c["l3"] + 8, c["l3"] + 6), d["L3_xcond_fc1_w"], c["l3b1"],
                  d["L3_xcond_fc2_w"], d["L3_xcond_fc2_b"], 1, out)


def kernel(**inputs):
    import numpy as np
    import concourse.bacc as bacc
    from concourse.bass_utils import run_bass_kernel_spmd

    a = {n: np.ascontiguousarray(v) for n, v in inputs.items()}
    columns = lambda v: np.asarray(v).reshape(-1, P).T
    arrays = {
        "x": a["x"][0], "ctx": a["ctx_1024"][0], "cond": columns(a["cond_1024"]),
        "mask": np.pad(a["mask_BxS2_bf0"], ((0, 0), (0, -NS2 % 4))).view(np.int32),
        "ident": np.eye(P, dtype=np.float32),
        "l0_ln_wT": np.stack([a[f"L0_xcond_ln{i}_w"].T for i in (1, 2, 3)]),
        "l0_qkv_wT": a["L0_xcond_qkv_w"].T, "l0_sa_wT": a["L0_xcond_sa_out_w"].T,
        "l0_q_wT": a["L0_xcond_q_w"].T, "l0_k_wT": a["L0_xcond_k_w"].T, "l0_v_wT": a["L0_xcond_v_w"].T,
        "l0_ca_wT": a["L0_xcond_ca_out_w"].T, "l0_w1T": a["L0_xcond_ffn_w1"].T, "l0_w2T": a["L0_xcond_ffn_w2"].T,
        "e_w2T": a["L2_xcond_e_w2"].transpose(0, 2, 1),
        "e_b2_cols": columns(a["L2_xcond_e_b2"]),
        "bias_cols": np.concatenate([columns(a[n]) for n in (
            "L0_xcond_ln1_b", "L0_xcond_ln2_b", "L0_xcond_ln3_b", "L1_xcond_bss_q", "L1_xcond_bss_kv",
            "L3_xcond_ada_b", "L2_xcond_e_b1", "L2_xcond_gate_b1", "L2_xcond_ln_gamma", "L2_xcond_ln_beta",
            "L0_xcond_ffn_b1", "L3_xcond_fc1_b", "L1_xcond_bq")]
            + [columns(a["L1_xcond_bkv"][0:D])]
            + [columns(a["L3_xcond_qkv_b"][0:2 * D]), columns(a["L3_xcond_q_b"]), columns(a["L3_xcond_kv_b"][0:D])],
            axis=1),
    }
    half = DH // 2
    freq = (np.float32(1.0) / np.power(np.float32(10000.0), np.arange(half, dtype=np.float32) / np.float32(half))
            ).astype(np.float32)
    angle = np.arange(T, dtype=np.float32)[None, :] * freq[:, None]
    arrays["cos"] = np.tile(np.cos(angle), (P // half, 1)).astype(np.float32)
    arrays["sin"] = np.tile(np.concatenate([-np.sin(angle), np.sin(angle)]), (P // DH, 1)).astype(np.float32)
    swap = np.zeros((P, P), np.float32)
    swap[np.arange(P), np.arange(P) ^ half] = 1.0
    arrays["swap"] = swap
    for n in ("L1_xcond_Wss_q", "L1_xcond_Wss_kv", "L1_xcond_Wq", "L1_xcond_Wkv", "L1_xcond_bkv", "L1_xcond_Wp",
              "L1_xcond_bp", "L0_xcond_ffn_b2", "L2_xcond_Wq", "L2_xcond_Wk", "L2_xcond_Wv", "L2_xcond_router_W",
              "L2_xcond_router_b", "L2_xcond_e_w1", "L2_xcond_gate_w1", "L2_xcond_gate_w2", "L2_xcond_gate_b2",
              "L2_xcond_out_w", "L2_xcond_out_b", "L3_xcond_ada_w", "L3_xcond_ada_b", "L3_xcond_qkv_w",
              "L3_xcond_qkv_b", "L3_xcond_sa_proj_w", "L3_xcond_sa_proj_b", "L3_xcond_q_w", "L3_xcond_kv_w",
              "L3_xcond_kv_b", "L3_xcond_ca_proj_w", "L3_xcond_ca_proj_b", "L3_xcond_fc1_w", "L3_xcond_fc2_w",
              "L3_xcond_fc2_b"):
        arrays[n] = a[n]
    arrays = {"in_" + n: np.ascontiguousarray(v) for n, v in arrays.items()}
    nc = bacc.Bacc("TRN2", target_bir_lowering=False, num_devices=1)
    d = {n[3:]: nc.dram_tensor(n, v.shape, mybir.dt.from_np(v.dtype), kind="ExternalInput").ap()
         for n, v in arrays.items()}
    out = nc.dram_tensor("out_x", (T, D), F32, kind="ExternalOutput").ap()
    build(nc, d, out)
    r = run_bass_kernel_spmd(nc, [arrays], core_ids=[0])
    return r.results[0]["out_x"].reshape(1, T, D)
```
